# Optimizing a Trainium2 kernel written in Bass

```python
import numpy as np
import jax
import jax.numpy as jnp

def _softmax(x, axis=-1):
    return jax.nn.softmax(x, axis=axis)

def _gelu(x):
    return jax.nn.gelu(x, approximate=True)

def _silu(x):
    return jax.nn.silu(x)

def _sigmoid(x):
    return jax.nn.sigmoid(x)

def _layernorm(x, axis=-1, eps=1e-05):
    m = jnp.mean(x, axis=axis, keepdims=True)
    v = jnp.var(x, axis=axis, keepdims=True)
    return (x - m) / jnp.sqrt(v + eps)

def _scatter_add(tgt, idx, src, axis=0):
    return tgt.at[idx].add(src)

def _segment_sum(src, seg, n):
    return jax.ops.segment_sum(src, seg, n)
kernel_name = 'mk_flamingo_gated_d4_seqx_r4_7f114c'

def setup_inputs(seed: int=0):
    np.random.seed(seed)
    _w = jnp.asarray

    def _rec_inputs():
        import jax
        import jax.numpy as jnp
        _rk = jax.random.key(seed)
        x = -0.0002928 + 1 * jax.random.normal(jax.random.fold_in(_rk, 1), (8, 512, 256), jnp.float32)
        _lenS = 512 - jax.random.randint(jax.random.fold_in(_rk, 7), (8,), 0, max(1, 512 // 4) + 1, jnp.int32)
        _lenS2 = 512 - jax.random.randint(jax.random.fold_in(_rk, 8), (8,), 0, max(1, 512 // 4) + 1, jnp.int32)
        _ctx_1024P = jax.random.normal(jax.random.fold_in(_rk, 11), (8, 16, 256), jnp.float32)
        _ctx_1024c = jax.random.dirichlet(jax.random.fold_in(_rk, 511), 0.3 * jnp.ones((16,), jnp.float32), (8, 512))
        _ctx_1024t = jnp.einsum('bsk,bkd->bsd', _ctx_1024c, _ctx_1024P)
        _ctx_1024t = _ctx_1024t * jax.lax.rsqrt(jnp.mean(jnp.square(_ctx_1024t)) + 1e-12) * 0.953939
        ctx_1024 = -1.39393e-06 + 0.999914 * (_ctx_1024t + 0.3 * jax.random.normal(jax.random.fold_in(_rk, 611), (8, 512, 256), jnp.float32))
        itok_BxS2_0_2047 = jax.random.randint(jax.random.fold_in(_rk, 13), (8, 512), 0, 512, jnp.int32)
        _validS = jnp.arange(512)[None, :] < _lenS[:, None]
        _validS2 = jnp.arange(512)[None, :] < _lenS2[:, None]
        _causal = jnp.tril(jnp.ones((512, 512), dtype=bool))
        mask_BxS2_ik0 = jnp.where(jnp.broadcast_to(_validS2[:, :], (8, 512)), 0, 1).astype(jnp.int32)
        _g = jax.random.normal(jax.random.fold_in(_rk, 9001), (2, 4), jnp.float32)
        _g = jnp.sign(_g) * jnp.maximum(jnp.abs(_g), 1.0) + (_g == 0) * 1.0
        g_xattn = _g[0]
        g_ffn = _g[1]
        return (x, ctx_1024, itok_BxS2_0_2047, mask_BxS2_ik0, g_xattn, g_ffn)
    x, ctx_1024, itok_BxS2_0_2047, mask_BxS2_ik0, g_xattn, g_ffn = _rec_inputs()

    def _L0_xattn_setup():
        import jax, jax.numpy as jnp
        import numpy as np
        import math
        D_MODEL = 256
        NUM_HEADS = 16
        MAX_LEN = 512
        D_HEAD = D_MODEL // NUM_HEADS
        BATCH = 2
        SEQ = 512

        def _skew(QEr):
            B, H, R, C = QEr.shape
            padded = jnp.pad(QEr, ((0, 0), (0, 0), (0, 0), (1, 0)))
            reshaped = padded.reshape(B, H, C + 1, R)
            return reshaped[:, :, 1:, :]
        root = jax.random.key(seed)
        ks = jax.random.split(root, 10)
        s = 1.0 / math.sqrt(D_MODEL)
        return {'query': jax.random.normal(ks[0], (BATCH, SEQ, D_MODEL), jnp.float32), 'key': jax.random.normal(ks[1], (BATCH, SEQ, D_MODEL), jnp.float32), 'value': jax.random.normal(ks[2], (BATCH, SEQ, D_MODEL), jnp.float32), 'Wq': jax.random.normal(ks[3], (D_MODEL, D_MODEL), jnp.float32) * s, 'bq': jax.random.normal(ks[4], (D_MODEL,), jnp.float32) * s, 'Wk': jax.random.normal(ks[5], (D_MODEL, D_MODEL), jnp.float32) * s, 'bk': jax.random.normal(ks[6], (D_MODEL,), jnp.float32) * s, 'Wv': jax.random.normal(ks[7], (D_MODEL, D_MODEL), jnp.float32) * s, 'bv': jax.random.normal(ks[8], (D_MODEL,), jnp.float32) * s, 'Er': jax.random.normal(ks[9], (MAX_LEN, D_HEAD), jnp.float32)}
    _L0_xattn_all = _L0_xattn_setup()
    _L0_xattn_in = {k: v for k, v in _L0_xattn_all.items() if k in ('Wq', 'bq', 'Wk', 'bk', 'Wv', 'bv', 'Er')}
    del _L0_xattn_all

    def _L0_ffn_setup():
        import jax, jax.numpy as jnp
        import numpy as np
        BLOCK = 32
        W_BITS = 4
        ACT_BITS = 16

        def act_qdq(x):
            qmax = 2.0 ** (ACT_BITS - 1) - 1.0
            scale = jnp.maximum(jnp.max(jnp.abs(x)) / qmax, 1e-12)
            return jnp.clip(jnp.round(x / scale), -qmax - 1.0, qmax) * scale

        def fixed_qdq_u16(x):
            scale = 1.0 / 65536.0
            return jnp.clip(jnp.round(x / scale), 0.0, 65535.0) * scale

        def lpbq_dequant(w):
            O, I = w.shape
            qmax = 2.0 ** (W_BITS - 1) - 1.0
            wb = w.reshape(O, I // BLOCK, BLOCK)
            s = jnp.maximum(jnp.max(jnp.abs(wb), axis=-1, keepdims=True) / qmax, 1e-12)
            wq = jnp.clip(jnp.round(wb / s), -qmax - 1.0, qmax) * s
            return wq.reshape(O, I)
        key = jax.random.key(seed)
        k1, k2, k3, k4 = jax.random.split(key, 4)
        B, S, H, I = (2, 1024, 256, 768)
        x = jax.random.normal(k1, (B, S, H), jnp.float32)
        w_gate = jax.random.normal(k2, (I, H), jnp.float32) * 0.02
        w_up = jax.random.normal(k3, (I, H), jnp.float32) * 0.02
        w_down = jax.random.normal(k4, (H, I), jnp.float32) * 0.02
        return {'x': x, 'w_gate': w_gate, 'w_up': w_up, 'w_down': w_down}
    _L0_ffn_all = _L0_ffn_setup()
    _L0_ffn_in = {k: v for k, v in _L0_ffn_all.items() if k in ('w_gate', 'w_up', 'w_down')}
    del _L0_ffn_all

    def _L1_xattn_setup():
        import jax, jax.numpy as jnp
        import numpy as np
        B, N, N2 = (4, 512, 256)
        DIM, DIM_Y, H = (256, 256, 16)
        HD = DIM // H
        SCALE = HD ** (-0.5)
        key = jax.random.key(seed)
        ks = jax.random.split(key, 6)
        s = 0.02
        return {'x': jax.random.normal(ks[0], (B, N, DIM), dtype=jnp.float32), 'y': jax.random.normal(ks[1], (B, N2, DIM_Y), dtype=jnp.float32), 'pad_mask': jax.random.randint(ks[2], (B, N2), 0, 2, dtype=jnp.int32), 'Wq': jax.random.normal(ks[3], (DIM, DIM), dtype=jnp.float32) * s, 'Wkv': jax.random.normal(ks[4], (DIM_Y, 2 * DIM), dtype=jnp.float32) * s, 'Wproj': jax.random.normal(ks[5], (DIM, DIM), dtype=jnp.float32) * s, 'bproj': jnp.zeros((DIM,), dtype=jnp.float32)}
    _L1_xattn_all = _L1_xattn_setup()
    _L1_xattn_in = {k: v for k, v in _L1_xattn_all.items() if k in ('Wq', 'Wkv', 'Wproj', 'bproj')}
    del _L1_xattn_all

    def _L1_ffn_setup():
        import jax, jax.numpy as jnp
        import numpy as np
        E = 16
        G = 4
        EPG = E // G
        K = 4
        TOPK_GROUP = 2
        PER_GROUP_K = K // TOPK_GROUP

        def _route(xf, router_w, correction_bias):
            S = xf.shape[0]
            logits = xf @ router_w.T
            scores = jax.nn.sigmoid(logits)
            sb = scores + correction_bias
            grp_top = jax.lax.top_k(sb.reshape(S, G, EPG), PER_GROUP_K)[0]
            group_scores = grp_top.sum(axis=-1)
            _, group_idx = jax.lax.top_k(group_scores, TOPK_GROUP)
            group_mask = jnp.zeros((S, G), sb.dtype).at[jnp.arange(S)[:, None], group_idx].set(1.0)
            score_mask = jnp.broadcast_to(group_mask[:, :, None], (S, G, EPG)).reshape(S, E)
            masked = jnp.where(score_mask > 0, sb, -jnp.inf)
            _, topk_idx = jax.lax.top_k(masked, K)
            w = jnp.take_along_axis(scores, topk_idx, axis=1)
            w = w / (w.sum(axis=-1, keepdims=True) + 1e-20)
            return (topk_idx, w, scores)
        key = jax.random.key(seed)
        ks = jax.random.split(key, 9)
        B, T, C, H, HS = (2, 256, 256, 64, 512)
        std = 0.02
        return {'x': jax.random.normal(ks[0], (B, T, C), jnp.float32), 'router_w': jax.random.normal(ks[1], (E, C), jnp.float32) * std, 'correction_bias': jnp.zeros((E,), jnp.float32), 'gate_w': jax.random.normal(ks[2], (E, C, H), jnp.float32) * std, 'up_w': jax.random.normal(ks[3], (E, C, H), jnp.float32) * std, 'down_w': jax.random.normal(ks[4], (E, H, C), jnp.float32) * std, 'shared_gate_w': jax.random.normal(ks[5], (HS, C), jnp.float32) * std, 'shared_up_w': jax.random.normal(ks[6], (HS, C), jnp.float32) * std, 'shared_down_w': jax.random.normal(ks[7], (C, HS), jnp.float32) * std}
    _L1_ffn_all = _L1_ffn_setup()
    _L1_ffn_in = {k: v for k, v in _L1_ffn_all.items() if k in ('router_w', 'correction_bias', 'gate_w', 'up_w', 'down_w', 'shared_gate_w', 'shared_up_w', 'shared_down_w')}
    del _L1_ffn_all

    def _L2_xattn_setup():
        import jax, jax.numpy as jnp
        import numpy as np
        B, S, D, NH = (2, 512, 256, 8)
        DH = D // NH
        EPS = 1e-06
        LN_EPS = 1e-05

        def _mlstm_cell(q, k, v, igate_w, igate_b, fgate_w, fgate_b, ln_scale):
            Slen = q.shape[0]
            ifg = jnp.concatenate([q, k, v], axis=-1)
            ig = (ifg @ igate_w.T + igate_b).T
            fg = (ifg @ fgate_w.T + fgate_b).T
            qh = q.reshape(Slen, NH, DH).transpose(1, 0, 2)
            kh = k.reshape(Slen, NH, DH).transpose(1, 0, 2)
            vh = v.reshape(Slen, NH, DH).transpose(1, 0, 2)
            log_f = jax.nn.log_sigmoid(fg)
            cs = jnp.cumsum(log_f, axis=1)
            fg_mat = cs[:, :, None] - cs[:, None, :]
            mask = jnp.tril(jnp.ones((Slen, Slen), dtype=bool))
            log_fg_mat = jnp.where(mask, fg_mat, -jnp.inf)
            log_D = log_fg_mat + ig[:, None, :]
            max_log_D = jnp.max(log_D, axis=-1, keepdims=True)
            D_mat = jnp.exp(log_D - max_log_D)
            qk = jnp.einsum('hsd,htd->hst', qh, kh) / np.sqrt(DH)
            C = qk * D_mat
            normalizer = jnp.maximum(jnp.abs(C.sum(axis=-1, keepdims=True)), jnp.exp(-max_log_D))
            h = jnp.einsum('hst,htd->hsd', C / (normalizer + EPS), vh)
            h = h.transpose(1, 0, 2).reshape(Slen, D)
            mu = h.mean(axis=-1, keepdims=True)
            var = h.var(axis=-1, keepdims=True)
            return (h - mu) / jnp.sqrt(var + LN_EPS) * ln_scale
        key = jax.random.key(seed)
        ks = jax.random.split(key, 8)
        rnd = lambda k, sh, s=1.0: jax.random.normal(k, sh, dtype=jnp.float32) * s
        return {'q': rnd(ks[0], (B, S, D)), 'k': rnd(ks[1], (B, S, D)), 'v': rnd(ks[2], (B, S, D)), 'igate_w': rnd(ks[3], (NH, 3 * D), 0.02), 'igate_b': jnp.linspace(3.0, 6.0, NH, dtype=jnp.float32), 'fgate_w': rnd(ks[4], (NH, 3 * D), 0.02), 'fgate_b': rnd(ks[5], (NH,), 0.3162278), 'ln_scale': jnp.ones((D,), dtype=jnp.float32)}
    _L2_xattn_all = _L2_xattn_setup()
    _L2_xattn_in = {k: v for k, v in _L2_xattn_all.items() if k in ('igate_w', 'igate_b', 'fgate_w', 'fgate_b', 'ln_scale')}
    del _L2_xattn_all

    def _L2_ffn_setup():
        import jax, jax.numpy as jnp
        import numpy as np
        DIM = 256
        DEPTH = 2
        HEADS = 8
        DIM_HEAD = 64
        WINDOW = 128
        INNER = HEADS * DIM_HEAD
        HID = int(DIM * 4 * 2 / 3)
        B, N = (2, 2048)
        QK_SCALE = 8.0

        def shift_token(t):
            t1, t2 = jnp.split(t, 2, axis=-1)
            t2 = jnp.pad(t2, ((0, 0), (1, 0), (0, 0)))[:, :-1]
            return jnp.concatenate([t1, t2], axis=-1)

        def l2norm(t):
            return t / jnp.clip(jnp.linalg.norm(t, axis=-1, keepdims=True), 1e-12)

        def rotate_half(x):
            x1, x2 = jnp.split(x, 2, axis=-1)
            return jnp.concatenate([-x2, x1], axis=-1)

        def rotary_xpos(q, k):
            n = q.shape[-2]
            half_idx = jnp.arange(0, DIM_HEAD, 2, dtype=jnp.float32)
            inv_freq = 1.0 / 10000.0 ** (half_idx / DIM_HEAD)
            t = jnp.arange(n, dtype=jnp.float32)
            freqs = t[:, None] * inv_freq[None, :]
            freqs = jnp.concatenate([freqs, freqs], axis=-1)
            base = (half_idx + 0.4 * DIM_HEAD) / (1.4 * DIM_HEAD)
            power = (t - n // 2) / float(WINDOW // 2)
            scale = base[None, :] ** power[:, None]
            scale = jnp.concatenate([scale, scale], axis=-1)
            cos, sin = (jnp.cos(freqs), jnp.sin(freqs))
            q = q * cos * scale + rotate_half(q) * sin * scale
            k = k * cos / scale + rotate_half(k) * sin / scale
            return (q, k)

        def local_attention(q, k, v):
            b, h, n, d = q.shape
            w = n // WINDOW
            bq = q.reshape(b, h, w, WINDOW, d) * QK_SCALE
            bk = k.reshape(b, h, w, WINDOW, d)
            bv = v.reshape(b, h, w, WINDOW, d)

            def look_around(t):
                p = jnp.pad(t, ((0, 0), (0, 0), (1, 0), (0, 0), (0, 0)))
                return jnp.concatenate([p[:, :, :w], p[:, :, 1:]], axis=3)
            bk, bv = (look_around(bk), look_around(bv))
            bt = jnp.arange(n).reshape(w, WINDOW)
            btp = jnp.pad(bt, ((1, 0), (0, 0)), constant_values=-1)
            btk = jnp.concatenate([btp[:w], btp[1:]], axis=1)
            sim = jnp.einsum('bhwid,bhwjd->bhwij', bq, bk)
            i = bt[:, :, None]
            j = btk[:, None, :]
            mask = (i < j) | (i > j + WINDOW) | (j == -1)
            sim = jnp.where(mask, -jnp.finfo(sim.dtype).max, sim)
            attn = jax.nn.softmax(sim, axis=-1)
            out = jnp.einsum('bhwij,bhwjd->bhwid', attn, bv)
            return out.reshape(b, h, n, d)

        def _layer(x, wqkv, qs, ksc, wo, lg, lb, w1, b1, w2, b2):
            b, n, _ = x.shape
            h = shift_token(x)
            qkv = h @ wqkv
            q, k, v = jnp.split(qkv, 3, axis=-1)
            to_heads = lambda t: t.reshape(b, n, HEADS, DIM_HEAD).transpose(0, 2, 1, 3)
            q, k, v = (to_heads(q), to_heads(k), to_heads(v))
            q = l2norm(q) * qs
            k = l2norm(k) * ksc
            q, k = rotary_xpos(q, k)
            o = local_attention(q, k, v)
            o = o.transpose(0, 2, 1, 3).reshape(b, n, INNER)
            x = x + o @ wo
            h = shift_token(x)
            mu = h.mean(-1, keepdims=True)
            var = h.var(-1, keepdims=True)
            h = (h - mu) / jnp.sqrt(var + 1e-05) * lg + lb
            h = h @ w1 + b1
            a, g = jnp.split(h, 2, axis=-1)
            h = a * jax.nn.gelu(g, approximate=False)
            x = x + h @ w2 + b2
            return x
        key = jax.random.key(seed)
        ks = jax.random.split(key, 6)
        return {'x': jax.random.normal(ks[0], (B, N, DIM), jnp.float32), 'wqkv': jax.random.normal(ks[1], (DEPTH, DIM, 3 * INNER), jnp.float32) * 0.02, 'q_scale': jnp.ones((DEPTH, DIM_HEAD), jnp.float32), 'k_scale': jnp.ones((DEPTH, DIM_HEAD), jnp.float32), 'wo': jax.random.normal(ks[2], (DEPTH, INNER, DIM), jnp.float32) * 0.02, 'ln_g': jnp.ones((DEPTH, DIM), jnp.float32), 'ln_b': jnp.zeros((DEPTH, DIM), jnp.float32), 'w1': jax.random.normal(ks[3], (DEPTH, DIM, 2 * HID), jnp.float32) * 0.02, 'b1': jnp.zeros((DEPTH, 2 * HID), jnp.float32), 'w2': jax.random.normal(ks[4], (DEPTH, HID, DIM), jnp.float32) * 0.02, 'b2': jnp.zeros((DEPTH, DIM), jnp.float32)}
    _L2_ffn_all = _L2_ffn_setup()
    _L2_ffn_in = {k: v for k, v in _L2_ffn_all.items() if k in ('wqkv', 'q_scale', 'k_scale', 'wo', 'ln_g', 'ln_b', 'w1', 'b1', 'w2', 'b2')}
    del _L2_ffn_all

    def _L3_xattn_setup():
        import jax, jax.numpy as jnp
        import numpy as np
        DIM = 256
        HEADS = 16
        HEAD_DIM = DIM // HEADS
        SCALE = HEAD_DIM ** (-0.5)
        key = jax.random.key(seed)
        ks = jax.random.split(key, 13)
        B, Nq, Nk = (4, 512, 512)
        s = DIM ** (-0.5)
        return {'query': jax.random.normal(ks[0], (B, Nq, DIM), jnp.float32), 'key': jax.random.normal(ks[1], (B, Nk, DIM), jnp.float32), 'value': jax.random.normal(ks[2], (B, Nk, DIM), jnp.float32), 'qpos': jax.random.randint(ks[3], (B, Nq), 0, Nq), 'kpos': jax.random.randint(ks[4], (B, Nk), 0, Nk), 'Wq': jax.random.normal(ks[5], (DIM, DIM), jnp.float32) * s, 'bq': jnp.zeros((DIM,), jnp.float32), 'Wk': jax.random.normal(ks[6], (DIM, DIM), jnp.float32) * s, 'bk': jnp.zeros((DIM,), jnp.float32), 'Wv': jax.random.normal(ks[7], (DIM, DIM), jnp.float32) * s, 'bv': jnp.zeros((DIM,), jnp.float32), 'Wo': jax.random.normal(ks[8], (DIM, DIM), jnp.float32) * s, 'bo': jnp.zeros((DIM,), jnp.float32)}
    _L3_xattn_all = _L3_xattn_setup()
    _L3_xattn_in = {k: v for k, v in _L3_xattn_all.items() if k in ('Wq', 'bq', 'Wk', 'bk', 'Wv', 'bv', 'Wo', 'bo')}
    del _L3_xattn_all

    def _L3_ffn_setup():
        import jax, jax.numpy as jnp
        import numpy as np
        B, T, D, E, H = (4, 512, 256, 4, 8)
        EPS = 1e-05

        def _uniform(k, shape, bound):
            return jax.random.uniform(k, shape, jnp.float32, -bound, bound)

        def _layernorm(x, w, b):
            mu = jnp.mean(x, axis=-1, keepdims=True)
            var = jnp.mean(jnp.square(x - mu), axis=-1, keepdims=True)
            return (x - mu) * jax.lax.rsqrt(var + EPS) * w + b
        key = jax.random.key(seed)
        ks = jax.random.split(key, 12)
        wb = np.sqrt(6.0 / D) / np.sqrt(6.0)
        wb = 1.0 / np.sqrt(D)
        return {'x': jax.random.normal(ks[0], (B, T, D), jnp.float32), 'router_prob': jax.random.uniform(ks[1], (B, T, E), jnp.float32), 'norm_w': jnp.ones((D,), jnp.float32), 'norm_b': jnp.zeros((D,), jnp.float32), 'q_w': _uniform(ks[2], (D, D), wb), 'q_b': _uniform(ks[3], (D,), wb), 'k_w': _uniform(ks[4], (D, D), wb), 'k_b': _uniform(ks[5], (D,), wb), 'v_w': _uniform(ks[6], (D, D), wb), 'v_b': _uniform(ks[7], (D,), wb), 'o_w': _uniform(ks[8], (D, D), wb), 'o_b': _uniform(ks[9], (D,), wb)}
    _L3_ffn_all = _L3_ffn_setup()
    _L3_ffn_in = {k: v for k, v in _L3_ffn_all.items() if k in ('router_prob', 'norm_w', 'norm_b', 'q_w', 'q_b', 'k_w', 'k_b', 'v_w', 'v_b', 'o_w', 'o_b')}
    del _L3_ffn_all
    return {'x': x, 'ctx_1024': ctx_1024, 'itok_BxS2_0_2047': itok_BxS2_0_2047, 'mask_BxS2_ik0': mask_BxS2_ik0, 'g_xattn': g_xattn, 'g_ffn': g_ffn, 'L0_xattn_Wq': _L0_xattn_in['Wq'], 'L0_xattn_bq': _L0_xattn_in['bq'], 'L0_xattn_Wk': _L0_xattn_in['Wk'], 'L0_xattn_bk': _L0_xattn_in['bk'], 'L0_xattn_Wv': _L0_xattn_in['Wv'], 'L0_xattn_bv': _L0_xattn_in['bv'], 'L0_xattn_Er': _L0_xattn_in['Er'], 'L0_ffn_w_gate': _L0_ffn_in['w_gate'], 'L0_ffn_w_up': _L0_ffn_in['w_up'], 'L0_ffn_w_down': _L0_ffn_in['w_down'], 'L1_xattn_Wq': _L1_xattn_in['Wq'], 'L1_xattn_Wkv': _L1_xattn_in['Wkv'], 'L1_xattn_Wproj': _L1_xattn_in['Wproj'], 'L1_xattn_bproj': _L1_xattn_in['bproj'], 'L1_ffn_router_w': _L1_ffn_in['router_w'], 'L1_ffn_correction_bias': _L1_ffn_in['correction_bias'], 'L1_ffn_gate_w': _L1_ffn_in['gate_w'], 'L1_ffn_up_w': _L1_ffn_in['up_w'], 'L1_ffn_down_w': _L1_ffn_in['down_w'], 'L1_ffn_shared_gate_w': _L1_ffn_in['shared_gate_w'], 'L1_ffn_shared_up_w': _L1_ffn_in['shared_up_w'], 'L1_ffn_shared_down_w': _L1_ffn_in['shared_down_w'], 'L2_xattn_igate_w': _L2_xattn_in['igate_w'], 'L2_xattn_igate_b': _L2_xattn_in['igate_b'], 'L2_xattn_fgate_w': _L2_xattn_in['fgate_w'], 'L2_xattn_fgate_b': _L2_xattn_in['fgate_b'], 'L2_xattn_ln_scale': _L2_xattn_in['ln_scale'], 'L2_ffn_wqkv': _L2_ffn_in['wqkv'], 'L2_ffn_q_scale': _L2_ffn_in['q_scale'], 'L2_ffn_k_scale': _L2_ffn_in['k_scale'], 'L2_ffn_wo': _L2_ffn_in['wo'], 'L2_ffn_ln_g': _L2_ffn_in['ln_g'], 'L2_ffn_ln_b': _L2_ffn_in['ln_b'], 'L2_ffn_w1': _L2_ffn_in['w1'], 'L2_ffn_b1': _L2_ffn_in['b1'], 'L2_ffn_w2': _L2_ffn_in['w2'], 'L2_ffn_b2': _L2_ffn_in['b2'], 'L3_xattn_Wq': _L3_xattn_in['Wq'], 'L3_xattn_bq': _L3_xattn_in['bq'], 'L3_xattn_Wk': _L3_xattn_in['Wk'], 'L3_xattn_bk': _L3_xattn_in['bk'], 'L3_xattn_Wv': _L3_xattn_in['Wv'], 'L3_xattn_bv': _L3_xattn_in['bv'], 'L3_xattn_Wo': _L3_xattn_in['Wo'], 'L3_xattn_bo': _L3_xattn_in['bo'], 'L3_ffn_router_prob': _L3_ffn_in['router_prob'], 'L3_ffn_norm_w': _L3_ffn_in['norm_w'], 'L3_ffn_norm_b': _L3_ffn_in['norm_b'], 'L3_ffn_q_w': _L3_ffn_in['q_w'], 'L3_ffn_q_b': _L3_ffn_in['q_b'], 'L3_ffn_k_w': _L3_ffn_in['k_w'], 'L3_ffn_k_b': _L3_ffn_in['k_b'], 'L3_ffn_v_w': _L3_ffn_in['v_w'], 'L3_ffn_v_b': _L3_ffn_in['v_b'], 'L3_ffn_o_w': _L3_ffn_in['o_w'], 'L3_ffn_o_b': _L3_ffn_in['o_b']}

def reference(x, ctx_1024, itok_BxS2_0_2047, mask_BxS2_ik0, g_xattn, g_ffn, L0_xattn_Wq, L0_xattn_bq, L0_xattn_Wk, L0_xattn_bk, L0_xattn_Wv, L0_xattn_bv, L0_xattn_Er, L0_ffn_w_gate, L0_ffn_w_up, L0_ffn_w_down, L1_xattn_Wq, L1_xattn_Wkv, L1_xattn_Wproj, L1_xattn_bproj, L1_ffn_router_w, L1_ffn_correction_bias, L1_ffn_gate_w, L1_ffn_up_w, L1_ffn_down_w, L1_ffn_shared_gate_w, L1_ffn_shared_up_w, L1_ffn_shared_down_w, L2_xattn_igate_w, L2_xattn_igate_b, L2_xattn_fgate_w, L2_xattn_fgate_b, L2_xattn_ln_scale, L2_ffn_wqkv, L2_ffn_q_scale, L2_ffn_k_scale, L2_ffn_wo, L2_ffn_ln_g, L2_ffn_ln_b, L2_ffn_w1, L2_ffn_b1, L2_ffn_w2, L2_ffn_b2, L3_xattn_Wq, L3_xattn_bq, L3_xattn_Wk, L3_xattn_bk, L3_xattn_Wv, L3_xattn_bv, L3_xattn_Wo, L3_xattn_bo, L3_ffn_router_prob, L3_ffn_norm_w, L3_ffn_norm_b, L3_ffn_q_w, L3_ffn_q_b, L3_ffn_k_w, L3_ffn_k_b, L3_ffn_v_w, L3_ffn_v_b, L3_ffn_o_w, L3_ffn_o_b):
    import jax
    import jax.numpy as jnp

    def _L0_xattn_ref(query, key, value, Wq, bq, Wk, bk, Wv, bv, Er):
        import jax, jax.numpy as jnp
        import numpy as np
        import math
        D_MODEL = 256
        NUM_HEADS = 16
        MAX_LEN = 512
        D_HEAD = D_MODEL // NUM_HEADS
        BATCH = 2
        SEQ = 512

        def _skew(QEr):
            B, H, R, C = QEr.shape
            padded = jnp.pad(QEr, ((0, 0), (0, 0), (0, 0), (1, 0)))
            reshaped = padded.reshape(B, H, C + 1, R)
            return reshaped[:, :, 1:, :]
        B, S, D = query.shape
        H, dh = (NUM_HEADS, D_HEAD)
        q = (jnp.einsum('bsd,ed->bse', query, Wq) + bq).reshape(B, S, H, dh).transpose(0, 2, 1, 3)
        k = (jnp.einsum('bsd,ed->bse', key, Wk) + bk).reshape(B, S, H, dh).transpose(0, 2, 1, 3)
        v = (jnp.einsum('bsd,ed->bse', value, Wv) + bv).reshape(B, S, H, dh).transpose(0, 2, 1, 3)
        start = MAX_LEN - S
        Er_s = Er[start:, :]
        QEr = jnp.einsum('bhsd,ld->bhsl', q, Er_s)
        Srel = _skew(QEr)
        QK = jnp.einsum('bhsd,bhtd->bhst', q, k)
        attn = (QK + Srel) / math.sqrt(dh)
        causal = jnp.tril(jnp.ones((S, S), dtype=bool))
        attn = jnp.where(causal[None, None], attn, -jnp.inf)
        attn = jax.nn.softmax(attn, axis=-1)
        out = jnp.einsum('bhst,bhtd->bhsd', attn, v)
        out = out.transpose(0, 2, 1, 3).reshape(B, S, D)
        return out

    def _L0_ffn_ref(x, w_gate, w_up, w_down):
        import jax, jax.numpy as jnp
        import numpy as np
        BLOCK = 32
        W_BITS = 4
        ACT_BITS = 16

        def act_qdq(x):
            qmax = 2.0 ** (ACT_BITS - 1) - 1.0
            scale = jnp.maximum(jnp.max(jnp.abs(x)) / qmax, 1e-12)
            return jnp.clip(jnp.round(x / scale), -qmax - 1.0, qmax) * scale

        def fixed_qdq_u16(x):
            scale = 1.0 / 65536.0
            return jnp.clip(jnp.round(x / scale), 0.0, 65535.0) * scale

        def lpbq_dequant(w):
            O, I = w.shape
            qmax = 2.0 ** (W_BITS - 1) - 1.0
            wb = w.reshape(O, I // BLOCK, BLOCK)
            s = jnp.maximum(jnp.max(jnp.abs(wb), axis=-1, keepdims=True) / qmax, 1e-12)
            wq = jnp.clip(jnp.round(wb / s), -qmax - 1.0, qmax) * s
            return wq.reshape(O, I)
        x = act_qdq(x)
        up = act_qdq(x @ lpbq_dequant(w_up).T)
        gate = act_qdq(x @ lpbq_dequant(w_gate).T)
        sig = fixed_qdq_u16(jax.nn.sigmoid(gate))
        gate = act_qdq(gate * sig)
        o = act_qdq(gate * up)
        return o @ lpbq_dequant(w_down).T

    def _L1_xattn_ref(x, y, pad_mask, Wq, Wkv, Wproj, bproj):
        import jax, jax.numpy as jnp
        import numpy as np
        B, N, N2 = (4, 512, 256)
        DIM, DIM_Y, H = (256, 256, 16)
        HD = DIM // H
        SCALE = HD ** (-0.5)
        b, n, c = x.shape
        n2 = y.shape[1]
        q = (x @ Wq).reshape(b, n, H, HD).transpose(0, 2, 1, 3)
        kv = (y @ Wkv).reshape(b, n2, 2, H, HD).transpose(2, 0, 3, 1, 4)
        k, v = (kv[0], kv[1])
        scores = jnp.einsum('bhnd,bhmd->bhnm', q * SCALE, k)
        keep = pad_mask.astype(bool)[:, None, None, :]
        scores = jnp.where(keep, scores, -jnp.inf)
        attn = jax.nn.softmax(scores, axis=-1)
        out = jnp.einsum('bhnm,bhmd->bhnd', attn, v)
        out = out.transpose(0, 2, 1, 3).reshape(b, n, c)
        return out @ Wproj + bproj

    def _L1_ffn_ref(x, router_w, correction_bias, gate_w, up_w, down_w, shared_gate_w, shared_up_w, shared_down_w):
        import jax, jax.numpy as jnp
        import numpy as np
        E = 16
        G = 4
        EPG = E // G
        K = 4
        TOPK_GROUP = 2
        PER_GROUP_K = K // TOPK_GROUP

        def _route(xf, router_w, correction_bias):
            S = xf.shape[0]
            logits = xf @ router_w.T
            scores = jax.nn.sigmoid(logits)
            sb = scores + correction_bias
            grp_top = jax.lax.top_k(sb.reshape(S, G, EPG), PER_GROUP_K)[0]
            group_scores = grp_top.sum(axis=-1)
            _, group_idx = jax.lax.top_k(group_scores, TOPK_GROUP)
            group_mask = jnp.zeros((S, G), sb.dtype).at[jnp.arange(S)[:, None], group_idx].set(1.0)
            score_mask = jnp.broadcast_to(group_mask[:, :, None], (S, G, EPG)).reshape(S, E)
            masked = jnp.where(score_mask > 0, sb, -jnp.inf)
            _, topk_idx = jax.lax.top_k(masked, K)
            w = jnp.take_along_axis(scores, topk_idx, axis=1)
            w = w / (w.sum(axis=-1, keepdims=True) + 1e-20)
            return (topk_idx, w, scores)
        B, T, C = x.shape
        S = B * T
        xf = x.reshape(S, C)
        sg = xf @ shared_gate_w.T
        su = xf @ shared_up_w.T
        shared_out = jax.nn.silu(sg) * su @ shared_down_w.T
        topk_idx, w, _scores = _route(xf, router_w, correction_bias)
        combine = jnp.zeros((S, E), xf.dtype).at[jnp.arange(S)[:, None], topk_idx].add(w)
        g = jnp.einsum('sc,ech->esh', xf, gate_w)
        u = jnp.einsum('sc,ech->esh', xf, up_w)
        h = jax.nn.silu(g) * u
        hw = h * combine.T[:, :, None]
        routed = jnp.einsum('esh,ehc->sc', hw, down_w)
        return (shared_out + routed).reshape(B, T, C)

    def _L2_xattn_ref(q, k, v, igate_w, igate_b, fgate_w, fgate_b, ln_scale):
        import jax, jax.numpy as jnp
        import numpy as np
        B, S, D, NH = (2, 512, 256, 8)
        DH = D // NH
        EPS = 1e-06
        LN_EPS = 1e-05

        def _mlstm_cell(q, k, v, igate_w, igate_b, fgate_w, fgate_b, ln_scale):
            Slen = q.shape[0]
            ifg = jnp.concatenate([q, k, v], axis=-1)
            ig = (ifg @ igate_w.T + igate_b).T
            fg = (ifg @ fgate_w.T + fgate_b).T
            qh = q.reshape(Slen, NH, DH).transpose(1, 0, 2)
            kh = k.reshape(Slen, NH, DH).transpose(1, 0, 2)
            vh = v.reshape(Slen, NH, DH).transpose(1, 0, 2)
            log_f = jax.nn.log_sigmoid(fg)
            cs = jnp.cumsum(log_f, axis=1)
            fg_mat = cs[:, :, None] - cs[:, None, :]
            mask = jnp.tril(jnp.ones((Slen, Slen), dtype=bool))
            log_fg_mat = jnp.where(mask, fg_mat, -jnp.inf)
            log_D = log_fg_mat + ig[:, None, :]
            max_log_D = jnp.max(log_D, axis=-1, keepdims=True)
            D_mat = jnp.exp(log_D - max_log_D)
            qk = jnp.einsum('hsd,htd->hst', qh, kh) / np.sqrt(DH)
            C = qk * D_mat
            normalizer = jnp.maximum(jnp.abs(C.sum(axis=-1, keepdims=True)), jnp.exp(-max_log_D))
            h = jnp.einsum('hst,htd->hsd', C / (normalizer + EPS), vh)
            h = h.transpose(1, 0, 2).reshape(Slen, D)
            mu = h.mean(axis=-1, keepdims=True)
            var = h.var(axis=-1, keepdims=True)
            return (h - mu) / jnp.sqrt(var + LN_EPS) * ln_scale
        return jax.vmap(lambda qq, kk, vv: _mlstm_cell(qq, kk, vv, igate_w, igate_b, fgate_w, fgate_b, ln_scale))(q, k, v)

    def _L2_ffn_ref(x, wqkv, q_scale, k_scale, wo, ln_g, ln_b, w1, b1, w2, b2):
        import jax, jax.numpy as jnp
        import numpy as np
        DIM = 256
        DEPTH = 2
        HEADS = 8
        DIM_HEAD = 64
        WINDOW = 128
        INNER = HEADS * DIM_HEAD
        HID = int(DIM * 4 * 2 / 3)
        B, N = (2, 2048)
        QK_SCALE = 8.0

        def shift_token(t):
            t1, t2 = jnp.split(t, 2, axis=-1)
            t2 = jnp.pad(t2, ((0, 0), (1, 0), (0, 0)))[:, :-1]
            return jnp.concatenate([t1, t2], axis=-1)

        def l2norm(t):
            return t / jnp.clip(jnp.linalg.norm(t, axis=-1, keepdims=True), 1e-12)

        def rotate_half(x):
            x1, x2 = jnp.split(x, 2, axis=-1)
            return jnp.concatenate([-x2, x1], axis=-1)

        def rotary_xpos(q, k):
            n = q.shape[-2]
            half_idx = jnp.arange(0, DIM_HEAD, 2, dtype=jnp.float32)
            inv_freq = 1.0 / 10000.0 ** (half_idx / DIM_HEAD)
            t = jnp.arange(n, dtype=jnp.float32)
            freqs = t[:, None] * inv_freq[None, :]
            freqs = jnp.concatenate([freqs, freqs], axis=-1)
            base = (half_idx + 0.4 * DIM_HEAD) / (1.4 * DIM_HEAD)
            power = (t - n // 2) / float(WINDOW // 2)
            scale = base[None, :] ** power[:, None]
            scale = jnp.concatenate([scale, scale], axis=-1)
            cos, sin = (jnp.cos(freqs), jnp.sin(freqs))
            q = q * cos * scale + rotate_half(q) * sin * scale
            k = k * cos / scale + rotate_half(k) * sin / scale
            return (q, k)

        def local_attention(q, k, v):
            b, h, n, d = q.shape
            w = n // WINDOW
            bq = q.reshape(b, h, w, WINDOW, d) * QK_SCALE
            bk = k.reshape(b, h, w, WINDOW, d)
            bv = v.reshape(b, h, w, WINDOW, d)

            def look_around(t):
                p = jnp.pad(t, ((0, 0), (0, 0), (1, 0), (0, 0), (0, 0)))
                return jnp.concatenate([p[:, :, :w], p[:, :, 1:]], axis=3)
            bk, bv = (look_around(bk), look_around(bv))
            bt = jnp.arange(n).reshape(w, WINDOW)
            btp = jnp.pad(bt, ((1, 0), (0, 0)), constant_values=-1)
            btk = jnp.concatenate([btp[:w], btp[1:]], axis=1)
            sim = jnp.einsum('bhwid,bhwjd->bhwij', bq, bk)
            i = bt[:, :, None]
            j = btk[:, None, :]
            mask = (i < j) | (i > j + WINDOW) | (j == -1)
            sim = jnp.where(mask, -jnp.finfo(sim.dtype).max, sim)
            attn = jax.nn.softmax(sim, axis=-1)
            out = jnp.einsum('bhwij,bhwjd->bhwid', attn, bv)
            return out.reshape(b, h, n, d)

        def _layer(x, wqkv, qs, ksc, wo, lg, lb, w1, b1, w2, b2):
            b, n, _ = x.shape
            h = shift_token(x)
            qkv = h @ wqkv
            q, k, v = jnp.split(qkv, 3, axis=-1)
            to_heads = lambda t: t.reshape(b, n, HEADS, DIM_HEAD).transpose(0, 2, 1, 3)
            q, k, v = (to_heads(q), to_heads(k), to_heads(v))
            q = l2norm(q) * qs
            k = l2norm(k) * ksc
            q, k = rotary_xpos(q, k)
            o = local_attention(q, k, v)
            o = o.transpose(0, 2, 1, 3).reshape(b, n, INNER)
            x = x + o @ wo
            h = shift_token(x)
            mu = h.mean(-1, keepdims=True)
            var = h.var(-1, keepdims=True)
            h = (h - mu) / jnp.sqrt(var + 1e-05) * lg + lb
            h = h @ w1 + b1
            a, g = jnp.split(h, 2, axis=-1)
            h = a * jax.nn.gelu(g, approximate=False)
            x = x + h @ w2 + b2
            return x
        for l in range(DEPTH):
            x = _layer(x, wqkv[l], q_scale[l], k_scale[l], wo[l], ln_g[l], ln_b[l], w1[l], b1[l], w2[l], b2[l])
        return x

    def _L3_xattn_ref(query, key, value, qpos, kpos, Wq, bq, Wk, bk, Wv, bv, Wo, bo):
        import jax, jax.numpy as jnp
        import numpy as np
        DIM = 256
        HEADS = 16
        HEAD_DIM = DIM // HEADS
        SCALE = HEAD_DIM ** (-0.5)
        B, Nq, C = query.shape

        def split_heads(x):
            return x.reshape(x.shape[0], x.shape[1], HEADS, HEAD_DIM).transpose(0, 2, 1, 3)
        q = split_heads(query @ Wq + bq)
        k = split_heads(key @ Wk + bk)
        v = split_heads(value @ Wv + bv)
        attn = jnp.einsum('bhqd,bhkd->bhqk', q, k) * SCALE
        attn = jax.nn.softmax(attn, axis=-1)
        x = jnp.einsum('bhqk,bhkd->bhqd', attn, v)
        x = x.transpose(0, 2, 1, 3).reshape(B, Nq, C)
        return x @ Wo + bo

    def _L3_ffn_ref(x, router_prob, norm_w, norm_b, q_w, q_b, k_w, k_b, v_w, v_b, o_w, o_b):
        import jax, jax.numpy as jnp
        import numpy as np
        B, T, D, E, H = (4, 512, 256, 4, 8)
        EPS = 1e-05

        def _uniform(k, shape, bound):
            return jax.random.uniform(k, shape, jnp.float32, -bound, bound)

        def _layernorm(x, w, b):
            mu = jnp.mean(x, axis=-1, keepdims=True)
            var = jnp.mean(jnp.square(x - mu), axis=-1, keepdims=True)
            return (x - mu) * jax.lax.rsqrt(var + EPS) * w + b
        e_cnt = router_prob.shape[2]
        b, t, d = x.shape
        n = t // e_cnt
        h = H
        scale = d ** (-0.5)
        qs, ks_, vs = ([], [], [])
        for e in range(e_cnt):
            xe = x[:, e * n:(e + 1) * n, :]
            xn = _layernorm(xe, norm_w, norm_b)
            m = d // 2 ** e
            xm = xn[..., :m]
            qs.append(jnp.einsum('bnm,dm->bnd', xm, q_w[:, :m]) + q_b)
            ks_.append(jnp.einsum('bnm,dm->bnd', xm, k_w[:, :m]) + k_b)
            vs.append(jnp.einsum('bnm,dm->bnd', xm, v_w[:, :m]) + v_b)
        q = jnp.concatenate(qs, axis=1)
        k = jnp.concatenate(ks_, axis=1)
        v = jnp.concatenate(vs, axis=1)
        dh = d // h
        q = q.reshape(b, t, h, dh).transpose(0, 2, 1, 3)
        k = k.reshape(b, t, h, dh).transpose(0, 2, 1, 3)
        v = v.reshape(b, t, h, dh).transpose(0, 2, 1, 3)
        attn = jnp.einsum('bhqd,bhkd->bhqk', q, k) * scale
        attn = jax.nn.softmax(attn, axis=-1)
        attn_out = jnp.einsum('bhqk,bhkd->bhqd', attn, v)
        attn_out = attn_out.transpose(0, 2, 1, 3).reshape(b, t, d)
        outs = []
        for e in range(e_cnt):
            sl = slice(e * n, (e + 1) * n)
            m = d // 2 ** e
            xm = attn_out[:, sl, :m]
            out = jnp.einsum('bnm,om->bno', xm, o_w[:m, :m]) + o_b[:m]
            pad = d - m
            if pad:
                out = jnp.pad(out, ((0, 0), (0, 0), (0, pad)))
            outs.append(out + x[:, sl, :])
        return jnp.concatenate(outs, axis=1)
    x = x + jnp.tanh(g_xattn[0]) * _L0_xattn_ref(_layernorm(x, axis=-1), ctx_1024, ctx_1024, L0_xattn_Wq, L0_xattn_bq, L0_xattn_Wk, L0_xattn_bk, L0_xattn_Wv, L0_xattn_bv, L0_xattn_Er)
    x = x + jnp.tanh(g_ffn[0]) * _L0_ffn_ref(_layernorm(x, axis=-1), L0_ffn_w_gate, L0_ffn_w_up, L0_ffn_w_down)
    x = x + jnp.tanh(g_xattn[1]) * _L1_xattn_ref(_layernorm(x, axis=-1), ctx_1024, mask_BxS2_ik0, L1_xattn_Wq, L1_xattn_Wkv, L1_xattn_Wproj, L1_xattn_bproj)
    x = x + jnp.tanh(g_ffn[1]) * _L1_ffn_ref(_layernorm(x, axis=-1), L1_ffn_router_w, L1_ffn_correction_bias, L1_ffn_gate_w, L1_ffn_up_w, L1_ffn_down_w, L1_ffn_shared_gate_w, L1_ffn_shared_up_w, L1_ffn_shared_down_w)
    x = x + jnp.tanh(g_xattn[2]) * _L2_xattn_ref(_layernorm(x, axis=-1), ctx_1024, ctx_1024, L2_xattn_igate_w, L2_xattn_igate_b, L2_xattn_fgate_w, L2_xattn_fgate_b, L2_xattn_ln_scale)
    x = x + jnp.tanh(g_ffn[2]) * _L2_ffn_ref(_layernorm(x, axis=-1), L2_ffn_wqkv, L2_ffn_q_scale, L2_ffn_k_scale, L2_ffn_wo, L2_ffn_ln_g, L2_ffn_ln_b, L2_ffn_w1, L2_ffn_b1, L2_ffn_w2, L2_ffn_b2)
    x = x + jnp.tanh(g_xattn[3]) * _L3_xattn_ref(_layernorm(x, axis=-1), ctx_1024, ctx_1024, itok_BxS2_0_2047, itok_BxS2_0_2047, L3_xattn_Wq, L3_xattn_bq, L3_xattn_Wk, L3_xattn_bk, L3_xattn_Wv, L3_xattn_bv, L3_xattn_Wo, L3_xattn_bo)
    x = x + jnp.tanh(g_ffn[3]) * _L3_ffn_ref(_layernorm(x, axis=-1), L3_ffn_router_prob, L3_ffn_norm_w, L3_ffn_norm_b, L3_ffn_q_w, L3_ffn_q_b, L3_ffn_k_w, L3_ffn_k_b, L3_ffn_v_w, L3_ffn_v_b, L3_ffn_o_w, L3_ffn_o_b)
    return x

_drawn_inputs = setup_inputs


def setup_inputs(seed=0):
    import zlib

    import numpy as np

    out = dict(_drawn_inputs(seed))
    spreads = {'L1_xattn_bproj': (0.0, 0.1),
     'L1_ffn_correction_bias': (0.0, 0.522),
     'L2_xattn_ln_scale': (1.0, 0.2),
     'L2_ffn_q_scale': (1.0, 0.6),
     'L2_ffn_k_scale': (1.0, 0.6),
     'L2_ffn_ln_g': (1.0, 0.6),
     'L2_ffn_ln_b': (0.0, 0.8),
     'L2_ffn_b1': (0.0, 0.309),
     'L2_ffn_b2': (0.0, 0.1),
     'L3_xattn_bq': (0.0, 0.295),
     'L3_xattn_bk': (0.0, 2.0),
     'L3_xattn_bv': (0.0, 0.1),
     'L3_xattn_bo': (0.0, 0.1),
     'L3_ffn_norm_w': (1.0, 0.6),
     'L3_ffn_norm_b': (0.0, 0.8)}
    factors = {'L0_xattn_bk': 64.0,
     'L1_xattn_Wq': 5.999,
     'L1_ffn_router_w': 4.629,
     'L1_ffn_gate_w': 3.746,
     'L1_ffn_up_w': 3.602,
     'L1_ffn_down_w': 3.446,
     'L3_ffn_q_w': 8.0,
     'L3_ffn_q_b': 29.371,
     'L3_ffn_k_w': 8.0,
     'L3_ffn_k_b': 64.0,
     'L3_ffn_v_b': 8.0,
     'L3_ffn_o_b': 3.77}
    for name, (base, spread) in spreads.items():
        noise = np.random.default_rng([zlib.crc32(name.encode()), seed]).standard_normal(out[name].shape)
        drawn = base * np.exp(spread * noise) if base else spread * noise
        out[name] = jnp.asarray(drawn.astype(out[name].dtype))
    for name, factor in factors.items():
        out[name] = (out[name] * factor).astype(out[name].dtype)
    return out
```

```python
from contextlib import ExitStack, contextmanager

import concourse.bass as bass
from concourse import mybir

STAGES = (0, 1, 2, 3, 4, 5, 6, 7)

F32 = mybir.dt.float32
BF16 = mybir.dt.bfloat16
ALU = mybir.AluOpType
ACT = mybir.ActivationFunctionType
AX = mybir.AxisListType

P = 128
NB = 8
S = 512
D = 256
NT = S // P
TT = NB * NT
KT = D // P
TOK = NB * S
BIG = 1.0e30
LN_EPS = 1e-5
ds = bass.ds

TERMS = ((1, 1), (1, 2), (2, 1), (1, 3), (3, 1), (2, 2))


def alone(eng):
    eng.nop(nofuse=True)


class Chain:

    def __init__(self, eng, sem):
        self.eng, self.sem, self.base, self.n = eng, sem, 0, 0

    def at(self, base):
        self.base, self.n = base, 0

    def mark(self, ins):
        ins.then_inc(self.sem, 1)
        self.n += 1
        return self.n

    def wait(self, n=None):
        self.eng.wait_ge(self.sem, self.base + (self.n if n is None else n))

    def link(self, ins):
        self.mark(ins)
        self.wait()

    def done(self, k):
        assert self.n == k, (self.n, k)


@contextmanager
def phase(nc, name, sems):
    with ExitStack() as ctx:
        got = {s: nc.alloc_semaphore(f"{name}_{s}") for s in sems.split()}

        def sb(what, shape, dt=F32):
            return ctx.enter_context(nc.sbuf_tensor(f"{name}_{what}", shape, dt))

        def ps(what, shape, dt=F32):
            return ctx.enter_context(nc.psum_tensor(f"{name}_{what}", shape, dt))

        yield got, sb, ps
    nc.clear_and_free_semaphores(list(got.values()))
    nc.all_engine_barrier()


def w_view(w):
    return w.rearrange("(k p) n -> p k n", p=P)


def constants(nc, G, a):
    with phase(nc, "const", "loaded cast done") as (s, sb, ps):
        masks32 = sb("masks32", [P, 3, P])
        graw = sb("graw", [P, 8])
        with nc.Block() as block:

            @block.sync
            def _(sp):
                sp.dma_start(G.X[:, :, :], a["x"].rearrange("b (t p) d -> p (b t) d", p=P)).then_inc(s["loaded"], 16)
                sp.dma_start(G.ident[:, :], a["c_ident"]).then_inc(s["loaded"], 16)
                sp.dma_start(masks32[:, :, :], a["c_masks"].rearrange("m p c -> p m c")).then_inc(s["loaded"], 16)
                sp.dma_start(graw[:, 0:4], a["g_xattn"].unsqueeze(0).broadcast_to([P, 4])).then_inc(s["loaded"], 16)
                sp.dma_start(graw[:, 4:8], a["g_ffn"].unsqueeze(0).broadcast_to([P, 4])).then_inc(s["loaded"], 16)

            @block.scalar
            def _(act):
                act.wait_ge(s["loaded"], 80)
                nc.scalar.activation(G.gate[:, :], graw[:, :], ACT.Tanh).then_inc(s["done"], 1)

            @block.vector
            def _(dve):
                dve.wait_ge(s["loaded"], 80)
                nc.vector.tensor_copy(G.identb[:, :], G.ident[:, :])
                nc.vector.tensor_copy(G.masks[:, :, :], masks32[:, :, :])
                nc.vector.memset(G.ones[:, :], 1.0)
                nc.vector.memset(G.mhalf[:, :], -0.5).then_inc(s["done"], 1)


def store(nc, G, a):
    with phase(nc, "store", "stored") as (s, sb, ps):
        with nc.Block() as block:

            @block.sync
            def _(sp):
                sp.dma_start(a["out"].rearrange("b (t p) d -> p (b t) d", p=P), G.X[:, :, :]).then_inc(s["stored"], 16)
                sp.wait_ge(s["stored"], 16)


def qkv(nc, G, name, src, jobs, weights, vjob, ctx=None, affine=None, tile_k=None, nlog=0):
    nj = len(jobs)
    scaled = sorted({(j[3], j[4]) for j in jobs if j[3] and j[4] != 1.0})
    with phase(nc, name, "w c0 c1 c_free stats rstd xn xn_free xt_ps xt_ps_free xt xt_free "
               "job job_free q32 q32_free parts parts_st0 parts_st1 v v_free v_sb v_st0 v_st1 dvc poolc actc") as (s, sb, ps):
        W = {k: sb(k, shape) for k, (view, shape) in weights.items()}
        xn = sb("xn", [P, 2, NT, D])
        xT = sb("xT", [P, 2, KT, S])
        cT = sb("cT", [P, 2, KT, S])
        st = sb("st", [P, NT, 6])
        mv = sb("mv", [P, 2, NT, 2])
        rstd = sb("rstd", [P, 2, NT])
        q32 = sb("q32", [P, 2, S])
        r1 = sb("r1", [P, S])
        r2 = sb("r2", [P, S])
        parts = sb("parts", [P, 2, 3, S], BF16)
        vw, vsrc, vb, vdst, VW = vjob
        NVB = NT * VW // S
        VT = S // VW
        vsb = sb("vsb", [P, 2, NT, VW])
        xps = ps("xps", [P, KT, S])
        jps = ps("jps", [P, 4, S])
        vps = ps("vps", [P, 2, S])
        link_per_batch = 5 * nj + 1

        with nc.Block() as block:

            @block.sync
            def _(sp):
                for c in ("parts_st0", "parts_st1", "v_st0", "v_st1"):
                    sp.sem_inc(s[c], 16)
                for k, (view, shape) in weights.items():
                    sp.dma_start(W[k][tuple(slice(None) for _ in shape)], view).then_inc(s["w"], 16)
                with sp.Fori(0, NB // 2) as it:
                    for p in range(2):
                        b = it * 2 + p
                        if ctx is not None:
                            sp.wait_ge(s["c_free"], b + 1)
                            sp.dma_start(cT[:, p], ctx.rearrange("(k p) t -> p k t", p=P)[:, :, ds(b * S, S)]).then_inc(s[f"c{p}"], 16)
                        for j, (wn, blk, sc, bias, scale, dst, row) in enumerate(jobs):
                            sp.wait_ge(s["parts"], b * nj + j + 1)
                            alone(sp)
                            sp.dma_start(dst.rearrange("r f t -> f r t")[row:row + P, :, ds(b * S, S)],
                                         parts[:, j % 2]).then_inc(s[f"parts_st{j % 2}"], 16)
                        sp.wait_ge(s["v_sb"], (b + 1) * NVB)
                        sp.dma_start(vdst.rearrange("(t p) d -> p t d", p=P)[:, ds(b * NT, NT), :], vsb[:, p]).then_inc(s[f"v_st{p}"], 16)
                sp.wait_ge(s["parts_st0"], 16 + 16 * NB * ((nj + 1) // 2))
                sp.wait_ge(s["parts_st1"], 16 + 16 * NB * (nj // 2))
                for p in range(2):
                    sp.wait_ge(s[f"v_st{p}"], 16 + 16 * NB // 2)

            @block.gpsimd
            def _(pool):
                ch = Chain(pool, s["poolc"])
                with pool.Fori(0, NB // 2) as it:
                    for p in range(2):
                        b = it * 2 + p
                        ch.at(b)
                        pool.wait_ge(s["stats"], b + 1)
                        alone(pool)
                        ch.link(nc.gpsimd.tensor_scalar(rstd[:, p, :], mv[:, p, :, 1], LN_EPS, None, ALU.add))
                        nc.gpsimd.tensor_tensor(rstd[:, p, :], rstd[:, p, :], G.mhalf[:, 0:NT], ALU.pow).then_inc(s["rstd"], 1)
                        ch.done(1)

            @block.vector
            def _(dve):
                ch = Chain(dve, s["dvc"])
                dve.sem_inc(s["q32_free"], 2)
                with dve.Fori(0, NB // 2) as it:
                    for p in range(2):
                        b = it * 2 + p
                        ch.at(b * link_per_batch)
                        for t in range(NT):
                            last = nc.vector.bn_stats(st[:, t, :], src[:, ds(b * NT + t, 1), :].rearrange("p o d -> p (o d)"))
                        ch.link(last)
                        alone(dve)
                        for t in range(NT):
                            last = nc.vector.bn_aggr(mv[:, p, t, :], st[:, t, :])
                        last.then_inc(s["stats"], 1)
                        dve.wait_ge(s["rstd"], b + 1)
                        dve.wait_ge(s["xn_free"], b + 1)
                        for t in range(NT):
                            last = nc.vector.tensor_scalar(xn[:, p, t, :], src[:, ds(b * NT + t, 1), :].rearrange("p o d -> p (o d)"),
                                                           mv[:, p, t, 0:1], rstd[:, p, t:t + 1], ALU.subtract, ALU.mult)
                        last.then_inc(s["xn"], 1)
                        for j in range(nj):
                            dve.wait_ge(s["q32"], b * nj + j + 1)
                            q = q32[:, j % 2, :]
                            k = (nj + 1 - j % 2) // 2
                            dve.wait_ge(s[f"parts_st{j % 2}"], b * (16 * k) + 16 * (j // 2) + 16)
                            ch.link(nc.vector.tensor_copy(parts[:, j % 2, 0, :], q))
                            ch.link(nc.vector.tensor_tensor(r1[:, :], q, parts[:, j % 2, 0, :], ALU.subtract))
                            ch.link(nc.vector.tensor_copy(parts[:, j % 2, 1, :], r1[:, :]))
                            ch.link(nc.vector.tensor_tensor(r2[:, :], r1[:, :], parts[:, j % 2, 1, :], ALU.subtract))
                            ch.link(nc.vector.tensor_copy(parts[:, j % 2, 2, :], r2[:, :]))
                            dve.sem_inc(s["parts"], 1)
                            dve.sem_inc(s["q32_free"], 1)
                        ch.done(link_per_batch)

            @block.scalar
            def _(act):
                act.sem_inc(s["xt_ps_free"], 1)
                act.sem_inc(s["job_free"], 4)
                act.sem_inc(s["v_free"], 2)
                act.wait_ge(s["w"], 16 * len(weights))
                for bias, scale in scaled:
                    nc.scalar.activation(W[bias][:, :], W[bias][:, :], ACT.Copy, scale=scale).then_inc(s["actc"], 1)
                if scaled:
                    act.wait_ge(s["actc"], len(scaled))
                with act.Fori(0, NB // 2) as it:
                    for p in range(2):
                        b = it * 2 + p
                        act.wait_ge(s["xt_ps"], b + 1)
                        act.wait_ge(s["xt_free"], b + 1)
                        for k in range(KT):
                            if affine:
                                last = nc.scalar.activation(xT[:, p, k, :], xps[:, k, :], ACT.Identity,
                                                            scale=W[affine[0]][:, k:k + 1], bias=W[affine[1]][:, k:k + 1])
                            else:
                                last = nc.scalar.copy(xT[:, p, k, :], xps[:, k, :])
                        last.then_inc(s["xt"], 1)
                        act.sem_inc(s["xt_ps_free"], 1)
                        for j, (wn, blk, sc, bias, scale, dst, row) in enumerate(jobs):
                            act.wait_ge(s["job"], b * nj + j + 1)
                            act.wait_ge(s["q32_free"], b * nj + j + 1)
                            o = q32[:, j % 2, :]
                            if bias:
                                ins = nc.scalar.activation(o, jps[:, j % 4, :], ACT.Identity, scale=scale, bias=W[bias][:, blk:blk + 1])
                            else:
                                ins = nc.scalar.activation(o, jps[:, j % 4, :], ACT.Copy, scale=scale)
                            ins.then_inc(s["q32"], 1)
                            act.wait_ge(s["q32"], b * nj + j + 1)
                            act.sem_inc(s["job_free"], 1)
                        act.wait_ge(s[f"v_st{p}"], it * 16 + 16)
                        for v in range(NVB):
                            act.wait_ge(s["v"], b * NVB + v + 1)
                            nc.scalar.copy(vsb[:, p, v * VT:(v + 1) * VT, :], vps[:, v % 2, :].rearrange("p (t d) -> p t d", d=VW)).then_inc(s["v_sb"], 1)
                            act.wait_ge(s["v_sb"], b * NVB + v + 1)
                            act.sem_inc(s["v_free"], 1)

            @block.tensor
            def _(pe):
                pe.sem_inc(s["xn_free"], 2)
                pe.sem_inc(s["xt_free"], 2)
                pe.sem_inc(s["c_free"], 2)
                pe.wait_ge(s["w"], 16 * len(weights))
                with pe.Fori(0, NB // 2) as it:
                    for p in range(2):
                        b = it * 2 + p
                        pe.wait_ge(s["xn"], b + 1)
                        pe.wait_ge(s["xt_ps_free"], b + 1)
                        for k in range(KT):
                            for t in range(NT):
                                last = nc.tensor.transpose(xps[:, k, t * P:(t + 1) * P], xn[:, p, t, k * P:(k + 1) * P], G.ident[:, :])
                        last.then_inc(s["xt_ps"], 1)
                        pe.wait_ge(s["xt_ps"], b + 1)
                        pe.sem_inc(s["xn_free"], 1)
                        if ctx is not None:
                            pe.wait_ge(s[f"c{p}"], it * 16 + 16)
                        xt_waited = False

                        def source(sc):
                            return xT if sc == "x" else cT

                        order = list(enumerate(jobs))
                        for j, (wn, blk, sc, bias, scale, dst, row) in order:
                            if sc == "x" and not xt_waited:
                                pe.wait_ge(s["xt"], b + 1)
                                xt_waited = True
                            pe.wait_ge(s["job_free"], b * nj + j + 1)
                            o, w, x = jps[:, j % 4, :], W[wn], source(sc)
                            if tile_k:
                                for t in range(NT):
                                    ks = tile_k(t)
                                    for i, (k, rows) in enumerate(ks):
                                        last = nc.tensor.matmul(o[:, t * P:(t + 1) * P], w[0:rows, k, blk * P:(blk + 1) * P],
                                                                x[0:rows, p, k, t * P:(t + 1) * P], start=i == 0, stop=i == len(ks) - 1)
                            else:
                                for k in range(KT):
                                    last = nc.tensor.matmul(o, w[:, k, blk * P:(blk + 1) * P], x[:, p, k, :], start=k == 0, stop=k == KT - 1)
                            last.then_inc(s["job"], 1)
                        if vsrc == "x" and not xt_waited:
                            pe.wait_ge(s["xt"], b + 1)
                        for v in range(NVB):
                            pe.wait_ge(s["v_free"], b * NVB + v + 1)
                            for t in range(v * VT, (v + 1) * VT):
                                o = vps[:, v % 2, (t % VT) * VW:(t % VT + 1) * VW]
                                ks = tile_k(t) if tile_k else [(k, P) for k in range(KT)]
                                for i, (k, rows) in enumerate(ks):
                                    last = nc.tensor.matmul(o, source(vsrc)[0:rows, p, k, t * P:(t + 1) * P], W[vw][0:rows, k, 0:VW],
                                                            start=i == 0, stop=i == len(ks) - 1 and vb is None)
                                if vb:
                                    last = nc.tensor.matmul(o, G.ones[0:1, :], W[vb][0:1, 0:VW], start=False, stop=True)
                            last.then_inc(s["v"], 1)
                        pe.wait_ge(s["v"], (b + 1) * NVB)
                        pe.sem_inc(s["xt_free"], 1)
                        pe.sem_inc(s["c_free"], 1)


def attention(nc, G, name, qs, ks, vs, H, DH, blocks, masks=None, rel=None, maskrow=None, direct=None, odst=None):
    NC = max(1, 6 * DH // P + (6 * DH % P > 0)) if DH < 64 else 3
    TPC = 6 // NC
    KR = TPC * DH
    KX = KR + (1 if maskrow is not None else 0)
    HD = H * DH
    OB = NT * HD // S
    OD = 2 if OB <= 2 else 1
    TOT = sum(blocks(t)[1] - blocks(t)[0] for t in range(NT))
    OFF = [sum(blocks(u)[1] - blocks(u)[0] for u in range(t)) * P for t in range(NT)]
    RD = 2
    with phase(nc, name, "qk0 qk1 qk_free v0 v1 rel0 rel1 rel_free score least prob pt cp_dve cp_act pv "
               "out_free den_free o_sb o_st0 o_st1 o_st_sum dvc ones") as (s, sb, ps):
        Q = sb("Q", [P, 2, NC, H, S], BF16)
        K = sb("K", [P, 2, NC, H, S], BF16)
        V = sb("V", [P, 2, NT, HD])
        prob = sb("prob", [P, 2, S])
        probT = sb("probT", [P, 2, S])
        nmax = sb("nmax", [P, NT])
        den = sb("den", [P, 2, NT, H])
        rden = sb("rden", [P, NT, H])
        osb = sb("osb", [P, 2, NT, HD])
        if rel is not None:
            relsb = sb("relsb", [P, RD, TOT * P])
            summed = sb("summed", [P, 2, S])
        sps = ps("sps", [P, 2, S])
        tps = ps("tps", [P, 2, S])
        ops = ps("ops", [P, OD * OB, S])
        NL = 2 * (2 if direct is None else 3)
        LB = NL // 2
        nload = 12 + (1 if maskrow is not None else 0)

        def unit(b, h, t):
            return b * (H * NT) + h * NT + t

        with nc.Block() as block:

            @block.gpsimd
            def _(pool):
                if maskrow is not None:
                    for p in range(2):
                        last = nc.gpsimd.memset(Q[KR:KR + 1, p, 0], 1.0)
                    last.then_inc(s["ones"], 1)
                    pool.wait_ge(s["ones"], 1)
                with pool.Fori(0, NB // 2) as it:
                    for p in range(2):
                        b = it * 2 + p
                        pool.wait_ge(s["qk_free"], b + 1)
                        for i, (qp, kp) in enumerate(TERMS):
                            c, r = i // TPC, i % TPC
                            for dst, part, src in ((Q, qp, qs), (K, kp, ks)):
                                pool.dma_start(dst[r * DH:(r + 1) * DH, p, c],
                                               src[part - 1].rearrange("(h d) t -> d h t", d=DH)[:, :, ds(b * S, S)]).then_inc(s[f"qk{p}"], 16)
                        if maskrow is not None:
                            pool.dma_start(K[KR:KR + 1, p, 0], maskrow[ds(b, 1), :].unsqueeze(1).broadcast_to([1, H, S])).then_inc(s[f"qk{p}"], 16)
                        pool.dma_start(V[:, p], vs.rearrange("(t p) d -> p t d", p=P)[:, ds(b * NT, NT), :]).then_inc(s[f"v{p}"], 16)

            @block.sync
            def _(sp):
                if direct is None:
                    for p in range(2):
                        sp.sem_inc(s[f"o_st{p}"], 16)
                with sp.Fori(0, NB // 2) as it:
                    for p in range(2):
                        b = it * 2 + p
                        if rel is not None:
                            with sp.Fori(0, H // 2) as hh:
                                for hp in range(2):
                                    n = b * H + hh * 2 + hp
                                    sp.wait_ge(s["rel_free"], n + 1)
                                    alone(sp)
                                    for t in range(NT):
                                        w = (blocks(t)[1] - blocks(t)[0]) * P
                                        row = rel[t][ds(n, 1), P - 1:]
                                        skewed = bass.AP(row.tensor, row.offset, [[w - 1, P], [1, w]])
                                        sp.dma_start(relsb[:, hp, OFF[t]:OFF[t] + w], skewed).then_inc(s[f"rel{hp}"], 16)
                        if direct is None:
                            sp.wait_ge(s["o_sb"], b + 1)
                            alone(sp)
                            sp.dma_start(odst.rearrange("(t p) d -> p t d", p=P)[:, ds(b * NT, NT), :], osb[:, p]).then_inc(s[f"o_st{p}"], 16)
                if direct is None:
                    for p in range(2):
                        sp.wait_ge(s[f"o_st{p}"], 16 + 16 * NB // 2)

            @block.tensor
            def _(pe):
                pe.sem_inc(s["qk_free"], 2)

                def scores(p, b, h, t):
                    lo, hi = blocks(t)
                    w = (hi - lo) * P
                    o = sps[:, t % 2, 0:w]
                    extra = masks(t) if masks else []
                    for i, (kb, m) in enumerate(extra):
                        nc.tensor.matmul(o[:, (kb - lo) * P:(kb - lo + 1) * P], G.identb[:, :], G.masks[:, m, :],
                                         start=i == 0, stop=False, skip_group_check=True)
                    for c in range(NC):
                        rows = KX if c == 0 else KR
                        last = nc.tensor.matmul(o, Q[0:rows, p, c, ds(h, 1), t * P:(t + 1) * P].rearrange("p o t -> p (o t)"),
                                                K[0:rows, p, c, ds(h, 1), lo * P:hi * P].rearrange("p o t -> p (o t)"),
                                                start=c == 0 and not extra, stop=c == NC - 1, skip_group_check=bool(extra))
                    last.then_inc(s["score"], 1)

                def turn(p, b, h, t):
                    pe.wait_ge(s["prob"], unit(b, h, t) + 1)
                    lo, hi = blocks(t)
                    for kb in range(hi - lo):
                        last = nc.tensor.transpose(tps[:, t % 2, kb * P:(kb + 1) * P], prob[:, t % 2, kb * P:(kb + 1) * P], G.ident[:, :])
                    last.then_inc(s["pt"], 1)

                def weigh(p, b, h, t):
                    n = b * (H * NT // 2) + h * (NT // 2) + t // 2 + 1
                    pe.wait_ge(s["cp_act" if t % 2 else "cp_dve"], n)
                    lo, hi = blocks(t)
                    if HD == D:
                        o = ops[:, (p % OD) * OB + t // 2, ds(h * DH + (t % 2) * D, DH)]
                    else:
                        o = ops[:, t, ds(h * DH, DH)]
                    for kb in range(lo, hi):
                        last = nc.tensor.matmul(o, probT[:, t % 2, (kb - lo) * P:(kb - lo + 1) * P], V[:, p, kb, ds(h * DH, DH)],
                                                start=kb == lo, stop=kb == hi - 1, skip_group_check=True)
                    return last

                def head(p, b, h, final):
                    for t in range(NT):
                        if not (final and t >= NT - 2):
                            scores(p, b, h + (t + 2) // NT, (t + 2) % NT)
                        if not (final and t >= NT - 1):
                            turn(p, b, h + (t + 1) // NT, (t + 1) % NT)
                        last = weigh(p, b, h, t)
                    if final:
                        last.then_inc(s["pv"], 1)

                with pe.Fori(0, NB // 2) as it:
                    for p in range(2):
                        b = it * 2 + p
                        pe.wait_ge(s[f"qk{p}"], it * (16 * nload) + 16 * nload)
                        scores(p, b, 0, 0)
                        scores(p, b, 0, 1)
                        turn(p, b, 0, 0)
                        pe.wait_ge(s[f"v{p}"], it * 16 + 16)
                        pe.wait_ge(s["out_free"], b + 1)
                        alone(pe)
                        with pe.Fori(0, H - 1) as h:
                            head(p, b, h, False)
                        head(p, b, H - 1, True)
                        pe.wait_ge(s["pv"], b + 1)
                        pe.sem_inc(s["qk_free"], 1)

            @block.vector
            def _(dve):
                ch = Chain(dve, s["dvc"])
                dve.sem_inc(s["out_free"], OD)
                dve.sem_inc(s["den_free"], 2)
                if rel is not None:
                    dve.sem_inc(s["rel_free"], RD)

                def least(p, b, h, t):
                    lo, hi = blocks(t)
                    w = (hi - lo) * P
                    dve.wait_ge(s["score"], unit(b, h, t) + 1)
                    if rel is not None:
                        alone(dve)
                        nc.vector.tensor_tensor_reduce(out=summed[:, t % 2, 0:w], in0=sps[:, t % 2, 0:w],
                                                       in1=relsb[:, h_par[0], OFF[t]:OFF[t] + w], scale=1.0, scalar=3.0e38,
                                                       op0=ALU.add, op1=ALU.min, accum_out=nmax[:, t:t + 1]).then_inc(s["least"], 1)
                    else:
                        nc.vector.tensor_reduce(nmax[:, t:t + 1], sps[:, t % 2, 0:w], AX.X, ALU.max, negate=True).then_inc(s["least"], 1)

                h_par = [0]

                def copy(p, b, h, t):
                    lo, hi = blocks(t)
                    w = (hi - lo) * P
                    dve.wait_ge(s["pt"], unit(b, h, t) + 1)
                    nc.vector.tensor_copy(probT[:, t % 2, 0:w], tps[:, t % 2, 0:w]).then_inc(s["cp_dve"], 1)

                def head(p, b, h, hp, final):
                    for t in range(NT):
                        if t % 2 == 0:
                            copy(p, b, h, t)
                        if t == 2 and rel is not None:
                            dve.wait_ge(s["least"], unit(b, h, NT - 1) + 1)
                            dve.sem_inc(s["rel_free"], 1)
                            if not final:
                                if hp == 0:
                                    dve.wait_ge(s["rel1"], b * (8 * H * NT) + h_half(h, hp) * (16 * NT) + 16 * NT)
                                else:
                                    dve.wait_ge(s["rel0"], b * (8 * H * NT) + (h_half(h, hp) + 1) * (16 * NT) + 16 * NT)
                        if not (final and t >= NT - 2):
                            h_par[0] = hp if t < NT - 2 else 1 - hp
                            least(p, b, h + (t + 2) // NT, (t + 2) % NT)

                half_reg = [None]

                def h_half(h, hp):
                    return half_reg[0]

                with dve.Fori(0, NB // 2) as it:
                    for p in range(2):
                        b = it * 2 + p
                        h_par[0] = 0
                        if rel is not None:
                            dve.wait_ge(s["rel0"], b * (8 * H * NT) + 16 * NT)
                        least(p, b, 0, 0)
                        least(p, b, 0, 1)
                        if rel is None:
                            with dve.Fori(0, H - 1) as h:
                                head(p, b, h, 0, False)
                            head(p, b, H - 1, 0, True)
                        else:
                            with dve.Fori(0, H // 2 - 1) as hh:
                                half_reg[0] = hh
                                head(p, b, hh * 2, 0, False)
                                head(p, b, hh * 2 + 1, 1, False)
                            half_reg[0] = H // 2 - 1
                            head(p, b, H - 2, 0, False)
                            head(p, b, H - 1, 1, True)
                        ch.at(b * LB)
                        dve.wait_ge(s["pv"], b + 1)
                        dve.wait_ge(s["prob"], (b + 1) * (H * NT))
                        ch.link(nc.vector.reciprocal(rden[:, :, :], den[:, p, :, :]))
                        if direct is None:
                            dve.wait_ge(s[f"o_st{p}"], it * 16 + 16)
                        tb = NT // OB
                        for t in range(NT):
                            o = ops[:, (p % OD) * OB + t // tb, (t % tb) * HD:(t % tb + 1) * HD]
                            last = nc.vector.tensor_tensor(osb[:, p, t, :].rearrange("p (h d) -> p h d", d=DH),
                                                           o.rearrange("p (h d) -> p h d", d=DH),
                                                           rden[:, t, :].unsqueeze(2).broadcast_to([P, H, DH]), ALU.mult)
                        ch.link(last)
                        dve.sem_inc(s["out_free"], 1)
                        dve.sem_inc(s["den_free"], 1)
                        if direct is None:
                            dve.sem_inc(s["o_sb"], 1)
                        else:
                            x = G.X[:, ds(b * NT, NT), :].rearrange("p t d -> p (t d)")
                            ch.link(nc.vector.scalar_tensor_tensor(x, osb[:, p].rearrange("p t d -> p (t d)"),
                                                                   G.gate[:, direct:direct + 1], x, ALU.mult, ALU.add))
                        ch.done(LB)

            @block.scalar
            def _(act):
                def expo(p, b, h, t):
                    lo, hi = blocks(t)
                    w = (hi - lo) * P
                    act.wait_ge(s["least"], unit(b, h, t) + 1)
                    source = sps[:, t % 2, 0:w] if rel is None else summed[:, t % 2, 0:w]
                    nc.scalar.activation(prob[:, t % 2, 0:w], source, ACT.Exp, scale=1.0 if rel is None else -1.0,
                                         bias=nmax[:, t:t + 1], accum_out=den[:, p, t, ds(h, 1)]).then_inc(s["prob"], 1)

                def copy(p, b, h, t):
                    lo, hi = blocks(t)
                    w = (hi - lo) * P
                    act.wait_ge(s["pt"], unit(b, h, t) + 1)
                    nc.scalar.copy(probT[:, t % 2, 0:w], tps[:, t % 2, 0:w]).then_inc(s["cp_act"], 1)

                def head(p, b, h, final):
                    for t in range(NT):
                        if not (final and t == NT - 1):
                            expo(p, b, h + (t + 1) // NT, (t + 1) % NT)
                        if t % 2:
                            copy(p, b, h, t)

                with act.Fori(0, NB // 2) as it:
                    for p in range(2):
                        b = it * 2 + p
                        act.wait_ge(s["den_free"], b + 1)
                        expo(p, b, 0, 0)
                        with act.Fori(0, H - 1) as h:
                            head(p, b, h, False)
                        head(p, b, H - 1, True)


def rel_scores(nc, G, name, qs, er, rel):
    H, DH = 16, 16
    KR = 6 * DH
    with phase(nc, name, "er cast erp q0 q1 q_free mm mm_free_a mm_free_v cp_a cp_v st0 st1 dvc") as (s, sb, ps):
        er32 = sb("er32", [KR, S])
        erk = sb("erk", [KR, S], BF16)
        r1 = sb("r1", [KR, S])
        pbf = sb("pbf", [DH, 3, S], BF16)
        Q = sb("Q", [KR, 2, H, S], BF16)
        out = sb("out", [P, 2, 10 * P])
        o = ps("o", [P, 8, S])
        OFF = [0, P, 3 * P, 6 * P]

        with nc.Block() as block:

            @block.gpsimd
            def _(pool):
                pool.dma_start(er32[0:DH, :], er).then_inc(s["er"], 16)
                pool.wait_ge(s["cast"], 1)
                for i, (qp, kp) in enumerate(TERMS):
                    pool.dma_start(erk[i * DH:(i + 1) * DH, :], pbf[:, kp - 1, :]).then_inc(s["erp"], 16)
                with pool.Fori(0, NB // 2) as it:
                    for p in range(2):
                        b = it * 2 + p
                        pool.wait_ge(s["q_free"], b + 1)
                        for i, (qp, kp) in enumerate(TERMS):
                            pool.dma_start(Q[i * DH:(i + 1) * DH, p],
                                           qs[qp - 1].rearrange("(h d) t -> d h t", d=DH)[:, :, ds(b * S, S)]).then_inc(s[f"q{p}"], 16)

            @block.sync
            def _(sp):
                for hp in range(2):
                    sp.sem_inc(s[f"st{hp}"], 16 * NT)
                with sp.Fori(0, NB * H // 2) as i:
                    for hp in range(2):
                        n = i * 2 + hp
                        sp.wait_ge(s["cp_a"], n * 2 + 2)
                        sp.wait_ge(s["cp_v"], n * 2 + 2)
                        alone(sp)
                        for t in range(NT):
                            w = (t + 1) * P
                            sp.dma_start(rel[t][ds(n, 1), :].rearrange("o (p c) -> (o p) c", c=w),
                                         out[:, hp, OFF[t]:OFF[t] + w]).then_inc(s[f"st{hp}"], 16)
                for hp in range(2):
                    sp.wait_ge(s[f"st{hp}"], 16 * NT + 16 * NT * NB * H // 2)

            @block.tensor
            def _(pe):
                pe.sem_inc(s["q_free"], 2)
                pe.wait_ge(s["erp"], 96)
                with pe.Fori(0, NB // 2) as it:
                    for p in range(2):
                        b = it * 2 + p
                        pe.wait_ge(s[f"q{p}"], it * 96 + 96)
                        alone(pe)
                        with pe.Fori(0, H // 2) as hh:
                            for hp in range(2):
                                n = b * H + hh * 2 + hp
                                pe.wait_ge(s["mm_free_a"], n + 1)
                                pe.wait_ge(s["mm_free_v"], n + 1)
                                for t in range(NT):
                                    w = (t + 1) * P
                                    last = nc.tensor.matmul(o[:, hp * NT + t, 0:w], Q[:, p, ds(hh * 2 + hp, 1), t * P:(t + 1) * P].rearrange("p o t -> p (o t)"),
                                                            erk[:, S - w:S], start=True, stop=True)
                                last.then_inc(s["mm"], 1)
                        pe.wait_ge(s["mm"], (b + 1) * H)
                        pe.sem_inc(s["q_free"], 1)

            @block.vector
            def _(dve):
                ch = Chain(dve, s["dvc"])
                dve.wait_ge(s["er"], 16)
                ch.link(nc.vector.tensor_copy(pbf[:, 0, :], er32[0:DH, :]))
                ch.link(nc.vector.tensor_tensor(r1[0:DH, :], er32[0:DH, :], pbf[:, 0, :], ALU.subtract))
                ch.link(nc.vector.tensor_copy(pbf[:, 1, :], r1[0:DH, :]))
                ch.link(nc.vector.tensor_tensor(r1[0:DH, :], r1[0:DH, :], pbf[:, 1, :], ALU.subtract))
                nc.vector.tensor_copy(pbf[:, 2, :], r1[0:DH, :]).then_inc(s["cast"], 1)
                dve.sem_inc(s["mm_free_v"], 2)
                with dve.Fori(0, NB * H // 2) as i:
                    for hp in range(2):
                        n = i * 2 + hp
                        dve.wait_ge(s["mm"], n + 1)
                        dve.wait_ge(s[f"st{hp}"], i * (16 * NT) + 16 * NT)
                        for t in (0, 3):
                            w = (t + 1) * P
                            nc.vector.tensor_copy(out[:, hp, OFF[t]:OFF[t] + w], o[:, hp * NT + t, 0:w]).then_inc(s["cp_v"], 1)
                        dve.wait_ge(s["cp_v"], n * 2 + 2)
                        dve.sem_inc(s["mm_free_v"], 1)

            @block.scalar
            def _(act):
                act.sem_inc(s["mm_free_a"], 2)
                with act.Fori(0, NB * H // 2) as i:
                    for hp in range(2):
                        n = i * 2 + hp
                        act.wait_ge(s["mm"], n + 1)
                        act.wait_ge(s[f"st{hp}"], i * (16 * NT) + 16 * NT)
                        for t in (1, 2):
                            w = (t + 1) * P
                            nc.scalar.copy(out[:, hp, OFF[t]:OFF[t] + w], o[:, hp * NT + t, 0:w]).then_inc(s["cp_a"], 1)
                        act.wait_ge(s["cp_a"], n * 2 + 2)
                        act.sem_inc(s["mm_free_a"], 1)


def outproj(nc, G, name, src, w, shape, bias, gate, onto, also=None, tile_k=None):
    KO = shape[1]
    with phase(nc, name, "w o0 o1 o_free xt_ps xt_ps_free xt xt_free y y_free dvc") as (s, sb, ps):
        W = sb("W", shape)
        B = sb("B", [1, D])
        rows = sb("rows", [P, 2, NT, KO * P])
        xT = sb("xT", [P, 2, KO, S])
        xps = ps("xps", [P, KO, S])
        yps = ps("yps", [P, 2, S])
        nw = 2 if bias is not None else 1
        with nc.Block() as block:

            @block.sync
            def _(sp):
                sp.dma_start(W[:, :, :], w).then_inc(s["w"], 16)
                if bias is not None:
                    sp.dma_start(B[:, :], bias).then_inc(s["w"], 16)
                with sp.Fori(0, NB // 2) as it:
                    for p in range(2):
                        b = it * 2 + p
                        sp.wait_ge(s["o_free"], b + 1)
                        alone(sp)
                        sp.dma_start(rows[:, p], src.rearrange("(t p) d -> p t d", p=P)[:, ds(b * NT, NT), :]).then_inc(s[f"o{p}"], 16)

            @block.tensor
            def _(pe):
                pe.sem_inc(s["o_free"], 2)
                pe.sem_inc(s["xt_free"], 2)
                pe.wait_ge(s["w"], 16 * nw)
                with pe.Fori(0, NB // 2) as it:
                    for p in range(2):
                        b = it * 2 + p
                        pe.wait_ge(s[f"o{p}"], it * 16 + 16)
                        pe.wait_ge(s["xt_ps_free"], b + 1)
                        for k in range(KO):
                            for t in range(NT):
                                last = nc.tensor.transpose(xps[:, k, t * P:(t + 1) * P], rows[:, p, t, k * P:(k + 1) * P], G.ident[:, :])
                        last.then_inc(s["xt_ps"], 1)
                        pe.wait_ge(s["xt_ps"], b + 1)
                        pe.sem_inc(s["o_free"], 1)
                        pe.wait_ge(s["xt"], b + 1)
                        for v in range(2):
                            pe.wait_ge(s["y_free"], b * 2 + v + 1)
                            for t in (2 * v, 2 * v + 1):
                                ks = tile_k(t) if tile_k else [(k, P) for k in range(KO)]
                                m = min(D, sum(r for _, r in ks)) if tile_k else D
                                o = yps[:, v, (t % 2) * D:(t % 2) * D + m]
                                for i, (k, r) in enumerate(ks):
                                    last = nc.tensor.matmul(o, xT[0:r, p, k, t * P:(t + 1) * P], W[0:r, k, 0:m],
                                                            start=i == 0, stop=i == len(ks) - 1 and bias is None)
                                if bias is not None:
                                    last = nc.tensor.matmul(o, G.ones[0:1, :], B[0:1, 0:m], start=False, stop=True)
                            last.then_inc(s["y"], 1)
                        pe.wait_ge(s["y"], b * 2 + 2)
                        pe.sem_inc(s["xt_free"], 1)

            @block.scalar
            def _(act):
                act.sem_inc(s["xt_ps_free"], 1)
                with act.Fori(0, NB // 2) as it:
                    for p in range(2):
                        b = it * 2 + p
                        act.wait_ge(s["xt_ps"], b + 1)
                        act.wait_ge(s["xt_free"], b + 1)
                        for k in range(KO):
                            last = nc.scalar.copy(xT[:, p, k, :], xps[:, k, :])
                        last.then_inc(s["xt"], 1)
                        act.wait_ge(s["xt"], b + 1)
                        act.sem_inc(s["xt_ps_free"], 1)

            @block.vector
            def _(dve):
                ch = Chain(dve, s["dvc"])
                K = 4 if also is not None else 2
                dve.sem_inc(s["y_free"], 2)
                g = 1.0 if gate is None else G.gate[:, gate:gate + 1]
                with dve.Fori(0, NB // 2) as it:
                    for p in range(2):
                        b = it * 2 + p
                        ch.at(b * K)
                        for v in range(2):
                            dve.wait_ge(s["y"], b * 2 + v + 1)
                            if tile_k:
                                for t in (2 * v, 2 * v + 1):
                                    m = sum(r for _, r in tile_k(t))
                                    x = onto[:, ds(b * NT + t, 1), 0:m].rearrange("p o d -> p (o d)")
                                    last = nc.vector.scalar_tensor_tensor(x, yps[:, v, (t % 2) * D:(t % 2) * D + m], g, x, ALU.mult, ALU.add)
                            else:
                                x = onto[:, ds(b * NT + 2 * v, 2), :].rearrange("p t d -> p (t d)")
                                last = nc.vector.scalar_tensor_tensor(x, yps[:, v, :], g, x, ALU.mult, ALU.add)
                            ch.link(last)
                            dve.sem_inc(s["y_free"], 1)
                            if also is not None:
                                x = onto[:, ds(b * NT + 2 * v, 2), :].rearrange("p t d -> p (t d)")
                                y = also[:, ds(b * NT + 2 * v, 2), :].rearrange("p t d -> p (t d)")
                                ch.link(nc.vector.scalar_tensor_tensor(x, y, g, x, ALU.mult, ALU.add))
                        ch.done(K)


def normalise(nc, G, name, src, dst, absmax=None):
    with phase(nc, name, "stats rstd dvc poolc") as (s, sb, ps):
        st = sb("st", [P, TT, 6])
        mv = sb("mv", [P, TT, 2])
        rstd = sb("rstd", [P, TT])
        with nc.Block() as block:

            @block.vector
            def _(dve):
                ch = Chain(dve, s["dvc"])
                for t in range(TT):
                    last = nc.vector.bn_stats(st[:, t, :], src[:, t, :])
                ch.link(last)
                for t in range(TT):
                    last = nc.vector.bn_aggr(mv[:, t, :], st[:, t, :])
                last.then_inc(s["stats"], 1)
                dve.wait_ge(s["rstd"], 1)
                for t in range(TT):
                    last = nc.vector.tensor_scalar(dst[:, t, :], src[:, t, :], mv[:, t, 0:1], rstd[:, t:t + 1], ALU.subtract, ALU.mult)
                if absmax is not None:
                    ch.link(last)
                    nc.vector.tensor_reduce(absmax, dst, AX.X, ALU.max, apply_absolute_value=True)

            @block.gpsimd
            def _(pool):
                ch = Chain(pool, s["poolc"])
                pool.wait_ge(s["stats"], 1)
                ch.link(nc.gpsimd.tensor_scalar(rstd[:, :], mv[:, :, 1], LN_EPS, None, ALU.add))
                nc.gpsimd.tensor_tensor(rstd[:, :], rstd[:, :], G.mhalf[:, 0:TT], ALU.pow).then_inc(s["rstd"], 1)


def key_mask(nc, G, name, mask, dst):
    with phase(nc, name, "in cast out dvc") as (s, sb, ps):
        m = sb("m", [NB, S], mybir.dt.int32)
        f = sb("f", [NB, S])
        o = sb("o", [NB, S], BF16)
        with nc.Block() as block:

            @block.sync
            def _(sp):
                sp.dma_start(m[:, :], mask).then_inc(s["in"], 16)
                sp.wait_ge(s["cast"], 1)
                sp.dma_start(dst, o[:, :]).then_inc(s["out"], 16)
                sp.wait_ge(s["out"], 16)

            @block.vector
            def _(dve):
                dve.wait_ge(s["in"], 16)
                nc.vector.tensor_copy(f[:, :], m[:, :]).then_inc(s["dvc"], 1)
                dve.wait_ge(s["dvc"], 1)
                nc.vector.tensor_scalar(o[:, :], f[:, :], 0.0, -BIG, ALU.is_equal, ALU.mult).then_inc(s["cast"], 1)


MAGIC = 12582912.0


def turn(nc, G, name, src, dst, quant=None):
    with phase(nc, name, "ready turned copied dvc") as (s, sb, ps):
        rows = sb("rows", [P, 2, NT, D])
        xps = ps("xps", [P, 2, KT, S])
        with nc.Block() as block:

            @block.vector
            def _(dve):
                ch = Chain(dve, s["dvc"])
                with dve.Fori(0, NB // 2) as it:
                    for p in range(2):
                        b = it * 2 + p
                        ch.at(b)
                        x = src[:, ds(b * NT, NT), :]
                        dve.wait_ge(s["turned"], b + 1)
                        if quant is not None:
                            ch.link(nc.vector.tensor_scalar(rows[:, p], x, G.quant[:, quant, 1:2], MAGIC, ALU.mult, ALU.add))
                            nc.vector.tensor_scalar(rows[:, p], rows[:, p], MAGIC, G.quant[:, quant, 0:1], ALU.subtract, ALU.mult).then_inc(s["ready"], 1)
                        else:
                            ch.mark(nc.vector.tensor_copy(rows[:, p], x))
                            ch.wait()
                            dve.sem_inc(s["ready"], 1)

            @block.tensor
            def _(pe):
                pe.sem_inc(s["turned"], 2)
                with pe.Fori(0, NB // 2) as it:
                    for p in range(2):
                        b = it * 2 + p
                        pe.wait_ge(s["ready"], b + 1)
                        pe.wait_ge(s["copied"], b + 1)
                        for k in range(KT):
                            for t in range(NT):
                                last = nc.tensor.transpose(xps[:, p, k, t * P:(t + 1) * P], rows[:, p, t, k * P:(k + 1) * P], G.ident[:, :])
                        last.then_inc(s["turned"], 1)

            @block.scalar
            def _(act):
                act.sem_inc(s["copied"], 2)
                with act.Fori(0, NB // 2) as it:
                    for p in range(2):
                        b = it * 2 + p
                        act.wait_ge(s["turned"], b + 3)
                        for k in range(KT):
                            last = nc.scalar.copy(dst[:, k, ds(b * S, S)], xps[:, p, k, :])
                        last.then_inc(s["copied"], 1)


def grid(nc, G, name, maxima, what):
    with phase(nc, name, "mx all dvc") as (s, sb, ps):
        m = sb("m", [P, len(maxima)])
        g = sb("g", [P, len(maxima)])
        with nc.Block() as block:

            @block.vector
            def _(dve):
                ch = Chain(dve, s["dvc"])
                for i, x in enumerate(maxima):
                    last = nc.vector.tensor_reduce(m[:, i:i + 1], x, AX.X, ALU.max)
                last.then_inc(s["mx"], 1)
                dve.wait_ge(s["all"], 1)
                for i, q in enumerate(what):
                    ch.link(nc.vector.tensor_scalar(G.quant[:, q, 0:1], g[:, i:i + 1], 1.0 / 32767.0, 1e-12, ALU.mult, ALU.max))
                    nc.vector.reciprocal(G.quant[:, q, 1:2], G.quant[:, q, 0:1])

            @block.gpsimd
            def _(pool):
                pool.wait_ge(s["mx"], 1)
                nc.gpsimd.partition_all_reduce(g[:, :], m[:, :], P, bass.bass_isa.ReduceOp.max).then_inc(s["all"], 1)


def dequantise(nc, G, name, wg, wu, wd, gT, uT, dT):
    with phase(nc, name, "w ready turned copied dvc") as (s, sb, ps):
        NBK = 48
        raw = sb("raw", [P, 3, NBK, 32])
        amax = sb("amax", [P, 3, NBK])
        sc = sb("sc", [P, 3, NBK])
        inv = sb("inv", [P, 3, NBK])
        wps = ps("wps", [P, 2, S])
        with nc.Block() as block:

            @block.sync
            def _(sp):
                for i, (w, n) in enumerate(((wg, 8), (wu, 8), (wd, 24))):
                    sp.dma_start(raw[:, i].rearrange("p (o n) k -> p o (n k)", n=n), w.rearrange("(o p) i -> p o i", p=P)).then_inc(s["w"], 16)

            @block.vector
            def _(dve):
                ch = Chain(dve, s["dvc"])
                dve.wait_ge(s["w"], 48)
                flat = raw[:, :].rearrange("p w n k -> p (w n) k")
                a2, s2, i2 = (x[:, :].rearrange("p w n -> p (w n)") for x in (amax, sc, inv))
                ch.link(nc.vector.tensor_reduce(a2, flat, AX.X, ALU.max, apply_absolute_value=True))
                ch.link(nc.vector.tensor_scalar(s2, a2, 1.0 / 7.0, 1e-12, ALU.mult, ALU.max))
                ch.link(nc.vector.reciprocal(i2, s2))
                ch.link(nc.vector.tensor_tensor(flat, flat, i2.unsqueeze(2).broadcast_to([P, 3 * NBK, 32]), ALU.mult))
                ch.link(nc.vector.tensor_scalar(flat, flat, MAGIC, None, ALU.add))
                ch.link(nc.vector.tensor_scalar(flat, flat, MAGIC, None, ALU.subtract))
                ch.link(nc.vector.tensor_tensor(flat, flat, s2.unsqueeze(2).broadcast_to([P, 3 * NBK, 32]), ALU.mult))
                dve.sem_inc(s["ready"], 1)

            def turns():
                for i, dst in ((0, gT), (1, uT)):
                    v = raw[:, i].rearrange("p (o n) k -> p o (n k)", n=8)
                    for o in range(6):
                        for k in range(2):
                            yield v[:, o, k * P:(k + 1) * P], dst[:, k, o * P:(o + 1) * P]
                v = raw[:, 2].rearrange("p (o n) k -> p o (n k)", n=24)
                for o in range(2):
                    for k in range(6):
                        yield v[:, o, k * P:(k + 1) * P], dT[:, k, o * P:(o + 1) * P]

            @block.tensor
            def _(pe):
                pe.wait_ge(s["ready"], 1)
                for n, (src, dst) in enumerate(turns()):
                    if n >= 2:
                        pe.wait_ge(s["copied"], n - 1)
                    nc.tensor.transpose(wps[:, n % 2, 0:P], src, G.ident[:, :]).then_inc(s["turned"], 1)

            @block.scalar
            def _(act):
                for n, (src, dst) in enumerate(turns()):
                    act.wait_ge(s["turned"], n + 1)
                    nc.scalar.copy(dst, wps[:, n % 2, 0:P]).then_inc(s["copied"], 1)


def quantised_ffn(nc, G, a):
    FT = 6
    TOKS = NB * S
    with ExitStack() as ctx:
        def sb(name, shape, dt=F32):
            return ctx.enter_context(nc.sbuf_tensor(name, shape, dt))

        G.quant = sb("quant", [P, 5, 2])
        gT = sb("gateT", [P, KT, FT * P])
        uT = sb("upT", [P, KT, FT * P])
        dT = sb("downT", [P, FT, D])
        mx = sb("mx", [P, 4, NB * FT])
        xT = sb("gridT", [P, KT, TOKS])
        act_ = sb("hidden", [P, FT, TOKS])
        Y = act_[:, 0:2, :].rearrange("p a (t d) -> p (a t) d", d=D)
        dequantise(nc, G, "f1w", a["L0_ffn_w_gate"], a["L0_ffn_w_up"], a["L0_ffn_w_down"], gT, uT, dT)
        normalise(nc, G, "f1n", G.X, Y, absmax=mx[:, 0, 0:TT])
        grid(nc, G, "f1g", [mx[:, 0, 0:TT]], [0])
        turn(nc, G, "f1t", Y, xT, quant=0)

        with phase(nc, "f1a", "g u g_cp u_mx") as (s, psb, ps):
            gps = ps("gps", [P, 4, S])
            ups = ps("ups", [P, 4, S])
            with nc.Block() as block:

                @block.tensor
                def _(pe):
                    with pe.Fori(0, NB) as b:
                        for m in range(FT):
                            n = b * FT + m
                            pe.wait_ge(s["g_cp"], n + 1)
                            for k in range(KT):
                                last = nc.tensor.matmul(gps[:, m % 2, :], gT[:, k, m * P:(m + 1) * P], xT[:, k, ds(b * S, S)], start=k == 0, stop=k == 1)
                            last.then_inc(s["g"], 1)
                            pe.wait_ge(s["u_mx"], n + 1)
                            for k in range(KT):
                                last = nc.tensor.matmul(ups[:, m % 2, :], uT[:, k, m * P:(m + 1) * P], xT[:, k, ds(b * S, S)], start=k == 0, stop=k == 1)
                            last.then_inc(s["u"], 1)

                @block.scalar
                def _(act):
                    act.sem_inc(s["g_cp"], 2)
                    with act.Fori(0, NB) as b:
                        for m in range(FT):
                            act.wait_ge(s["g"], b * FT + m + 1)
                            nc.scalar.copy(act_[:, m, ds(b * S, S)], gps[:, m % 2, :]).then_inc(s["g_cp"], 1)

                @block.vector
                def _(dve):
                    dve.sem_inc(s["u_mx"], 2)
                    with dve.Fori(0, NB) as b:
                        for m in range(FT):
                            dve.wait_ge(s["u"], b * FT + m + 1)
                            nc.vector.tensor_reduce(mx[:, 1, ds(b * FT + m, 1)], ups[:, m % 2, :], AX.X, ALU.max, apply_absolute_value=True).then_inc(s["u_mx"], 1)
                        dve.wait_ge(s["g_cp"], b * FT + FT + 2)
                        alone(dve)
                        nc.vector.tensor_reduce(mx[:, 2, ds(b, 1)], act_[:, :, ds(b * S, S)], AX.XY, ALU.max, apply_absolute_value=True)

        grid(nc, G, "f1h", [mx[:, 1, :], mx[:, 2, 0:NB]], [1, 2])

        with phase(nc, "f1b", "r sig r2 sig_free dvc poolc") as (s, psb, ps):
            sg = psb("sg", [P, 2, FT, S // 2])
            with nc.Block() as block:
                W2 = S // 2
                N2 = NB * 2

                @block.vector
                def _(dve):
                    ch = Chain(dve, s["dvc"])

                    def first(i, c):
                        x = act_[:, :, ds(i * (2 * W2) + c * W2, W2)]
                        ch.link(nc.vector.tensor_scalar(x, x, G.quant[:, 2, 1:2], MAGIC, ALU.mult, ALU.add))
                        nc.vector.tensor_scalar(x, x, MAGIC, G.quant[:, 2, 0:1], ALU.subtract, ALU.mult).then_inc(s["r"], 1)

                    def second(i, c):
                        x = act_[:, :, ds(i * (2 * W2) + c * W2, W2)]
                        y = sg[:, c, :, :]
                        dve.wait_ge(s["sig"], i * 2 + c + 1)
                        ch.link(nc.vector.tensor_scalar(y, y, 65536.0, MAGIC, ALU.mult, ALU.add))
                        ch.link(nc.vector.tensor_scalar(y, y, MAGIC, 65535.0, ALU.subtract, ALU.min))
                        ch.link(nc.vector.tensor_scalar(y, y, 1.0 / 65536.0, None, ALU.mult))
                        ch.link(nc.vector.tensor_tensor(x, y, x, ALU.mult))
                        ch.link(nc.vector.tensor_reduce(mx[:, 3, ds(i * 2 + c, 1)], x, AX.XY, ALU.max, apply_absolute_value=True))
                        dve.sem_inc(s["sig_free"], 1)

                    dve.sem_inc(s["sig_free"], 2)
                    with dve.Fori(0, NB) as i:
                        ch.at(i * 12)
                        first(i, 0)
                        first(i, 1)
                        second(i, 0)
                        second(i, 1)
                        ch.done(12)

                @block.scalar
                def _(act):
                    with act.Fori(0, NB) as i:
                        for c in range(2):
                            act.wait_ge(s["r"], i * 2 + c + 1)
                            act.wait_ge(s["sig_free"], i * 2 + c + 1)
                            nc.scalar.activation(sg[:, c, :, :], act_[:, :, ds(i * (2 * W2) + c * W2, W2)], ACT.Sigmoid).then_inc(s["sig"], 1)

        grid(nc, G, "f1i", [mx[:, 3, 0:2 * NB]], [3])

        with phase(nc, "f1c", "u u_cp up up_free dvc actc") as (s, psb, ps):
            up = psb("up", [P, FT, S])
            magic = psb("magic", [P, 1])
            ups = ps("ups", [P, 4, S])
            with nc.Block() as block:

                @block.tensor
                def _(pe):
                    with pe.Fori(0, NB) as b:
                        for m in range(FT):
                            pe.wait_ge(s["u_cp"], b * FT + m + 1)
                            for k in range(KT):
                                last = nc.tensor.matmul(ups[:, m % 2, :], uT[:, k, m * P:(m + 1) * P], xT[:, k, ds(b * S, S)], start=k == 0, stop=k == 1)
                            last.then_inc(s["u"], 1)

                @block.scalar
                def _(act):
                    act.sem_inc(s["u_cp"], 2)
                    act.wait_ge(s["actc"], 1)
                    with act.Fori(0, NB) as b:
                        act.wait_ge(s["up_free"], b + 1)
                        for m in range(FT):
                            act.wait_ge(s["u"], b * FT + m + 1)
                            nc.scalar.activation(up[:, m, :], ups[:, m % 2, :], ACT.Identity, scale=G.quant[:, 1, 1:2], bias=magic[:, 0:1]).then_inc(s["u_cp"], 1)

                @block.vector
                def _(dve):
                    ch = Chain(dve, s["dvc"])
                    nc.vector.memset(magic[:, :], MAGIC).then_inc(s["actc"], 1)
                    dve.sem_inc(s["up_free"], 1)
                    with dve.Fori(0, NB) as b:
                        ch.at(b * 5)
                        x = act_[:, :, ds(b * S, S)]
                        ch.link(nc.vector.tensor_scalar(x, x, G.quant[:, 3, 1:2], MAGIC, ALU.mult, ALU.add))
                        ch.link(nc.vector.tensor_scalar(x, x, MAGIC, G.quant[:, 3, 0:1], ALU.subtract, ALU.mult))
                        dve.wait_ge(s["u_cp"], b * FT + FT + 2)
                        ch.link(nc.vector.tensor_scalar(up[:, :, :], up[:, :, :], MAGIC, G.quant[:, 1, 0:1], ALU.subtract, ALU.mult))
                        ch.link(nc.vector.tensor_tensor(x, x, up[:, :, :], ALU.mult))
                        dve.sem_inc(s["up_free"], 1)
                        ch.link(nc.vector.tensor_reduce(mx[:, 0, ds(b, 1)], x, AX.XY, ALU.max, apply_absolute_value=True))
                        ch.done(5)

        grid(nc, G, "f1j", [mx[:, 0, 0:NB]], [4])

        with phase(nc, "f1d", "h h_free y y_free dvc") as (s, psb, ps):
            h = psb("h", [P, 2, FT, S // 2])
            yps = ps("yps", [P, 4, S])
            with nc.Block() as block:
                @block.vector
                def _(dve):
                    ch = Chain(dve, s["dvc"])
                    dve.sem_inc(s["y_free"], 2)
                    g = G.gate[:, 4:5]

                    def grid_rows(i, c):
                        x = act_[:, :, ds(i * S + c * (S // 2), S // 2)]
                        dve.wait_ge(s["h_free"], i * 2 + c + 1)
                        ch.link(nc.vector.tensor_scalar(h[:, c], x, G.quant[:, 4, 1:2], MAGIC, ALU.mult, ALU.add))
                        nc.vector.tensor_scalar(h[:, c], h[:, c], MAGIC, G.quant[:, 4, 0:1], ALU.subtract, ALU.mult).then_inc(s["h"], 1)

                    def add(i, c):
                        dve.wait_ge(s["y"], i * 2 + c + 1)
                        x = G.X[:, ds(i * NT + c * 2, 2), :].rearrange("p t d -> p (t d)")
                        ch.link(nc.vector.scalar_tensor_tensor(x, yps[:, c, :], g, x, ALU.mult, ALU.add))
                        dve.sem_inc(s["y_free"], 1)

                    with dve.Fori(0, NB) as i:
                        ch.at(i * 4)
                        grid_rows(i, 0)
                        grid_rows(i, 1)
                        add(i, 0)
                        add(i, 1)
                        ch.done(4)

                @block.tensor
                def _(pe):
                    pe.sem_inc(s["h_free"], 2)
                    with pe.Fori(0, NB) as i:
                        for c in range(2):
                            pe.wait_ge(s["h"], i * 2 + c + 1)
                            pe.wait_ge(s["y_free"], i * 2 + c + 1)
                            for t in range(2):
                                for k in range(FT):
                                    last = nc.tensor.matmul(yps[:, c, t * D:(t + 1) * D], h[:, c, k, t * P:(t + 1) * P], dT[:, k, :], start=k == 0, stop=k == FT - 1)
                            last.then_inc(s["y"], 1)
                            pe.wait_ge(s["y"], i * 2 + c + 1)
                            pe.sem_inc(s["h_free"], 1)


def route(nc, G, name, xT, rw, bias, combT):
    E, GR, EPG, TOPG, TOPK = 16, 4, 4, 2, 4
    QT = TT // 4
    with phase(nc, name, "w lg lg_cp lt sc comb ct ct_cp dvc") as (s, sb, ps):
        RW = sb("RW", [P, KT, E])
        cb = sb("cb", [P, E])
        before = sb("before", [P, E, E])
        lg = sb("lg", [E, 2, S])
        score = sb("score", [P, TT, E])
        biased = sb("biased", [P, TT, E])
        comb = sb("comb", [P, TT, E])
        hi = sb("hi", [P, TT, GR, 2])
        lo = sb("lo", [P, TT, GR, 2])
        gs = sb("gs", [P, TT, GR])
        g2 = sb("g2", [P, TT, GR])
        gt = sb("gt", [P, QT, E, E])
        eq = sb("eq", [P, QT, E, E])
        tot = sb("tot", [P, TT])
        lps = ps("lps", [P, 2, S])
        tps = ps("tps", [P, 2, S])
        cps = ps("cps", [P, 2, S])
        with nc.Block() as block:

            @block.sync
            def _(sp):
                sp.dma_start(RW[:, :, :], rw).then_inc(s["w"], 16)
                sp.dma_start(cb[:, :], bias.unsqueeze(0).broadcast_to([P, E])).then_inc(s["w"], 16)
                sp.dma_start(before[:, :, :].rearrange("p a b -> p (a b)"), G.before.unsqueeze(0).broadcast_to([P, E * E])).then_inc(s["w"], 16)

            @block.tensor
            def _(pe):
                pe.wait_ge(s["w"], 48)
                with pe.Fori(0, NB // 2) as it:
                    for p in range(2):
                        b = it * 2 + p
                        pe.wait_ge(s["lg_cp"], b + 1)
                        for k in range(KT):
                            last = nc.tensor.matmul(lps[0:E, p, :], RW[:, k, :], xT[:, k, ds(b * S, S)], start=k == 0, stop=k == KT - 1)
                        last.then_inc(s["lg"], 1)
                        pe.wait_ge(s["lg_cp"], b + 3)
                        pe.wait_ge(s["sc"], b + 1)
                        alone(pe)
                        for t in range(NT):
                            last = nc.tensor.transpose(tps[:, p, t * E:(t + 1) * E], lg[:, p, t * P:(t + 1) * P], G.ident[0:E, 0:E])
                        last.then_inc(s["lt"], 1)
                pe.wait_ge(s["comb"], 1)
                for b in range(NB):
                    if b >= 2:
                        pe.wait_ge(s["ct_cp"], b - 1)
                    for t in range(NT):
                        last = nc.tensor.transpose(cps[0:E, b % 2, t * P:(t + 1) * P], comb[:, b * NT + t, :], G.ident[:, :])
                    last.then_inc(s["ct"], 1)

            @block.scalar
            def _(act):
                act.sem_inc(s["lg_cp"], 2)
                act.sem_inc(s["sc"], 2)
                with act.Fori(0, NB // 2) as it:
                    for p in range(2):
                        b = it * 2 + p
                        act.wait_ge(s["lg"], b + 1)
                        nc.scalar.copy(lg[:, p, :], lps[0:E, p, :]).then_inc(s["lg_cp"], 1)
                        act.wait_ge(s["lt"], b + 1)
                        nc.scalar.activation(score[:, ds(b * NT, NT), :], tps[:, p, 0:NT * E].rearrange("p (t e) -> p t e", e=E), ACT.Sigmoid).then_inc(s["sc"], 1)
                for b in range(NB):
                    act.wait_ge(s["ct"], b + 1)
                    nc.scalar.copy(combT[:, b * S:(b + 1) * S], cps[0:E, b % 2, :]).then_inc(s["ct_cp"], 1)

            @block.vector
            def _(dve):
                ch = Chain(dve, s["dvc"])
                V = nc.vector
                dve.wait_ge(s["w"], 48)
                dve.wait_ge(s["sc"], NB + 2)
                ch.link(V.tensor_tensor(biased[:, :, :], score[:, :, :], cb[:, :].unsqueeze(1).broadcast_to([P, TT, E]), ALU.add))
                bg = biased[:, :, :].rearrange("p t (g i) -> p (t g) i", i=EPG)
                h, l = (x[:, :, :, :].rearrange("p t g i -> p (t g) i") for x in (hi, lo))
                g, r = (x[:, :, :].rearrange("p t g -> p (t g)").unsqueeze(2) for x in (gs, g2))
                V.tensor_tensor(h, bg[:, :, 0:2], bg[:, :, 2:4], ALU.max)
                ch.link(V.tensor_tensor(l, bg[:, :, 0:2], bg[:, :, 2:4], ALU.min))
                ch.link(V.tensor_tensor(g, h[:, :, 0:1], h[:, :, 1:2], ALU.max))
                ch.link(V.tensor_tensor(r, h[:, :, 0:1], h[:, :, 1:2], ALU.min))
                ch.link(V.tensor_tensor(h[:, :, 0:1], l[:, :, 0:1], l[:, :, 1:2], ALU.max))
                ch.link(V.tensor_tensor(r, r, h[:, :, 0:1], ALU.max))
                ch.link(V.tensor_tensor(gs[:, :, :], gs[:, :, :], g2[:, :, :], ALU.add))

                def rank(x, n, out, limit):
                    T = x.shape[1]
                    gv, ev = (y[:, :, :, :].rearrange("p t a b -> p (t a b)")[:, 0:T * n * n].rearrange("p (t a b) -> p t a b", a=n, b=n) for y in (gt, eq))
                    one, other = x.unsqueeze(3).broadcast_to([P, T, n, n]), x.unsqueeze(2).broadcast_to([P, T, n, n])
                    V.tensor_tensor(gv, other, one, ALU.is_gt)
                    ch.link(V.tensor_tensor(ev, other, one, ALU.is_equal))
                    ch.link(V.tensor_tensor(ev, ev, before[:, 0:n, 0:n].unsqueeze(1).broadcast_to([P, T, n, n]), ALU.mult))
                    ch.link(V.tensor_tensor(gv, gv, ev, ALU.add))
                    ch.link(V.tensor_reduce(out, gv, AX.X, ALU.add))
                    ch.link(V.tensor_scalar(out, out, float(limit) - 0.5, None, ALU.is_lt))

                rank(gs[:, :, :], GR, g2[:, :, :], TOPG)
                each = g2[:, :, :].rearrange("p t g -> p (t g)").unsqueeze(2).broadcast_to([P, TT * GR, EPG])
                ch.link(V.tensor_tensor(bg, bg, each, ALU.mult))
                ch.link(V.tensor_scalar(g2[:, :, :], g2[:, :, :], 1.0, BIG, ALU.subtract, ALU.mult))
                ch.link(V.tensor_tensor(bg, bg, each, ALU.add))
                for q in range(4):
                    rank(biased[:, q * QT:(q + 1) * QT, :], E, comb[:, q * QT:(q + 1) * QT, :], TOPK)
                ch.link(V.tensor_tensor(comb[:, :, :], comb[:, :, :], score[:, :, :], ALU.mult))
                ch.link(V.tensor_reduce(tot[:, :], comb[:, :, :], AX.X, ALU.add))
                ch.link(V.tensor_scalar(tot[:, :], tot[:, :], 1e-20, None, ALU.add))
                ch.link(V.reciprocal(tot[:, :], tot[:, :]))
                V.tensor_tensor(comb[:, :, :], comb[:, :, :], tot[:, :].unsqueeze(2).broadcast_to([P, TT, E]), ALU.mult).then_inc(s["comb"], 1)


def gated_mlp(nc, G, name, front, wg, wu, wd, NF, func, onto, gate, bg=None, bu=None, bd=None, combT=None, routed=0):
    shift = isinstance(front, tuple)
    nw = len(wg) + len(wu) + len(wd) + (4 if bg is not None else 0) + (1 if shift else 0) + (1 if combT is not None else 0)
    with phase(nc, name, "w in0 in1 in_free xn xn_free stats rstd xt_ps xt_ps_free xt xt_free g g_free u u_free c c_free gl gl_free "
               "h h_free y y_free zero dvc poolc") as (s, sb, ps):
        WG = sb("WG", [P, KT, NF * P])
        WU = sb("WU", [P, KT, NF * P])
        WD = sb("WD", [P, NF, D])
        gl = sb("gl", [P, 2, S])
        h = sb("h", [P, NF, S])
        if bg is not None:
            BG = sb("BG", [P, NF])
            BU = sb("BU", [P, NF])
            BD = sb("BD", [1, D])
        if combT is not None:
            sel = sb("sel", [16, 8, P])
        if shift:
            rows = sb("rows", [P, 2, NT, D])
            xn = sb("xn", [P, 2, NT, D])
            xT = sb("xT", [P, KT, S])
            aff = sb("aff", [P, 2, KT])
            st = sb("st", [P, NT, 6])
            mv = sb("mv", [P, NT, 2])
            rstd = sb("rstd", [P, NT])
            xps = ps("xps", [P, KT, S])
        gps = ps("gps", [P, 2, S])
        ups = ps("ups", [P, 2, S])
        if combT is not None:
            cps = ps("cps", [P, 2, S])
        yps = ps("yps", [P, 2, S])
        RK = NF
        g = 1.0 if gate is None else G.gate[:, gate:gate + 1]

        with nc.Block() as block:

            @block.sync
            def _(sp):
                for view, c in wg:
                    sp.dma_start(WG[:, :, c:c + view.shape[2]], view).then_inc(s["w"], 16)
                for view, c in wu:
                    sp.dma_start(WU[:, :, c:c + view.shape[2]], view).then_inc(s["w"], 16)
                for view, c in wd:
                    sp.dma_start(WD[:, c:c + view.shape[1], :], view).then_inc(s["w"], 16)
                if bg is not None:
                    sp.dma_start(BG[:, :], bg).then_inc(s["w"], 16)
                    sp.dma_start(BU[:, :], bu).then_inc(s["w"], 16)
                    sp.dma_start(BD[:, :], bd).then_inc(s["w"], 16)
                    sp.dma_start(aff[:, 0, :], front[2]).then_inc(s["w"], 16)
                if shift:
                    sp.dma_start(aff[:, 1, :], front[3]).then_inc(s["w"], 16)
                if combT is not None:
                    sp.dma_start(sel[:, :, :], G.spread).then_inc(s["w"], 16)
                if shift:
                    sp.wait_ge(s["zero"], 1)
                    with sp.Fori(0, NB // 2) as it:
                        for p in range(2):
                            b = it * 2 + p
                            sp.wait_ge(s["in_free"], b + 1)
                            alone(sp)
                            shifted_rows(sp, front[1], rows[:, p], b, s[f"in{p}"])

            @block.gpsimd
            def _(pool):
                ch = Chain(pool, s["poolc"])
                if shift:
                    for p in range(2):
                        last = nc.gpsimd.memset(rows[0:1, p, 0, D // 2:D], 0.0)
                    last.then_inc(s["zero"], 1)
                    with pool.Fori(0, NB) as b:
                        ch.at(b)
                        pool.wait_ge(s["stats"], b + 1)
                        alone(pool)
                        ch.link(nc.gpsimd.tensor_scalar(rstd[:, :], mv[:, :, 1], LN_EPS, None, ALU.add))
                        nc.gpsimd.tensor_tensor(rstd[:, :], rstd[:, :], G.mhalf[:, 0:NT], ALU.pow).then_inc(s["rstd"], 1)

            @block.tensor
            def _(pe):
                if shift:
                    pe.sem_inc(s["xn_free"], 2)
                    pe.sem_inc(s["xt_free"], 1)
                pe.sem_inc(s["h_free"], 1)
                pe.wait_ge(s["w"], 16 * nw)

                def hidden(b, x):
                    for m in range(NF):
                        n = b * NF + m
                        for w, o, done, free in ((WG, gps, "g", "g_free"), (WU, ups, "u", "u_free")):
                            pe.wait_ge(s[free], n + 1)
                            for k in range(KT):
                                last = nc.tensor.matmul(o[:, m % 2, :], w[:, k, m * P:(m + 1) * P], x(k), start=k == 0, stop=k == KT - 1)
                            last.then_inc(s[done], 1)
                        if combT is not None and m < routed:
                            pe.wait_ge(s["c_free"], b * routed + m + 1)
                            alone(pe)
                            nc.tensor.matmul(cps[:, m % 2, :], sel[:, m, :], combT[:, ds(b * S, S)], start=True, stop=True).then_inc(s["c"], 1)

                def down(b):
                    pe.wait_ge(s["h"], b + 1)
                    for v in range(2):
                        pe.wait_ge(s["y_free"], b * 2 + v + 1)
                        for t in (2 * v, 2 * v + 1):
                            o = yps[:, v, (t % 2) * D:(t % 2 + 1) * D]
                            for k in range(NF):
                                last = nc.tensor.matmul(o, h[:, k, t * P:(t + 1) * P], WD[:, k, :], start=k == 0, stop=k == NF - 1 and bd is None)
                            if bd is not None:
                                last = nc.tensor.matmul(o, G.ones[0:1, :], BD[0:1, :], start=False, stop=True)
                        last.then_inc(s["y"], 1)
                    pe.wait_ge(s["y"], b * 2 + 2)
                    pe.sem_inc(s["h_free"], 1)

                if shift:
                    with pe.Fori(0, NB // 2) as it:
                        for p in range(2):
                            b = it * 2 + p
                            pe.wait_ge(s["xn"], b + 1)
                            pe.wait_ge(s["xt_ps_free"], b + 1)
                            for k in range(KT):
                                for t in range(NT):
                                    last = nc.tensor.transpose(xps[:, k, t * P:(t + 1) * P], xn[:, p, t, k * P:(k + 1) * P], G.ident[:, :])
                            last.then_inc(s["xt_ps"], 1)
                            pe.wait_ge(s["xt_ps"], b + 1)
                            pe.sem_inc(s["xn_free"], 1)
                            pe.wait_ge(s["xt"], b + 1)
                            hidden(b, lambda k: xT[:, k, :])
                            pe.wait_ge(s["u"], b * NF + NF)
                            pe.sem_inc(s["xt_free"], 1)
                            down(b)
                else:
                    with pe.Fori(0, NB) as b:
                        hidden(b, lambda k: front[:, k, ds(b * S, S)])
                        down(b)

            @block.scalar
            def _(act):
                if shift:
                    act.sem_inc(s["xt_ps_free"], 1)
                act.sem_inc(s["g_free"], 2)
                act.wait_ge(s["w"], 16 * nw)
                with act.Fori(0, NB) as b:
                    if shift:
                        act.wait_ge(s["xt_ps"], b + 1)
                        act.wait_ge(s["xt_free"], b + 1)
                        for k in range(KT):
                            last = nc.scalar.activation(xT[:, k, :], xps[:, k, :], ACT.Identity, scale=aff[:, 0, k:k + 1], bias=aff[:, 1, k:k + 1])
                        last.then_inc(s["xt"], 1)
                        act.wait_ge(s["xt"], b + 1)
                        act.sem_inc(s["xt_ps_free"], 1)
                    for m in range(NF):
                        n = b * NF + m
                        act.wait_ge(s["g"], n + 1)
                        act.wait_ge(s["gl_free"], n + 1)
                        nc.scalar.activation(gl[:, m % 2, :], gps[:, m % 2, :], func, bias=BG[:, m:m + 1] if bg is not None else 0.0).then_inc(s["gl"], 1)
                        act.wait_ge(s["gl"], n + 1)
                        act.sem_inc(s["g_free"], 1)

            @block.vector
            def _(dve):
                ch = Chain(dve, s["dvc"])
                dve.sem_inc(s["gl_free"], 2)
                if shift:
                    dve.sem_inc(s["in_free"], 2)
                dve.sem_inc(s["u_free"], 2)
                dve.sem_inc(s["y_free"], 2)
                if combT is not None:
                    dve.sem_inc(s["c_free"], 2)
                dve.wait_ge(s["w"], 16 * nw)
                KCH = NF + (routed if combT is not None else 0) + 2 + (2 if shift else 0)

                def body(b, p=None, it=None):
                    ch.at(b * KCH)
                    if shift:
                        dve.wait_ge(s[f"in{p}"], it * 64 + 64)
                        for t in range(NT):
                            last = nc.vector.bn_stats(st[:, t, :], rows[:, p, t, :])
                        ch.link(last)
                        alone(dve)
                        for t in range(NT):
                            last = nc.vector.bn_aggr(mv[:, t, :], st[:, t, :])
                        last.then_inc(s["stats"], 1)
                        dve.wait_ge(s["rstd"], b + 1)
                        dve.wait_ge(s["xn_free"], b + 1)
                        for t in range(NT):
                            last = nc.vector.tensor_scalar(xn[:, p, t, :], rows[:, p, t, :], mv[:, t, 0:1], rstd[:, t:t + 1], ALU.subtract, ALU.mult)
                        ch.link(last)
                        dve.sem_inc(s["xn"], 1)
                        dve.sem_inc(s["in_free"], 1)
                    dve.wait_ge(s["h_free"], b + 1)
                    for m in range(NF):
                        n = b * NF + m
                        dve.wait_ge(s["gl"], n + 1)
                        dve.wait_ge(s["u"], n + 1)
                        if bu is not None:
                            ins = nc.vector.scalar_tensor_tensor(h[:, m, :], ups[:, m % 2, :], BU[:, m:m + 1], gl[:, m % 2, :], ALU.add, ALU.mult)
                        else:
                            ins = nc.vector.tensor_tensor(h[:, m, :], ups[:, m % 2, :], gl[:, m % 2, :], ALU.mult)
                        ch.link(ins)
                        dve.sem_inc(s["gl_free"], 1)
                        dve.sem_inc(s["u_free"], 1)
                        if combT is not None and m < routed:
                            dve.wait_ge(s["c"], b * routed + m + 1)
                            ch.link(nc.vector.tensor_tensor(h[:, m, :], cps[:, m % 2, :], h[:, m, :], ALU.mult))
                            dve.sem_inc(s["c_free"], 1)
                    dve.sem_inc(s["h"], 1)
                    for v in range(2):
                        dve.wait_ge(s["y"], b * 2 + v + 1)
                        x = onto[:, ds(b * NT + 2 * v, 2), :].rearrange("p t d -> p (t d)")
                        ch.link(nc.vector.scalar_tensor_tensor(x, yps[:, v, :], g, x, ALU.mult, ALU.add))
                        dve.sem_inc(s["y_free"], 1)
                    ch.done(KCH)

                if shift:
                    with dve.Fori(0, NB // 2) as it:
                        for p in range(2):
                            body(it * 2 + p, p, it)
                else:
                    with dve.Fori(0, NB) as b:
                        body(b)


def shifted_rows(eng, src, rows, b, sem):
    H = D // 2
    eng.dma_start(rows[:, :, 0:H], src[:, ds(b * NT, NT), 0:H]).then_inc(sem, 16)
    eng.dma_start(rows[1:P, :, H:D], src[0:P - 1, ds(b * NT, NT), H:D]).then_inc(sem, 16)
    eng.dma_start(rows[0:1, 1:NT // 2 + 1, H:D], src[P - 1:P, ds(b * NT, NT // 2), H:D]).then_inc(sem, 16)
    eng.dma_start(rows[0:1, NT // 2 + 1:NT, H:D], src[P - 1:P, ds(b * NT + NT // 2, NT // 2 - 1), H:D]).then_inc(sem, 16)


def rotary_qkv(nc, G, name, src, wqkv, q_scale, k_scale, qs, ks, vs):
    H, DH = 8, 64
    HD = H * DH
    HW = DH // 2
    with phase(nc, name, "w zero in0 in1 rows_free xt_ps xt_ps_free xt xt_free qk qk_free v v_free v_sb v_st0 v_st1 sq ss rn "
               "qn qn_free side rot rot_free tp tp_free p1 r1 p2 pp p_st0 p_st1 dvc poolc tab") as (s, sb, ps):
        W = sb("W", [P, KT, 3 * HD])
        rows = sb("rows", [P, 2, NT, D])
        xT = sb("xT", [P, KT, S])
        tab = sb("tab", [P, 4, NT, DH])
        sc = sb("sc", [P, 2, 2, DH])
        sq = sb("sq", [P, HD])
        ss = sb("ss", [P, 2, H])
        rn = sb("rn", [P, 2, H])
        qn = sb("qn", [P, 2, HD])
        straight = sb("straight", [P, HD])
        crossed = sb("crossed", [P, HD])
        rot = sb("rot", [P, 2, HD])
        parts = sb("parts", [P, 2, 3, NT, S], BF16)
        r1 = sb("r1", [P, S])
        vsb = sb("vsb", [P, 2, HD])
        xps = ps("xps", [P, KT, S])
        qps = ps("qps", [P, 2, S])
        vps = ps("vps", [P, 2, S])
        tps = ps("tps", [P, 2, S])
        NU = 2 * NT

        with nc.Block() as block:

            @block.sync
            def _(sp):
                sp.dma_start(W[:, :, :], w_view(wqkv)).then_inc(s["w"], 16)
                sp.dma_start(tab[:, :, :, :], G.rotary.rearrange("w (t p) d -> p w t d", p=P)).then_inc(s["w"], 16)
                for i, x in enumerate((q_scale, k_scale)):
                    x = x.unsqueeze(0)
                    sp.dma_start(sc[:, i, 0, :], x.broadcast_to([P, DH])).then_inc(s["w"], 16)
                    sp.dma_start(sc[:, i, 1, 0:HW], x[:, HW:DH].broadcast_to([P, HW])).then_inc(s["w"], 16)
                    sp.dma_start(sc[:, i, 1, HW:DH], x[:, 0:HW].broadcast_to([P, HW])).then_inc(s["w"], 16)
                sp.wait_ge(s["zero"], 1)
                for c in ("v_st0", "v_st1", "p_st0", "p_st1"):
                    sp.sem_inc(s[c], 16)
                with sp.Fori(0, NB // 2) as it:
                    for p in range(2):
                        b = it * 2 + p
                        sp.wait_ge(s["rows_free"], b + 1)
                        alone(sp)
                        shifted_rows(sp, src, rows[:, p], b, s[f"in{p}"])
                        for t in range(NT):
                            sp.wait_ge(s["v_sb"], b * NT + t + 1)
                            alone(sp)
                            sp.dma_start(vs[ds(b * S + t * P, P), :], vsb[:, t % 2, :]).then_inc(s[f"v_st{t % 2}"], 16)
                        sp.wait_ge(s["pp"], (b + 1) * NU)
                        alone(sp)
                        for i, dst in enumerate((qs, ks)):
                            for j in range(3):
                                sp.dma_start(dst[j].rearrange("(f p) t -> p f t", p=P)[:, :, ds(b * S, S)], parts[:, i, j]).then_inc(s["p_st0"], 16)
                for p in range(2):
                    sp.wait_ge(s[f"v_st{p}"], 16 + 16 * NB * NT // 2)
                sp.wait_ge(s["p_st0"], 16 + 16 * NB * 6)

            @block.tensor
            def _(pe):
                pe.sem_inc(s["rows_free"], 2)
                pe.sem_inc(s["xt_free"], 1)
                pe.sem_inc(s["rot_free"], 2)
                pe.wait_ge(s["w"], 16 * 8)

                def turn_unit(n, u):
                    pe.wait_ge(s["rot"], n + 2)
                    pe.wait_ge(s["tp_free"], n + 1)
                    for f in range(NT):
                        last = nc.tensor.transpose(tps[:, u % 2, f * P:(f + 1) * P], rot[:, u % 2, f * P:(f + 1) * P], G.ident[:, :])
                    last.then_inc(s["tp"], 1)
                    pe.wait_ge(s["tp"], n + 1)
                    pe.sem_inc(s["rot_free"], 1)

                with pe.Fori(0, NB // 2) as it:
                    for p in range(2):
                        b = it * 2 + p
                        pe.wait_ge(s[f"in{p}"], it * 64 + 64)
                        pe.wait_ge(s["xt_ps_free"], b + 1)
                        for k in range(KT):
                            for t in range(NT):
                                last = nc.tensor.transpose(xps[:, k, t * P:(t + 1) * P], rows[:, p, t, k * P:(k + 1) * P], G.ident[:, :])
                        last.then_inc(s["xt_ps"], 1)
                        pe.wait_ge(s["xt_ps"], b + 1)
                        pe.sem_inc(s["rows_free"], 1)
                        pe.wait_ge(s["xt"], b + 1)
                        for t in range(NT):
                            for i in range(2):
                                u = 2 * t + i
                                pe.wait_ge(s["qk_free"], b * NU + u + 1)
                                for k in range(KT):
                                    last = nc.tensor.matmul(qps[:, i, :], xT[:, k, t * P:(t + 1) * P], W[:, k, i * HD:(i + 1) * HD], start=k == 0, stop=k == KT - 1)
                                last.then_inc(s["qk"], 1)
                            pe.wait_ge(s["v_free"], b * NT + t + 1)
                            for k in range(KT):
                                last = nc.tensor.matmul(vps[:, t % 2, :], xT[:, k, t * P:(t + 1) * P], W[:, k, 2 * HD:3 * HD], start=k == 0, stop=k == KT - 1)
                            last.then_inc(s["v"], 1)
                            if t >= 1:
                                for i in range(2):
                                    turn_unit(b * NU + 2 * t - 2 + i, i)
                        pe.wait_ge(s["v"], b * NT + NT)
                        pe.sem_inc(s["xt_free"], 1)
                        for i in range(2):
                            turn_unit(b * NU + 2 * NT - 2 + i, i)

            @block.scalar
            def _(act):
                act.sem_inc(s["xt_ps_free"], 1)
                act.sem_inc(s["v_free"], 2)
                with act.Fori(0, NB // 2) as it:
                    for p in range(2):
                        b = it * 2 + p
                        act.wait_ge(s["xt_ps"], b + 1)
                        act.wait_ge(s["xt_free"], b + 1)
                        for k in range(KT):
                            last = nc.scalar.copy(xT[:, k, :], xps[:, k, :])
                        last.then_inc(s["xt"], 1)
                        act.wait_ge(s["xt"], b + 1)
                        act.sem_inc(s["xt_ps_free"], 1)

                        def split(n, u, t):
                            i = u % 2
                            act.wait_ge(s["tp"], n + 1)
                            if u < 2:
                                act.wait_ge(s["p_st0"], b * 96 + 16)
                            nc.scalar.copy(parts[:, i, 0, :, t * P:(t + 1) * P], tps[:, i, :].rearrange("p (f t) -> p f t", t=P)).then_inc(s["p1"], 1)
                            act.wait_ge(s["r1"], n + 1)
                            nc.scalar.copy(parts[:, i, 1, :, t * P:(t + 1) * P], r1[:, :].rearrange("p (f t) -> p f t", t=P)).then_inc(s["p2"], 1)

                        for t in range(NT):
                            for i in range(2):
                                n = b * NU + 2 * t + i
                                act.wait_ge(s["qk"], n + 1)
                                act.wait_ge(s["ss"], n + 1)
                                nc.scalar.activation(sq[:, :], qps[:, i, :], ACT.Square).then_inc(s["sq"], 1)
                            act.wait_ge(s["v"], b * NT + t + 1)
                            act.wait_ge(s[f"v_st{t % 2}"], b * 32 + (t // 2) * 16 + 16)
                            nc.scalar.copy(vsb[:, t % 2, :], vps[:, t % 2, :]).then_inc(s["v_sb"], 1)
                            act.wait_ge(s["v_sb"], b * NT + t + 1)
                            act.sem_inc(s["v_free"], 1)
                            if t >= 1:
                                for i in range(2):
                                    split(b * NU + 2 * t - 2 + i, i if t == 1 else 2 + i, t - 1)
                        for i in range(2):
                            split(b * NU + 2 * NT - 2 + i, 2 + i, NT - 1)

            @block.gpsimd
            def _(pool):
                ch = Chain(pool, s["poolc"])
                for p in range(2):
                    last = nc.gpsimd.memset(rows[0:1, p, 0, D // 2:D], 0.0)
                last.then_inc(s["zero"], 1)
                pool.wait_ge(s["tab"], 1)
                with pool.Fori(0, NB) as b:
                    ch.at(b * NU * 2)
                    for u in range(NU):
                        t, i = u // 2, u % 2
                        n = b * NU + u
                        pool.wait_ge(s["ss"], n + 2)
                        alone(pool)
                        ch.link(nc.gpsimd.tensor_scalar(rn[:, i, :], ss[:, i, :], 1e-24, None, ALU.max))
                        nc.gpsimd.tensor_tensor(rn[:, i, :], rn[:, i, :], G.mhalf[:, 0:H], ALU.pow).then_inc(s["rn"], 1)
                        pool.wait_ge(s["qn"], n + 1)
                        pool.wait_ge(s["rot"], n + 1)
                        ch.link(nc.gpsimd.tensor_tensor(straight[:, :].rearrange("p (h d) -> p h d", d=DH), qn[:, i, :].rearrange("p (h d) -> p h d", d=DH),
                                                        tab[:, 2 * i, t, :].unsqueeze(1).broadcast_to([P, H, DH]), ALU.mult))
                        pool.sem_inc(s["side"], 1)
                    ch.done(NU * 2)

            @block.vector
            def _(dve):
                ch = Chain(dve, s["dvc"])
                dve.wait_ge(s["w"], 16 * 8)
                for i in range(2):
                    for j in range(2):
                        x = tab[:, 2 * i + j]
                        last = nc.vector.tensor_tensor(x, x, sc[:, i, j, :].unsqueeze(1).broadcast_to([P, NT, DH]), ALU.mult)
                last.then_inc(s["tab"], 1)
                dve.wait_ge(s["tab"], 1)
                dve.sem_inc(s["qk_free"], 2)
                dve.sem_inc(s["ss"], 1)
                dve.sem_inc(s["tp_free"], 2)
                dve.sem_inc(s["rot"], 1)

                def parts_of(b, n, u):
                    i, t = u % 2, u // 2
                    dve.wait_ge(s["p1"], n + 1)
                    ch.link(nc.vector.tensor_tensor(r1[:, :].rearrange("p (f t) -> p f t", t=P), tps[:, i, :].rearrange("p (f t) -> p f t", t=P),
                                                    parts[:, i, 0, :, t * P:(t + 1) * P], ALU.subtract))
                    dve.sem_inc(s["tp_free"], 1)
                    dve.sem_inc(s["r1"], 1)
                    dve.wait_ge(s["p2"], n + 1)
                    ch.link(nc.vector.tensor_tensor(parts[:, i, 2, :, t * P:(t + 1) * P], r1[:, :].rearrange("p (f t) -> p f t", t=P),
                                                    parts[:, i, 1, :, t * P:(t + 1) * P], ALU.subtract))
                    dve.sem_inc(s["pp"], 1)

                KCH = NU * 6
                with dve.Fori(0, NB) as b:
                    ch.at(b * KCH)
                    for u in range(NU):
                        t, i = u // 2, u % 2
                        n = b * NU + u
                        dve.wait_ge(s["sq"], n + 1)
                        ch.link(nc.vector.tensor_reduce(ss[:, i, :], sq[:, :].rearrange("p (h d) -> p h d", d=DH), AX.X, ALU.add))
                        dve.sem_inc(s["ss"], 1)
                        dve.wait_ge(s["rn"], n + 1)
                        ch.link(nc.vector.tensor_tensor(qn[:, i, :].rearrange("p (h d) -> p h d", d=DH), qps[:, i, :].rearrange("p (h d) -> p h d", d=DH),
                                                        rn[:, i, :].unsqueeze(2).broadcast_to([P, H, DH]), ALU.mult))
                        dve.sem_inc(s["qk_free"], 1)
                        dve.sem_inc(s["qn"], 1)
                        x, y = (z.rearrange("p (h s d) -> p h s d", s=2, d=HW) for z in (qn[:, i, :], crossed[:, :]))
                        for k in range(2):
                            last = nc.vector.tensor_tensor(y[:, :, k, :], x[:, :, 1 - k, :], tab[:, 2 * i + 1, t, k * HW:(k + 1) * HW].unsqueeze(1).broadcast_to([P, H, HW]), ALU.mult)
                        ch.link(last)
                        dve.wait_ge(s["side"], n + 1)
                        dve.wait_ge(s["rot_free"], n + 1)
                        ch.link(nc.vector.tensor_tensor(rot[:, i, :], straight[:, :], crossed[:, :], ALU.add))
                        dve.sem_inc(s["rot"], 1)
                        if i == 1 and t >= 1:
                            for v in (u - 3, u - 2):
                                parts_of(b, b * NU + v, v)
                    for v in (NU - 2, NU - 1):
                        parts_of(b, b * NU + v, v)
                    ch.done(KCH)


def add_stream(nc, G, name, gate):
    with phase(nc, name, "done") as (s, sb, ps):
        with nc.Block() as block:

            @block.vector
            def _(dve):
                for c in range(4):
                    x, y = (v[:, c * 8:(c + 1) * 8, :].rearrange("p t d -> p (t d)") for v in (G.X, G.Y))
                    nc.vector.scalar_tensor_tensor(x, y, G.gate[:, gate:gate + 1], x, ALU.mult, ALU.add)


def cell_gates(nc, G, name, xT, a, Mrow, gT, eT):
    H = 8
    NH = NB * H
    with phase(nc, name, "w c0 c1 c_free gi gi_cp gf_cp lay lin ex ln sc m_st tp tp_cp dvc actc") as (s, sb, ps):
        WI = sb("WI", [P, 6, H])
        WF = sb("WF", [P, 6, H])
        bi = sb("bi", [H, 2])
        cT = sb("cT", [P, 2, KT, S])
        raw = sb("raw", [H, 2, TOK])
        ig = sb("ig", [NH, S])
        fg = sb("fg", [NH, S])
        t1 = sb("t1", [NH, S])
        cs = sb("cs", [NH, S])
        one = sb("one", [NH, S])
        M = sb("M", [NH, S])
        ips = ps("ips", [P, 2, S])
        fps = ps("fps", [P, 2, S])
        tps = ps("tps", [P, 2, S])
        with nc.Block() as block:

            @block.sync
            def _(sp):
                sp.dma_start(WI[:, :, :], w_view(a["L2_xattn_igate_w"])).then_inc(s["w"], 16)
                sp.dma_start(WF[:, :, :], w_view(a["L2_xattn_fgate_w"])).then_inc(s["w"], 16)
                sp.dma_start(bi[:, 0:1], a["L2_xattn_igate_b"]).then_inc(s["w"], 16)
                sp.dma_start(bi[:, 1:2], a["L2_xattn_fgate_b"]).then_inc(s["w"], 16)
                with sp.Fori(0, NB // 2) as it:
                    for p in range(2):
                        b = it * 2 + p
                        sp.wait_ge(s["c_free"], b + 1)
                        alone(sp)
                        sp.dma_start(cT[:, p], a["ctx_T"].rearrange("(k p) t -> p k t", p=P)[:, :, ds(b * S, S)]).then_inc(s[f"c{p}"], 16)
                sp.wait_ge(s["gi_cp"], NB + 2)
                sp.wait_ge(s["gf_cp"], NB + 2)
                for b in range(NB):
                    sp.dma_start(ig[b * H:(b + 1) * H, :], raw[:, 0, b * S:(b + 1) * S]).then_inc(s["lay"], 16)
                    sp.dma_start(fg[b * H:(b + 1) * H, :], raw[:, 1, b * S:(b + 1) * S]).then_inc(s["lay"], 16)
                sp.wait_ge(s["sc"], 1)
                sp.dma_start(Mrow, M[:, :]).then_inc(s["m_st"], 16)
                sp.wait_ge(s["m_st"], 16)

            @block.tensor
            def _(pe):
                pe.sem_inc(s["c_free"], 2)
                pe.wait_ge(s["w"], 64)
                with pe.Fori(0, NB // 2) as it:
                    for p in range(2):
                        b = it * 2 + p
                        pe.wait_ge(s[f"c{p}"], it * 16 + 16)
                        pe.wait_ge(s["gi_cp"], b + 1)
                        pe.wait_ge(s["gf_cp"], b + 1)
                        for W, o in ((WI, ips), (WF, fps)):
                            for j in range(6):
                                x = xT[:, j, ds(b * S, S)] if j < 2 else cT[:, p, j % 2, :]
                                last = nc.tensor.matmul(o[0:H, p, :], W[:, j, :], x, start=j == 0, stop=j == 5)
                        last.then_inc(s["gi"], 1)
                        pe.wait_ge(s["gi"], b + 1)
                        pe.sem_inc(s["c_free"], 1)
                pe.wait_ge(s["sc"], 1)
                for t in range(NT):
                    if t:
                        pe.wait_ge(s["tp_cp"], t)
                    nc.tensor.transpose(tps[:, 0, 0:NH], ig[:, t * P:(t + 1) * P], G.ident[0:NH, 0:NH])
                    nc.tensor.transpose(tps[:, 0, NH:2 * NH], fg[:, t * P:(t + 1) * P], G.ident[0:NH, 0:NH]).then_inc(s["tp"], 1)

            @block.scalar
            def _(act):
                act.wait_ge(s["w"], 64)
                act.sem_inc(s["gi_cp"], 2)
                act.sem_inc(s["gf_cp"], 2)
                with act.Fori(0, NB // 2) as it:
                    for p in range(2):
                        b = it * 2 + p
                        act.wait_ge(s["gi"], b + 1)
                        nc.scalar.activation(raw[:, 0, ds(b * S, S)], ips[0:H, p, :], ACT.Identity, bias=bi[:, 0:1]).then_inc(s["gi_cp"], 1)
                        nc.scalar.activation(raw[:, 1, ds(b * S, S)], fps[0:H, p, :], ACT.Identity, bias=bi[:, 1:2]).then_inc(s["gf_cp"], 1)
                act.wait_ge(s["lin"], 1)
                nc.scalar.activation(t1[:, :], t1[:, :], ACT.Exp).then_inc(s["actc"], 1)
                act.wait_ge(s["actc"], 1)
                nc.scalar.activation(t1[:, :], t1[:, :], ACT.Ln, bias=1.0).then_inc(s["ln"], 1)
                act.wait_ge(s["ex"], 1)
                nc.scalar.activation(fg[:, :], cs[:, :], ACT.Exp, scale=-1.0).then_inc(s["sc"], 1)
                for t in range(NT):
                    act.wait_ge(s["tp"], t + 1)
                    nc.scalar.copy(gT[:, t, :], tps[:, 0, 0:NH])
                    nc.scalar.copy(eT[:, t, :], tps[:, 0, NH:2 * NH]).then_inc(s["tp_cp"], 1)

            @block.vector
            def _(dve):
                ch = Chain(dve, s["dvc"])
                V = nc.vector
                V.memset(one[:, :], 1.0)
                dve.wait_ge(s["lay"], 16 * 2 * NB)
                ch.link(V.tensor_scalar(t1[:, :], fg[:, :], -1.0, None, ALU.mult))
                V.tensor_tensor(t1[:, :], t1[:, :], fg[:, :], ALU.min).then_inc(s["lin"], 1)
                ch.link(V.tensor_scalar(fg[:, :], fg[:, :], 0.0, None, ALU.min))
                dve.wait_ge(s["ln"], 1)
                ch.link(V.tensor_tensor(fg[:, :], fg[:, :], t1[:, :], ALU.subtract))
                ch.link(V.tensor_tensor_scan(cs[:, :], one[:, :], fg[:, :], 0.0, ALU.mult, ALU.add))
                ch.link(V.tensor_tensor(ig[:, :], ig[:, :], cs[:, :], ALU.subtract))
                ch.link(V.tensor_tensor_scan(M[:, :], one[:, :], ig[:, :], -3.0e38, ALU.mult, ALU.max))
                V.tensor_tensor(cs[:, :], cs[:, :], M[:, :], ALU.add).then_inc(s["ex"], 1)


def cell(nc, G, name, qs, ks, vs, Mrow, gT, eT, ln_scale, gate):
    H, DH = 8, 32
    NC, TPC, KR = 2, 3, 96
    DA = DH + 1
    SC = float(DH) ** -0.5
    EPS = 1e-6
    with phase(nc, name, "w qk0 qk1 qk_free v0 v1 ones m0 m1 m_free diag score d ct pv out_free stats rstd tri dvc poolc") as (s, sb, ps):
        Q = sb("Q", [P, 2, NC, H, S], BF16)
        K = sb("K", [P, 2, NC, H, S], BF16)
        V = sb("V", [P, 2, NT, H, DA])
        Mb = sb("Mb", [P, 2, S])
        Md = sb("Md", [P, 2, S])
        tri = sb("tri", [P, P])
        lns = sb("lns", [P, D])
        decay = sb("decay", [P, 2, S])
        C = sb("C", [P, NT, S])
        den = sb("den", [P, NT, H])
        neg = sb("neg", [P, NT, H])
        hs = sb("hs", [P, NT, D])
        st = sb("st", [P, NT, 6])
        mv = sb("mv", [P, NT, 2])
        rstd = sb("rstd", [P, NT])
        sps = ps("sps", [P, 2, S])
        ops = ps("ops", [P, NT, S])

        def unit(b, h, k):
            return b * (H * NT) + h * NT + k

        with nc.Block() as block:

            @block.sync
            def _(sp):
                sp.dma_start(lns[:, :], ln_scale.unsqueeze(0).broadcast_to([P, D])).then_inc(s["w"], 16)
                with sp.Fori(0, NB * H // 2) as i:
                    for hp in range(2):
                        sp.wait_ge(s["m_free"], i * 2 + hp + 1)
                        alone(sp)
                        sp.dma_start(Mb[:, hp, :], Mrow[ds(i * 2 + hp, 1), :].broadcast_to([P, S])).then_inc(s[f"m{hp}"], 16)

            @block.gpsimd
            def _(pool):
                ch = Chain(pool, s["poolc"])
                for p in range(2):
                    for t in range(NT):
                        last = nc.gpsimd.memset(V[:, p, t, :, DH:DA], 1.0)
                ch.link(last)
                ch.link(nc.gpsimd.memset(tri[:, :], 0.0))
                nc.gpsimd.affine_select(out=tri[:, :], in_=tri[:, :], compare_op=ALU.is_ge, fill=BIG, base=0,
                                        pattern=[[1, P]], channel_multiplier=-1).then_inc(s["tri"], 1)
                pool.wait_ge(s["tri"], 1)

                def load(b, p):
                    pool.wait_ge(s["qk_free"], b + 1)
                    for i, (qp, kp) in enumerate(TERMS):
                        c, r = i // TPC, i % TPC
                        for dst, part, src in ((Q, qp, qs), (K, kp, ks)):
                            pool.dma_start(dst[r * DH:(r + 1) * DH, p, c],
                                           src[part - 1].rearrange("(h d) t -> d h t", d=DH)[:, :, ds(b * S, S)]).then_inc(s[f"qk{p}"], 16)
                    for t in range(NT):
                        pool.dma_start(V[:, p, t, :, 0:DH], vs[ds(b * S + t * P, P), :].rearrange("p (h d) -> p h d", d=DH)).then_inc(s[f"v{p}"], 16)

                load(0, 0)
                load(1, 1)

                def sequence(b, p, more):
                    with pool.Fori(0, H // 2) as hh:
                        for hp in range(2):
                            n = b * H + hh * 2 + hp
                            pool.wait_ge(s[f"m{hp}"], b * (8 * H) + hh * 16 + 16)
                            pool.wait_ge(s["m_free"], n + 1)
                            nc.gpsimd.tensor_tensor(Md[:, hp, :].rearrange("p (t c) -> p t c", c=P), Mb[:, hp, :].rearrange("p (t c) -> p t c", c=P),
                                                    tri[:, :].unsqueeze(1).broadcast_to([P, NT, P]), ALU.add).then_inc(s["diag"], 1)
                    pool.wait_ge(s["stats"], b + 1)
                    alone(pool)
                    ch.at(b + 2)
                    ch.link(nc.gpsimd.tensor_scalar(rstd[:, :], mv[:, :, 1], LN_EPS, None, ALU.add))
                    nc.gpsimd.tensor_tensor(rstd[:, :], rstd[:, :], G.mhalf[:, 0:NT], ALU.pow).then_inc(s["rstd"], 1)
                    if more:
                        load(b + 2, p)

                with pool.Fori(0, NB // 2 - 1) as it:
                    for p in range(2):
                        sequence(it * 2 + p, p, True)
                for p in range(2):
                    sequence(NB - 2 + p, p, False)

            @block.tensor
            def _(pe):
                pe.sem_inc(s["qk_free"], 2)

                def scores(p, b, h, k):
                    w = (NT - k) * P
                    for c in range(NC):
                        last = nc.tensor.matmul(sps[:, k % 2, 0:w], K[0:KR, p, c, ds(h, 1), k * P:(k + 1) * P].rearrange("p o t -> p (o t)"),
                                                Q[0:KR, p, c, ds(h, 1), k * P:S].rearrange("p o t -> p (o t)"), start=c == 0, stop=c == NC - 1)
                    last.then_inc(s["score"], 1)

                def head(p, b, h, final):
                    for k in range(NT):
                        pe.wait_ge(s["ct"], unit(b, h, k) + 3)
                        if not (final and k >= NT - 2):
                            scores(p, b, h + (k + 2) // NT, (k + 2) % NT)
                        for t in range(k, NT):
                            last = nc.tensor.matmul(ops[:, t, ds(h * DA, DA)], C[:, k, (t - k) * P:(t - k + 1) * P],
                                                    V[:, p, k, ds(h, 1), :].rearrange("p o d -> p (o d)"), start=k == 0, stop=k == t, skip_group_check=True)
                    if final:
                        last.then_inc(s["pv"], 1)

                with pe.Fori(0, NB // 2) as it:
                    for p in range(2):
                        b = it * 2 + p
                        pe.wait_ge(s[f"qk{p}"], it * (16 * 12) + 16 * 12)
                        scores(p, b, 0, 0)
                        scores(p, b, 0, 1)
                        pe.wait_ge(s[f"v{p}"], it * 64 + 64)
                        pe.wait_ge(s["out_free"], b + 1)
                        alone(pe)
                        with pe.Fori(0, H - 1) as h:
                            head(p, b, h, False)
                        head(p, b, H - 1, True)
                        pe.wait_ge(s["pv"], b + 1)
                        pe.sem_inc(s["qk_free"], 1)

            @block.scalar
            def _(act):
                act.sem_inc(s["m_free"], 2)
                with act.Fori(0, NB * H // 2) as i:
                    for hp in range(2):
                        n = i * 2 + hp
                        act.wait_ge(s["diag"], n + 1)
                        for k in range(NT):
                            act.wait_ge(s["ct"], n * NT + k + 1)
                            g = gT[:, k, ds(n, 1)]
                            last = nc.scalar.activation(decay[:, k % 2, 0:P], Md[:, hp, k * P:(k + 1) * P], ACT.Exp, scale=-1.0, bias=g)
                            if k < NT - 1:
                                last = nc.scalar.activation(decay[:, k % 2, P:(NT - k) * P], Mb[:, hp, (k + 1) * P:S], ACT.Exp, scale=-1.0, bias=g)
                            last.then_inc(s["d"], 1)
                        act.wait_ge(s["d"], n * NT + NT)
                        act.sem_inc(s["m_free"], 1)

            @block.vector
            def _(dve):
                ch = Chain(dve, s["dvc"])
                dve.sem_inc(s["ct"], 2)
                dve.sem_inc(s["out_free"], 1)
                dve.wait_ge(s["w"], 16)
                KCH = 10
                with dve.Fori(0, NB) as b:
                    with dve.Fori(0, H) as h:
                        for k in range(NT):
                            w = (NT - k) * P
                            dve.wait_ge(s["score"], unit(b, h, k) + 1)
                            dve.wait_ge(s["d"], unit(b, h, k) + 1)
                            nc.vector.scalar_tensor_tensor(C[:, k, 0:w], sps[:, k % 2, 0:w], SC, decay[:, k % 2, 0:w], ALU.mult, ALU.mult).then_inc(s["ct"], 1)
                    ch.at(b * KCH)
                    dve.wait_ge(s["pv"], b + 1)
                    rows = ops[:, :, 0:H * DA].rearrange("p t (h d) -> p t h d", d=DA)
                    total = rows[:, :, :, DH]
                    ch.link(nc.vector.tensor_scalar(neg[:, :, :], total, -1.0, None, ALU.mult))
                    ch.link(nc.vector.tensor_tensor(den[:, :, :], total, neg[:, :, :], ALU.max))
                    ch.link(nc.vector.tensor_tensor(den[:, :, :], den[:, :, :], eT[:, :, ds(b * H, H)], ALU.max))
                    ch.link(nc.vector.tensor_scalar(den[:, :, :], den[:, :, :], EPS, None, ALU.add))
                    ch.link(nc.vector.reciprocal(den[:, :, :], den[:, :, :]))
                    for t in range(NT):
                        last = nc.vector.tensor_tensor(hs[:, t, :].rearrange("p (h d) -> p h d", d=DH), rows[:, t, :, 0:DH],
                                                       den[:, t, :].unsqueeze(2).broadcast_to([P, H, DH]), ALU.mult)
                    ch.link(last)
                    dve.sem_inc(s["out_free"], 1)
                    for t in range(NT):
                        last = nc.vector.bn_stats(st[:, t, :], hs[:, t, :])
                    ch.link(last)
                    alone(dve)
                    for t in range(NT):
                        last = nc.vector.bn_aggr(mv[:, t, :], st[:, t, :])
                    last.then_inc(s["stats"], 1)
                    dve.wait_ge(s["rstd"], b + 1)
                    for t in range(NT):
                        last = nc.vector.tensor_scalar(hs[:, t, :], hs[:, t, :], mv[:, t, 0:1], rstd[:, t:t + 1], ALU.subtract, ALU.mult)
                    ch.link(last)
                    ch.link(nc.vector.tensor_tensor(hs[:, :, :], hs[:, :, :], lns[:, :].unsqueeze(1).broadcast_to([P, NT, D]), ALU.mult))
                    x = G.X[:, ds(b * NT, NT), :].rearrange("p t d -> p (t d)")
                    ch.link(nc.vector.scalar_tensor_tensor(x, hs[:, :, :].rearrange("p t d -> p (t d)"), G.gate[:, gate:gate + 1], x, ALU.mult, ALU.add))
                    ch.done(KCH)


class Globals:
    pass


def program(nc, a):
    G = Globals()
    with ExitStack() as ctx:
        def sb(name, shape, dt=F32):
            return ctx.enter_context(nc.sbuf_tensor(name, shape, dt))

        def dram(name, shape, dt=F32):
            return nc.dram_tensor(name, shape, dt).ap()

        G.X = sb("stream", [P, TT, D])
        G.ident = sb("ident", [P, P])
        G.identb = sb("identb", [P, P], BF16)
        G.masks = sb("masks", [P, 3, P], BF16)
        G.gate = sb("gate", [P, 8])
        G.ones = sb("ones", [1, P])
        G.mhalf = sb("mhalf", [P, 32])
        G.qs = dram("q_parts", [3, 512, TOK], BF16)
        G.ks = dram("k_parts", [3, 512, TOK], BF16)
        G.vs = dram("values", [TOK, D])
        G.os = dram("attended", [TOK, D])
        constants(nc, G, a)
        qs, ks = G.qs[:, 0:D, :], G.ks[:, 0:D, :]
        if 0 in STAGES:
            rel = [dram(f"rel{t}", [NB * 16, P * (t + 1) * P]) for t in range(NT)]
            qkv(nc, G, "a0", G.X,
                [("wk", i, "c", "bk", 1.0, ks, i * P) for i in range(KT)] + [("wq", i, "x", "bq", -0.25, qs, i * P) for i in range(KT)],
                {"wq": (w_view(a["L0_xattn_Wq"]), [P, KT, D]), "wk": (w_view(a["L0_xattn_Wk"]), [P, KT, D]),
                 "wv": (w_view(a["L0_xattn_Wv"]), [P, KT, D]), "bq": (a["L0_xattn_bq"], [P, KT]),
                 "bk": (a["L0_xattn_bk"], [P, KT]), "bv": (a["L0_xattn_bv"].unsqueeze(0), [1, D])},
                ("wv", "c", "bv", G.vs, D), ctx=a["ctx_T"])
            rel_scores(nc, G, "r0", qs, a["L0_xattn_Er"], rel)
            attention(nc, G, "t0", qs, ks, G.vs, 16, 16, lambda t: (0, t + 1), masks=lambda t: [(t, 2)], rel=rel, direct=0)
        every = lambda t: (0, NT)
        ident_tile = lambda t: [(k, min(P, (D >> t) - k * P)) for k in range(KT) if (D >> t) > k * P]
        if 1 in STAGES:
            quantised_ffn(nc, G, a)
        if 2 in STAGES:
            maskrow = dram("mask_row", [NB, S], BF16)
            key_mask(nc, G, "m1", a["mask_BxS2_ik0"], maskrow)
            wkv = w_view(a["L1_xattn_Wkv"])
            qkv(nc, G, "a1", G.X,
                [("wk", i, "c", None, 1.0, ks, i * P) for i in range(KT)] + [("wq", i, "x", None, 0.25, qs, i * P) for i in range(KT)],
                {"wq": (w_view(a["L1_xattn_Wq"]), [P, KT, D]), "wk": (wkv[:, :, 0:D], [P, KT, D]), "wv": (wkv[:, :, D:2 * D], [P, KT, D])},
                ("wv", "c", None, G.vs, D), ctx=a["ctx_T"])
            attention(nc, G, "t1", qs, ks, G.vs, 16, 16, every, maskrow=maskrow, odst=G.os)
            outproj(nc, G, "o1", G.os, w_view(a["L1_xattn_Wproj"]), [P, KT, D], a["L1_xattn_bproj"].unsqueeze(0), 1, G.X)
        if 3 in STAGES:
            with ExitStack() as part:
                xT = part.enter_context(nc.sbuf_tensor("moeT", [P, KT, TOK], F32))
                combT = part.enter_context(nc.sbuf_tensor("combT", [16, TOK], F32))
                with nc.sbuf_tensor("moe_rows", [P, TT, D], F32) as Y:
                    normalise(nc, G, "n3", G.X, Y)
                    turn(nc, G, "x3", Y, xT)
                G.before, G.spread = a["c_before"], a["c_spread"]
                route(nc, G, "r3", xT, w_view(a["L1_ffn_router_w"]), a["L1_ffn_correction_bias"], combT)
                R = 16 * 64

                def both(routed, shared):
                    return [(w_view(a[f"L1_ffn_{routed}_w"]), 0), (w_view(a[f"L1_ffn_shared_{shared}_w"]), R)]

                gated_mlp(nc, G, "f3", xT, both("gate", "gate"), both("up", "up"),
                          [(w_view(a["L1_ffn_down_w"]), 0), (w_view(a["L1_ffn_shared_down_w"]), R // P)],
                          12, ACT.Silu, G.X, 5, combT=combT, routed=8)
        if 4 in STAGES:
            with ExitStack() as part:
                gT = part.enter_context(nc.sbuf_tensor("cell_g", [P, NT, NB * 8], F32))
                eT = part.enter_context(nc.sbuf_tensor("cell_e", [P, NT, NB * 8], F32))
                Mrow = dram("cell_max", [NB * 8, S])
                with ExitStack() as part2:
                    xT = part2.enter_context(nc.sbuf_tensor("cellT", [P, KT, TOK], F32))
                    with nc.sbuf_tensor("cell_rows", [P, TT, D], F32) as Y:
                        normalise(nc, G, "n4", G.X, Y)
                        turn(nc, G, "x4", Y, xT)
                    cell_gates(nc, G, "g4", xT, a, Mrow, gT, eT)
                eye = (w_view(a["c_eye"]), [P, KT, D])
                qkv(nc, G, "a4", G.X,
                    [("eye", i, "c", None, 1.0, ks, i * P) for i in range(KT)] + [("eye", i, "x", None, 1.0, qs, i * P) for i in range(KT)],
                    {"eye": eye}, ("eye", "c", None, G.vs, D), ctx=a["ctx_T"])
                cell(nc, G, "t4", qs, ks, G.vs, Mrow, gT, eT, a["L2_xattn_ln_scale"], 2)
        if 5 in STAGES:
            with nc.sbuf_tensor("inner2", [P, TT, D], F32) as Y:
                G.Y = Y
                G.rotary = a["c_rotary"]
                vs5, os5 = dram("values5", [TOK, 512]), dram("attended5", [TOK, 512])
                normalise(nc, G, "n5", G.X, Y)
                for d in range(2):
                    rotary_qkv(nc, G, f"a5{d}", Y, a["L2_ffn_wqkv"][d], a["L2_ffn_q_scale"][d], a["L2_ffn_k_scale"][d], G.qs, G.ks, vs5)
                    attention(nc, G, f"t5{d}", G.qs, G.ks, vs5, 8, 64, lambda t: (max(0, t - 1), t + 1),
                              masks=lambda t: [(t, 0)] if t == 0 else [(t - 1, 1), (t, 0)], odst=os5)
                    outproj(nc, G, f"o5{d}", os5, w_view(a["L2_ffn_wo"][d]), [P, 4, D], None, None, Y)
                    w1 = w_view(a["L2_ffn_w1"][d])
                    gated_mlp(nc, G, f"f5{d}", ("shift", Y, a["L2_ffn_ln_g"][d], a["L2_ffn_ln_b"][d]),
                              [(w1[:, :, 768:1536], 0)], [(w1[:, :, 0:768], 0)], [(w_view(a["L2_ffn_w2"][d]), 0)], 6, ACT.Gelu, Y, None,
                              bg=a["L2_ffn_b1"][d, :, 6:12], bu=a["L2_ffn_b1"][d, :, 0:6], bd=a["L2_ffn_b2"][d:d + 1, :])
                add_stream(nc, G, "s5", 6)
        if 6 in STAGES:
            qkv(nc, G, "a3", G.X,
                [("wk", i, "c", "bk", 1.0, ks, i * P) for i in range(KT)] + [("wq", i, "x", "bq", 0.25, qs, i * P) for i in range(KT)],
                {"wq": (w_view(a["L3_xattn_Wq"]), [P, KT, D]), "wk": (w_view(a["L3_xattn_Wk"]), [P, KT, D]),
                 "wv": (w_view(a["L3_xattn_Wv"]), [P, KT, D]), "bq": (a["L3_xattn_bq"], [P, KT]),
                 "bk": (a["L3_xattn_bk"], [P, KT]), "bv": (a["L3_xattn_bv"].unsqueeze(0), [1, D])},
                ("wv", "c", "bv", G.vs, D), ctx=a["ctx_T"])
            attention(nc, G, "t3", qs, ks, G.vs, 16, 16, every, odst=G.os)
            outproj(nc, G, "o3", G.os, w_view(a["L3_xattn_Wo"]), [P, KT, D], a["L3_xattn_bo"].unsqueeze(0), 3, G.X)
        if 7 in STAGES:
            G.Y = sb("inner3", [P, TT, D])
            normalise(nc, G, "n7", G.X, G.Y)
            qkv(nc, G, "a7", G.Y,
                [("wk", i, "x", "bk", 1.0, ks, i * P) for i in range(KT)] + [("wq", i, "x", "bq", D ** -0.5, qs, i * P) for i in range(KT)],
                {"wq": (w_view(a["L3_ffn_q_w"]), [P, KT, D]), "wk": (w_view(a["L3_ffn_k_w"]), [P, KT, D]),
                 "wv": (w_view(a["L3_ffn_v_w"]), [P, KT, D]), "bq": (a["L3_ffn_q_b"], [P, KT]),
                 "bk": (a["L3_ffn_k_b"], [P, KT]), "bv": (a["L3_ffn_v_b"].unsqueeze(0), [1, D]),
                 "nw": (a["L3_ffn_norm_w"], [P, KT]), "nb": (a["L3_ffn_norm_b"], [P, KT])},
                ("wv", "x", "bv", G.vs, D), affine=("nw", "nb"), tile_k=ident_tile)
            attention(nc, G, "t7", qs, ks, G.vs, 8, 32, every, odst=G.os)
            outproj(nc, G, "o7", G.os, w_view(a["L3_ffn_o_w"]), [P, KT, D], a["L3_ffn_o_b"].unsqueeze(0), 7, G.X, also=G.Y, tile_k=ident_tile)
        store(nc, G, a)


TRANSPOSED = ("L0_xattn_Wq", "L0_xattn_Wk", "L0_xattn_Wv", "L0_xattn_Er",
              "L3_ffn_q_w", "L3_ffn_k_w", "L3_ffn_v_w", "L3_ffn_o_w", "L1_ffn_router_w", "L1_ffn_shared_gate_w",
              "L1_ffn_shared_up_w", "L1_ffn_shared_down_w", "L2_xattn_igate_w", "L2_xattn_fgate_w")

COLUMNS = ("L0_xattn_bq", "L0_xattn_bk", "L3_xattn_bq", "L3_xattn_bk", "L3_ffn_q_b", "L3_ffn_k_b", "L3_ffn_norm_w",
           "L3_ffn_norm_b")


def rotary_tables(np):
    DH, WINDOW = 64, 128
    half = np.arange(0, DH, 2, dtype=np.float32)
    inv_freq = (1.0 / np.float32(10000.0) ** (half / DH)).astype(np.float32)
    t = np.arange(S, dtype=np.float32)
    freqs = (t[:, None] * inv_freq[None, :]).astype(np.float32)
    base = ((half + 0.4 * DH) / (1.4 * DH)).astype(np.float32)
    power = ((t - S // 2) / (WINDOW // 2)).astype(np.float32)
    scale = (base[None, :] ** power[:, None]).astype(np.float32)
    cos, sin = np.cos(freqs), np.sin(freqs)
    turned = [np.concatenate(x, 1) for x in ((cos * scale, cos * scale), (-sin * scale, sin * scale), (cos / scale, cos / scale), (-sin / scale, sin / scale))]
    return np.stack([turned[0] * 8, turned[1] * 8, turned[2], turned[3]]).astype(np.float32)


def kernel(**inputs):
    import numpy as np
    import concourse.bacc as bacc
    from concourse.bass_utils import run_bass_kernel_spmd

    arrays = {}
    for name, v in inputs.items():
        v = np.asarray(v)
        if name in TRANSPOSED:
            v = v.T
        if name in COLUMNS:
            v = v.reshape(-1, P).T
        arrays[name] = np.ascontiguousarray(v)
    arrays["ctx_T"] = np.ascontiguousarray(arrays.pop("ctx_1024").transpose(2, 0, 1).reshape(D, TOK))
    p, c = np.meshgrid(np.arange(P), np.arange(P), indexing="ij")
    for n in ("gate", "up"):
        w = arrays[f"L1_ffn_{n}_w"]
        arrays[f"L1_ffn_{n}_w"] = np.ascontiguousarray(w.transpose(1, 0, 2).reshape(D, -1))
    arrays["L1_ffn_down_w"] = arrays["L1_ffn_down_w"].reshape(-1, D)
    for n in ("igate", "fgate"):
        arrays[f"L2_xattn_{n}_b"] = arrays[f"L2_xattn_{n}_b"].reshape(-1, 1)
    half, full = arrays["L2_ffn_w2"].shape[1], 6 * P
    for n, axis in (("L2_ffn_w1", 2), ("L2_ffn_b1", 1)):
        arrays[n] = np.concatenate([np.concatenate([x, np.zeros_like(x[..., :full - half])], axis) for x in np.split(arrays[n], 2, axis)], axis)
    arrays["L2_ffn_w2"] = np.concatenate([arrays["L2_ffn_w2"], np.zeros_like(arrays["L2_ffn_w2"][:, :full - half])], 1)
    for n in ("L2_ffn_b1", "L2_ffn_ln_g", "L2_ffn_ln_b"):
        arrays[n] = np.ascontiguousarray(arrays[n].reshape(2, -1, P).transpose(0, 2, 1))
    arrays["c_eye"] = np.eye(D, dtype=np.float32)
    arrays["c_before"] = np.tril(np.ones((16, 16), np.float32), -1).reshape(-1)
    arrays["c_spread"] = np.repeat(np.eye(16, dtype=np.float32).reshape(16, 8, 2), 64, axis=2)
    arrays["c_rotary"] = rotary_tables(np)
    arrays["c_ident"] = np.eye(P, dtype=np.float32)
    arrays["c_masks"] = np.stack([np.where(c <= p, 0.0, -BIG), np.where(c >= p, 0.0, -BIG), np.where(c <= p, 0.0, BIG)]).astype(np.float32)
    nc = bacc.Bacc("TRN2", target_bir_lowering=False, num_devices=1)
    feeds, a = {}, {}
    for name, v in arrays.items():
        feeds[f"in_{name}"] = v
        a[name] = nc.dram_tensor(f"in_{name}", v.shape, mybir.dt.from_np(v.dtype), kind="ExternalInput").ap()
    a["out"] = nc.dram_tensor("out_x", (NB, S, D), F32, kind="ExternalOutput").ap()
    program(nc, a)
    r = run_bass_kernel_spmd(nc, [feeds], core_ids=[0])
    return r.results[0]["out_x"]
```

```python
from contextlib import ExitStack, contextmanager

import concourse.bass as bass
from concourse import mybir

STAGES = (0, 1, 2, 3, 4, 5, 6, 7)

F32 = mybir.dt.float32
BF16 = mybir.dt.bfloat16
ALU = mybir.AluOpType
ACT = mybir.ActivationFunctionType
AX = mybir.AxisListType

P = 128
NB = 8
S = 512
D = 256
NT = S // P
TT = NB * NT
KT = D // P
TOK = NB * S
BIG = 1.0e30
LN_EPS = 1e-5
ds = bass.ds

TERMS = ((1, 1), (1, 2), (2, 1), (1, 3), (3, 1), (2, 2))


def alone(eng):
    eng.nop(nofuse=True)


class Chain:

    def __init__(self, eng, sem):
        self.eng, self.sem, self.base, self.n = eng, sem, 0, 0

    def at(self, base):
        self.base, self.n = base, 0

    def mark(self, ins):
        ins.then_inc(self.sem, 1)
        self.n += 1
        return self.n

    def wait(self, n=None):
        self.eng.wait_ge(self.sem, self.base + (self.n if n is None else n))

    def link(self, ins):
        self.mark(ins)
        self.wait()

    def done(self, k):
        assert self.n == k, (self.n, k)


@contextmanager
def phase(nc, name, sems):
    with ExitStack() as ctx:
        got = {s: nc.alloc_semaphore(f"{name}_{s}") for s in sems.split()}

        def sb(what, shape, dt=F32):
            return ctx.enter_context(nc.sbuf_tensor(f"{name}_{what}", shape, dt))

        def ps(what, shape, dt=F32):
            return ctx.enter_context(nc.psum_tensor(f"{name}_{what}", shape, dt))

        yield got, sb, ps
    nc.clear_and_free_semaphores(list(got.values()))
    nc.all_engine_barrier()


def w_view(w):
    return w.rearrange("(k p) n -> p k n", p=P)


def constants(nc, G, a):
    with phase(nc, "const", "loaded cast done") as (s, sb, ps):
        masks32 = sb("masks32", [P, 3, P])
        graw = sb("graw", [P, 8])
        with nc.Block() as block:

            @block.sync
            def _(sp):
                sp.dma_start(G.X[:, :, :], a["x"].rearrange("b (t p) d -> p (b t) d", p=P)).then_inc(s["loaded"], 16)
                sp.dma_start(G.ident[:, :], a["c_ident"]).then_inc(s["loaded"], 16)
                sp.dma_start(masks32[:, :, :], a["c_masks"].rearrange("m p c -> p m c")).then_inc(s["loaded"], 16)
                sp.dma_start(graw[:, 0:4], a["g_xattn"].unsqueeze(0).broadcast_to([P, 4])).then_inc(s["loaded"], 16)
                sp.dma_start(graw[:, 4:8], a["g_ffn"].unsqueeze(0).broadcast_to([P, 4])).then_inc(s["loaded"], 16)

            @block.scalar
            def _(act):
                act.wait_ge(s["loaded"], 80)
                nc.scalar.activation(G.gate[:, :], graw[:, :], ACT.Tanh).then_inc(s["done"], 1)

            @block.vector
            def _(dve):
                dve.wait_ge(s["loaded"], 80)
                nc.vector.tensor_copy(G.identb[:, :], G.ident[:, :])
                nc.vector.tensor_copy(G.masks[:, :, :], masks32[:, :, :])
                nc.vector.memset(G.ones[:, :], 1.0)
                nc.vector.memset(G.mhalf[:, :], -0.5).then_inc(s["done"], 1)


def store(nc, G, a):
    with phase(nc, "store", "stored") as (s, sb, ps):
        with nc.Block() as block:

            @block.sync
            def _(sp):
                sp.dma_start(a["out"].rearrange("b (t p) d -> p (b t) d", p=P), G.X[:, :, :]).then_inc(s["stored"], 16)
                sp.wait_ge(s["stored"], 16)


def qkv(nc, G, name, src, jobs, weights, vjob, ctx=None, affine=None, tile_k=None, nlog=0):
    nj = len(jobs)
    scaled = sorted({(j[3], j[4]) for j in jobs if j[3] and j[4] != 1.0})
    with phase(nc, name, "w c0 c1 c_free stats rstd xn xn_free xt_ps xt_ps_free xt xt_free "
               "job job_free q32 q32_free parts parts_st0 parts_st1 v v_free v_sb v_st0 v_st1 dvc poolc actc") as (s, sb, ps):
        W = {k: sb(k, shape) for k, (view, shape) in weights.items()}
        xn = sb("xn", [P, 2, NT, D])
        xT = sb("xT", [P, 2, KT, S])
        cT = sb("cT", [P, 2, KT, S])
        st = sb("st", [P, NT, 6])
        mv = sb("mv", [P, 2, NT, 2])
        rstd = sb("rstd", [P, 2, NT])
        q32 = sb("q32", [P, 2, S])
        r1 = sb("r1", [P, S])
        r2 = sb("r2", [P, S])
        parts = sb("parts", [P, 2, 3, S], BF16)
        vw, vsrc, vb, vdst, VW = vjob
        NVB = NT * VW // S
        VT = S // VW
        vsb = sb("vsb", [P, 2, NT, VW])
        xps = ps("xps", [P, KT, S])
        jps = ps("jps", [P, 4, S])
        vps = ps("vps", [P, 2, S])
        link_per_batch = 5 * nj + 1

        with nc.Block() as block:

            @block.sync
            def _(sp):
                for c in ("parts_st0", "parts_st1", "v_st0", "v_st1"):
                    sp.sem_inc(s[c], 16)
                for k, (view, shape) in weights.items():
                    sp.dma_start(W[k][tuple(slice(None) for _ in shape)], view).then_inc(s["w"], 16)

                def load(b, p):
                    if ctx is not None:
                        sp.wait_ge(s["c_free"], b + 1)
                        sp.dma_start(cT[:, p], ctx.rearrange("(k p) t -> p k t", p=P)[:, :, ds(b * S, S)]).then_inc(s[f"c{p}"], 16)

                def save(b, p):
                    for j, (wn, blk, sc, bias, scale, dst, row) in enumerate(jobs):
                        sp.wait_ge(s["parts"], b * nj + j + 1)
                        alone(sp)
                        sp.dma_start(dst.rearrange("r f t -> f r t")[row:row + P, :, ds(b * S, S)],
                                     parts[:, j % 2]).then_inc(s[f"parts_st{j % 2}"], 16)
                    sp.wait_ge(s["v_sb"], (b + 1) * NVB)
                    sp.dma_start(vdst.rearrange("(t p) d -> p t d", p=P)[:, ds(b * NT, NT), :], vsb[:, p]).then_inc(s[f"v_st{p}"], 16)

                load(0, 0)
                load(1, 1)
                with sp.Fori(0, NB // 2 - 1) as it:
                    for p in range(2):
                        b = it * 2 + p
                        save(b, p)
                        load(b + 2, p)
                for p in range(2):
                    save(NB - 2 + p, p)
                sp.wait_ge(s["parts_st0"], 16 + 16 * NB * ((nj + 1) // 2))
                sp.wait_ge(s["parts_st1"], 16 + 16 * NB * (nj // 2))
                for p in range(2):
                    sp.wait_ge(s[f"v_st{p}"], 16 + 16 * NB // 2)

            @block.gpsimd
            def _(pool):
                ch = Chain(pool, s["poolc"])
                with pool.Fori(0, NB // 2) as it:
                    for p in range(2):
                        b = it * 2 + p
                        ch.at(b)
                        pool.wait_ge(s["stats"], b + 1)
                        alone(pool)
                        ch.link(nc.gpsimd.tensor_scalar(rstd[:, p, :], mv[:, p, :, 1], LN_EPS, None, ALU.add))
                        nc.gpsimd.tensor_tensor(rstd[:, p, :], rstd[:, p, :], G.mhalf[:, 0:NT], ALU.pow).then_inc(s["rstd"], 1)
                        ch.done(1)

            @block.vector
            def _(dve):
                ch = Chain(dve, s["dvc"])
                dve.sem_inc(s["q32_free"], 2)

                def rows(b, p, before):
                    ch.at(before)
                    for t in range(NT):
                        last = nc.vector.bn_stats(st[:, t, :], src[:, ds(b * NT + t, 1), :].rearrange("p o d -> p (o d)"))
                    ch.link(last)
                    alone(dve)
                    for t in range(NT):
                        last = nc.vector.bn_aggr(mv[:, p, t, :], st[:, t, :])
                    last.then_inc(s["stats"], 1)
                    dve.wait_ge(s["rstd"], b + 1)
                    dve.wait_ge(s["xn_free"], b + 1)
                    for t in range(NT):
                        last = nc.vector.tensor_scalar(xn[:, p, t, :], src[:, ds(b * NT + t, 1), :].rearrange("p o d -> p (o d)"),
                                                       mv[:, p, t, 0:1], rstd[:, p, t:t + 1], ALU.subtract, ALU.mult)
                    last.then_inc(s["xn"], 1)

                def split(b, before):
                    ch.at(before)
                    for j in range(nj):
                        dve.wait_ge(s["q32"], b * nj + j + 1)
                        q = q32[:, j % 2, :]
                        k = (nj + 1 - j % 2) // 2
                        dve.wait_ge(s[f"parts_st{j % 2}"], b * (16 * k) + 16 * (j // 2) + 16)
                        ch.link(nc.vector.tensor_copy(parts[:, j % 2, 0, :], q))
                        ch.link(nc.vector.tensor_tensor(r1[:, :], q, parts[:, j % 2, 0, :], ALU.subtract))
                        ch.link(nc.vector.tensor_copy(parts[:, j % 2, 1, :], r1[:, :]))
                        ch.link(nc.vector.tensor_tensor(r2[:, :], r1[:, :], parts[:, j % 2, 1, :], ALU.subtract))
                        ch.link(nc.vector.tensor_copy(parts[:, j % 2, 2, :], r2[:, :]))
                        dve.sem_inc(s["parts"], 1)
                        dve.sem_inc(s["q32_free"], 1)

                rows(0, 0, 0)
                with dve.Fori(0, NB // 2 - 1) as it:
                    for p in range(2):
                        b = it * 2 + p
                        rows(b + 1, 1 - p, b * link_per_batch + 1)
                        split(b, b * link_per_batch + 2)
                rows(NB - 1, 1, (NB - 2) * link_per_batch + 1)
                split(NB - 2, (NB - 2) * link_per_batch + 2)
                split(NB - 1, (NB - 1) * link_per_batch + 1)

            @block.scalar
            def _(act):
                act.sem_inc(s["xt_ps_free"], 1)
                act.sem_inc(s["job_free"], 4)
                act.sem_inc(s["v_free"], 2)
                act.wait_ge(s["w"], 16 * len(weights))
                for bias, scale in scaled:
                    nc.scalar.activation(W[bias][:, :], W[bias][:, :], ACT.Copy, scale=scale).then_inc(s["actc"], 1)
                if scaled:
                    act.wait_ge(s["actc"], len(scaled))
                with act.Fori(0, NB // 2) as it:
                    for p in range(2):
                        b = it * 2 + p
                        act.wait_ge(s["xt_ps"], b + 1)
                        act.wait_ge(s["xt_free"], b + 1)
                        for k in range(KT):
                            if affine:
                                last = nc.scalar.activation(xT[:, p, k, :], xps[:, k, :], ACT.Identity,
                                                            scale=W[affine[0]][:, k:k + 1], bias=W[affine[1]][:, k:k + 1])
                            else:
                                last = nc.scalar.copy(xT[:, p, k, :], xps[:, k, :])
                        last.then_inc(s["xt"], 1)
                        act.sem_inc(s["xt_ps_free"], 1)
                        for j, (wn, blk, sc, bias, scale, dst, row) in enumerate(jobs):
                            act.wait_ge(s["job"], b * nj + j + 1)
                            act.wait_ge(s["q32_free"], b * nj + j + 1)
                            o = q32[:, j % 2, :]
                            if bias:
                                ins = nc.scalar.activation(o, jps[:, j % 4, :], ACT.Identity, scale=scale, bias=W[bias][:, blk:blk + 1])
                            else:
                                ins = nc.scalar.activation(o, jps[:, j % 4, :], ACT.Copy, scale=scale)
                            ins.then_inc(s["q32"], 1)
                            act.wait_ge(s["q32"], b * nj + j + 1)
                            act.sem_inc(s["job_free"], 1)
                        act.wait_ge(s[f"v_st{p}"], it * 16 + 16)
                        for v in range(NVB):
                            act.wait_ge(s["v"], b * NVB + v + 1)
                            nc.scalar.copy(vsb[:, p, v * VT:(v + 1) * VT, :], vps[:, v % 2, :].rearrange("p (t d) -> p t d", d=VW)).then_inc(s["v_sb"], 1)
                            act.wait_ge(s["v_sb"], b * NVB + v + 1)
                            act.sem_inc(s["v_free"], 1)

            @block.tensor
            def _(pe):
                pe.sem_inc(s["xn_free"], 2)
                pe.sem_inc(s["xt_free"], 2)
                pe.sem_inc(s["c_free"], 2)
                pe.wait_ge(s["w"], 16 * len(weights))
                with pe.Fori(0, NB // 2) as it:
                    for p in range(2):
                        b = it * 2 + p
                        pe.wait_ge(s["xn"], b + 1)
                        pe.wait_ge(s["xt_ps_free"], b + 1)
                        for k in range(KT):
                            for t in range(NT):
                                last = nc.tensor.transpose(xps[:, k, t * P:(t + 1) * P], xn[:, p, t, k * P:(k + 1) * P], G.ident[:, :])
                        last.then_inc(s["xt_ps"], 1)
                        pe.wait_ge(s["xt_ps"], b + 1)
                        pe.sem_inc(s["xn_free"], 1)
                        if ctx is not None:
                            pe.wait_ge(s[f"c{p}"], it * 16 + 16)
                        xt_waited = False

                        def source(sc):
                            return xT if sc == "x" else cT

                        order = list(enumerate(jobs))
                        for j, (wn, blk, sc, bias, scale, dst, row) in order:
                            if sc == "x" and not xt_waited:
                                pe.wait_ge(s["xt"], b + 1)
                                xt_waited = True
                            pe.wait_ge(s["job_free"], b * nj + j + 1)
                            o, w, x = jps[:, j % 4, :], W[wn], source(sc)
                            if tile_k:
                                for t in range(NT):
                                    ks = tile_k(t)
                                    for i, (k, rows) in enumerate(ks):
                                        last = nc.tensor.matmul(o[:, t * P:(t + 1) * P], w[0:rows, k, blk * P:(blk + 1) * P],
                                                                x[0:rows, p, k, t * P:(t + 1) * P], start=i == 0, stop=i == len(ks) - 1)
                            else:
                                for k in range(KT):
                                    last = nc.tensor.matmul(o, w[:, k, blk * P:(blk + 1) * P], x[:, p, k, :], start=k == 0, stop=k == KT - 1)
                            last.then_inc(s["job"], 1)
                        if vsrc == "x" and not xt_waited:
                            pe.wait_ge(s["xt"], b + 1)
                        for v in range(NVB):
                            pe.wait_ge(s["v_free"], b * NVB + v + 1)
                            for t in range(v * VT, (v + 1) * VT):
                                o = vps[:, v % 2, (t % VT) * VW:(t % VT + 1) * VW]
                                ks = tile_k(t) if tile_k else [(k, P) for k in range(KT)]
                                for i, (k, rows) in enumerate(ks):
                                    last = nc.tensor.matmul(o, source(vsrc)[0:rows, p, k, t * P:(t + 1) * P], W[vw][0:rows, k, 0:VW],
                                                            start=i == 0, stop=i == len(ks) - 1 and vb is None)
                                if vb:
                                    last = nc.tensor.matmul(o, G.ones[0:1, :], W[vb][0:1, 0:VW], start=False, stop=True)
                            last.then_inc(s["v"], 1)
                        pe.wait_ge(s["v"], (b + 1) * NVB)
                        pe.sem_inc(s["xt_free"], 1)
                        pe.sem_inc(s["c_free"], 1)


def attention(nc, G, name, qs, ks, vs, H, DH, blocks, masks, odst, sums, rel=None):
    NC = max(1, 6 * DH // P + (6 * DH % P > 0)) if DH < 64 else 3
    TPC = 6 // NC
    KR = TPC * DH
    HD, VW = H * DH, DH + 1
    GH = 4
    NG = H // GH
    SCORES, EXPO, TURN = 7, 6, 4
    width = [(blocks(t)[1] - blocks(t)[0]) * P for t in range(NT)]
    OFF = [sum(width[:t]) for t in range(NT)]
    WMAX = max(width)
    users = [[t for t in range(NT) if blocks(t)[0] <= kb < blocks(t)[1]] for kb in range(NT)]
    windowed = WMAX < S
    UW = WMAX if windowed else S
    nload = 13
    with phase(nc, name, "in0 in1 loaded qk_free vh vones rel0 rel1 score least expo turned cp_dve cp_act pv "
               "o_free o_st0 o_st1") as (s, sb, ps):
        Q = sb("Q", [P, 2, NC, H, S], BF16)
        K = sb("K", [P, 2, NC, H, S], BF16)
        V = sb("V", [P, 2, NT, HD])
        Vh = sb("Vh", [P, GH, NT, VW])
        prob = sb("prob", [P, NT, WMAX])
        expT = sb("expT", [P, 2, NT * UW])
        nmax = sb("nmax", [P, 2, NT])
        osb = sb("osb", [VW, GH, S])
        if rel is not None:
            relsb = sb("relsb", [P, 2, sum(width)])
            summed = sb("summed", [P, NT, WMAX])
        sps = ps("sps", [P, NT, S])
        tps = ps("tps", [P, 2, S])
        ops = ps("ops", [VW, 2, S])

        class Unit:

            def __init__(self, p, it, h, j, t, n, pair, first):
                self.p, self.it, self.h, self.slot, self.t, self.n, self.pair, self.first = p, it, h, j % GH, t, n, pair, first

        def walk(eng, step, head):
            def early(m):
                def at(k):
                    h, t = divmod(m + k, NT)
                    return Unit(0, 0, h, h, t, h, h // 2, False) if m + k >= 0 else None
                return at

            def group(p, it, g, final):
                b = it * 2 + p
                for i in range(GH):
                    for t in range(NT):
                        def at(k, i=i, t=t):
                            d, tt = divmod(t + k, NT)
                            j = i + d
                            n, pair = b * H + g * GH + j, b * (H // 2) + g * (GH // 2) + j // 2
                            if final and j >= GH:
                                return Unit(1 - p, it + p, j - GH, j, tt, n, pair, j == GH and tt == 0)
                            return Unit(p, it, g * GH + j, j, tt, n, pair, False)
                        step(at)
                        head(at, t, b * NG + g)

            for m in range(-SCORES, 0):
                step(early(m))
            with eng.Fori(0, NB // 2) as it:
                for p in range(2):
                    with eng.Fori(0, NG - 1) as g:
                        group(p, it, g, False)
                    group(p, it, NG - 1, True)
                    if eng is nc.tensor:
                        eng.wait_ge(s["pv"], (it * 2 + p) * H + H)
                        eng.sem_inc(s["qk_free"], 1)

        def wait(eng, what, n):
            if not (isinstance(n, int) and n <= 0):
                eng.wait_ge(s[what], n)

        def copied(u):
            lo, hi = blocks(u.t)
            src = tps[:, u.t % 2, 0:width[u.t]]
            if windowed:
                c = lo * UW + (u.t - users[lo][0]) * P
                return expT[:, u.slot % 2, c:c + width[u.t]], src
            dst = expT[:, u.slot % 2, :].rearrange("p (k q) -> p k q", q=UW)[:, lo:hi, u.t * P:(u.t + 1) * P]
            return dst, src.rearrange("p (k q) -> p k q", q=P)

        with nc.Block() as block:

            @block.gpsimd
            def _(pool):
                with pool.Fori(0, NB // 2) as it:
                    for p in range(2):
                        b = it * 2 + p
                        pool.wait_ge(s["qk_free"], b + 1)
                        for i, (qp, kp) in enumerate(TERMS):
                            c, r = i // TPC, i % TPC
                            for dst, part, src in ((Q, qp, qs), (K, kp, ks)):
                                pool.dma_start(dst[r * DH:(r + 1) * DH, p, c],
                                               src[part - 1].rearrange("(h d) t -> d h t", d=DH)[:, :, ds(b * S, S)]).then_inc(s[f"in{p}"], 16)
                        pool.dma_start(V[:, p], vs.rearrange("(t p) d -> p t d", p=P)[:, ds(b * NT, NT), :]).then_inc(s[f"in{p}"], 16)
                        pool.wait_ge(s[f"in{p}"], it * (16 * nload) + 16 * nload)
                        pool.sem_inc(s["loaded"], 1)
                pool.wait_ge(s["qk_free"], NB + 1)
                pool.sem_inc(s["loaded"], 1)

            @block.sync
            def _(sp):
                for i in range(2):
                    sp.sem_inc(s[f"o_st{i}"], 32)

                def load(n, slot):
                    if rel is None:
                        return
                    sp.wait_ge(s["least"], n * NT + NT)
                    alone(sp)
                    for t in range(NT):
                        w = width[t]
                        row = rel[t][ds(n, 1), P - 1:]
                        skewed = bass.AP(row.tensor, row.offset, [[w - 1, P], [1, w]])
                        sp.dma_start(relsb[:, slot % 2, OFF[t]:OFF[t] + w], skewed).then_inc(s[f"rel{slot % 2}"], 16)

                def save(b, g, i):
                    sp.wait_ge(s["o_free"], b * H + g * GH + 2 * i + 2 + 2)
                    alone(sp)
                    h = g * GH + 2 * i
                    sp.dma_start(odst.rearrange("(h d) t -> d h t", d=DH)[:, ds(h, 2), ds(b * S, S)], osb[0:DH, 2 * i:2 * i + 2]).then_inc(s[f"o_st{i}"], 16)
                    sp.dma_start(sums.unsqueeze(0)[:, ds(h, 2), ds(b * S, S)], osb[DH:VW, 2 * i:2 * i + 2]).then_inc(s[f"o_st{i}"], 16)

                def group(b, g, final=False):
                    for i in range(GH // 2):
                        for k in range(2):
                            if not final:
                                load(b * H + g * GH + 2 * i + k + GH, k)
                        if final and i == 0 and rel is not None:
                            sp.wait_ge(s["least"], NB * H * NT + 2 * NT)
                            sp.sem_inc(s["rel0"], 16 * NT)
                            sp.sem_inc(s["rel1"], 16 * NT)
                        save(b, g, i)

                for n in range(GH):
                    load(n, n)
                with sp.Fori(0, NB // 2 - 1) as it:
                    for p in range(2):
                        with sp.Fori(0, NG) as g:
                            group(it * 2 + p, g)
                with sp.Fori(0, NG) as g:
                    group(NB - 2, g)
                with sp.Fori(0, NG - 1) as g:
                    group(NB - 1, g)
                group(NB - 1, NG - 1, True)
                for i in range(2):
                    sp.wait_ge(s[f"o_st{i}"], 32 + 32 * NB * NG)

            @block.tensor
            def _(pe):
                pe.sem_inc(s["qk_free"], 2)

                def scores(u):
                    if u.first:
                        pe.wait_ge(s["loaded"], u.it * 2 + u.p + 1)
                    wait(pe, "expo", u.n * NT + u.t - 3)
                    lo, hi = blocks(u.t)
                    o = sps[:, u.t, 0:width[u.t]]
                    for i, (kb, m) in enumerate(masks(u.t)):
                        nc.tensor.matmul(o[:, (kb - lo) * P:(kb - lo + 1) * P], G.identb[:, :], G.masks[:, m, :],
                                         start=i == 0, stop=False, skip_group_check=True)
                    for c in range(NC):
                        last = nc.tensor.matmul(o, Q[0:KR, u.p, c, ds(u.h, 1), u.t * P:(u.t + 1) * P].rearrange("p o t -> p (o t)"),
                                                K[0:KR, u.p, c, ds(u.h, 1), lo * P:hi * P].rearrange("p o t -> p (o t)"),
                                                start=False, stop=c == NC - 1, skip_group_check=True)
                    last.then_inc(s["score"], 1)

                def turn(u):
                    pe.wait_ge(s["expo"], u.n * NT + u.t + 1)
                    wait(pe, "cp_act" if u.t % 2 else "cp_dve", u.n * 2 + u.t // 2)
                    for kb in range(width[u.t] // P):
                        last = nc.tensor.transpose(tps[:, u.t % 2, kb * P:(kb + 1) * P], prob[:, u.t, kb * P:(kb + 1) * P], G.ident[:, :])
                    last.then_inc(s["turned"], 1)

                def step(at):
                    scores(at(SCORES))
                    if at(TURN):
                        turn(at(TURN))

                def head(at, kb, g):
                    u = at(0)
                    if kb == 0:
                        pe.wait_ge(s["cp_dve"], u.n * 2 + 2)
                        pe.wait_ge(s["cp_act"], u.n * 2 + 2)
                        pe.wait_ge(s["vh"], u.n + 1)
                        pe.wait_ge(s["o_free"], u.n + 1)
                        alone(pe)
                    first, end = users[kb][0], users[kb][-1] + 1
                    c = kb * UW + (0 if windowed else first * P)
                    last = nc.tensor.matmul(ops[:, u.slot % 2, first * P:end * P], Vh[:, u.slot, kb, :],
                                            expT[:, u.slot % 2, c:c + (end - first) * P], start=kb == 0, stop=kb == NT - 1, skip_group_check=True)
                    if kb == NT - 1:
                        last.then_inc(s["pv"], 1)

                pe.wait_ge(s["loaded"], 1)
                walk(pe, step, head)

            @block.vector
            def _(dve):
                dve.sem_inc(s["o_free"], 2)
                dve.sem_inc(s["least"], 2 * NT)
                nc.vector.memset(Vh[:, :, :, :], 1.0).then_inc(s["vones"], 1)
                dve.wait_ge(s["vones"], 1)

                def values(p, h, slot):
                    nc.vector.tensor_copy(Vh[:, slot, :, 0:DH], V[:, p, :, ds(h * DH, DH)]).then_inc(s["vh"], 1)

                def step(at):
                    u = at(SCORES)
                    w = width[u.t]
                    if rel is not None and u.t == 0:
                        dve.wait_ge(s[f"rel{u.slot % 2}"], u.pair * (16 * NT) + 16 * NT)
                    dve.wait_ge(s["score"], u.n * NT + u.t + 1)
                    if rel is not None:
                        alone(dve)
                        nc.vector.tensor_tensor_reduce(out=summed[:, u.t, 0:w], in0=sps[:, u.t, 0:w],
                                                       in1=relsb[:, u.slot % 2, OFF[u.t]:OFF[u.t] + w], scale=1.0, scalar=3.0e38,
                                                       op0=ALU.add, op1=ALU.min, accum_out=nmax[:, u.slot % 2, u.t:u.t + 1]).then_inc(s["least"], 1)
                    else:
                        nc.vector.tensor_reduce(nmax[:, u.slot % 2, u.t:u.t + 1], sps[:, u.t, 0:w], AX.X, ALU.max, negate=True).then_inc(s["least"], 1)
                    u = at(TURN)
                    if u and u.t % 2 == 0:
                        dve.wait_ge(s["turned"], u.n * NT + u.t + 1)
                        nc.vector.tensor_copy(*copied(u)).then_inc(s["cp_dve"], 1)

                def head(at, t, g):
                    u = at(0)
                    if t == 0:
                        v = at(NT)
                        if v.first:
                            dve.wait_ge(s["loaded"], v.it * 2 + v.p + 1)
                            alone(dve)
                        values(v.p, v.h, v.slot)
                    if t == NT - 1:
                        if u.slot % 2 == 0:
                            dve.wait_ge(s[f"o_st{u.slot // 2}"], g * 32 + 32)
                        dve.wait_ge(s["pv"], u.n + 1)
                        alone(dve)
                        nc.vector.tensor_copy(osb[:, u.slot, :], ops[:, u.slot % 2, :]).then_inc(s["o_free"], 1)

                dve.wait_ge(s["loaded"], 1)
                values(0, 0, 0)
                walk(dve, step, head)

            @block.scalar
            def _(act):
                def step(at):
                    u = at(EXPO)
                    if u:
                        w = width[u.t]
                        act.wait_ge(s["least"], u.n * NT + u.t + 1 + 2 * NT)
                        source = sps[:, u.t, 0:w] if rel is None else summed[:, u.t, 0:w]
                        nc.scalar.activation(prob[:, u.t, 0:w], source, ACT.Exp, scale=1.0 if rel is None else -1.0,
                                             bias=nmax[:, u.slot % 2, u.t:u.t + 1]).then_inc(s["expo"], 1)
                    u = at(TURN)
                    if u and u.t % 2:
                        act.wait_ge(s["turned"], u.n * NT + u.t + 1)
                        nc.scalar.copy(*copied(u)).then_inc(s["cp_act"], 1)

                walk(act, step, lambda at, t, g: None)


def wide_attention(nc, G, name, qs, ks, vs, H, DH, odst, sums, maskrow=None):
    NC = max(1, -(-6 * DH // P))
    TPC = 6 // NC
    KR = TPC * DH
    KA = KR + (1 if maskrow is not None else 0)
    KB = KR + 4
    HD, VW = H * DH, DH + 1
    GH = 4
    NG = H // GH
    nload = 12 + (1 if maskrow is not None else 0)
    with phase(nc, name, "qk0 qk1 v0 v1 vh qk_free ones vones score maxed split shift_ps shift tscore expo pv "
               "o_free o_st0 o_st1 poolc") as (s, sb, ps):
        Q = sb("Q", [P, 2, NC, H, S], BF16)
        K = sb("K", [P, 2, NC, H, S], BF16)
        V = sb("V", [P, 2, NT, HD])
        Vh = sb("Vh", [P, GH, NT, VW])
        expT = sb("expT", [P, 2, NT, S])
        nmax = sb("nmax", [P, GH, NT])
        r1 = sb("r1", [P, NT])
        r2 = sb("r2", [P, NT])
        mparts = sb("mparts", [P, GH, NT, 4], BF16)
        osb = sb("osb", [VW, 2, H, S])
        aps = ps("aps", [P, 2, S])
        bps = ps("bps", [P, 2, S])
        ops = ps("ops", [VW, 2, S])
        mps = ps("mps", [P, S])

        def wait(eng, what, n):
            if not (isinstance(n, int) and n <= 0):
                eng.wait_ge(s[what], n)

        def place(p, b, g, i, k, final):
            n = b * H + g * GH + i + k
            if final and i + k >= GH:
                return 1 - p, i + k - GH, n
            return p, g * GH + i + k, n

        with nc.Block() as block:

            @block.sync
            def _(sp):
                for p in range(2):
                    sp.sem_inc(s[f"o_st{p}"], 32)

                def load(p, b):
                    for i, (qp, kp) in enumerate(TERMS):
                        c, r = i // TPC, i % TPC
                        for dst, part, src in ((Q, qp, qs), (K, kp, ks)):
                            sp.dma_start(dst[r * DH:(r + 1) * DH, p, c],
                                         src[part - 1].rearrange("(h d) t -> d h t", d=DH)[:, :, ds(b * S, S)]).then_inc(s[f"qk{p}"], 16)
                    if maskrow is not None:
                        sp.dma_start(K[KR:KR + 1, p, 0], maskrow[ds(b, 1), :].unsqueeze(1).broadcast_to([1, H, S])).then_inc(s[f"qk{p}"], 16)
                    sp.dma_start(V[:, p], vs.rearrange("(t p) d -> p t d", p=P)[:, ds(b * NT, NT), :]).then_inc(s[f"v{p}"], 16)

                def save(p, b):
                    sp.wait_ge(s["o_free"], b * H + H + 2)
                    alone(sp)
                    sp.dma_start(odst.rearrange("(h d) t -> d h t", d=DH)[:, :, ds(b * S, S)], osb[0:DH, p]).then_inc(s[f"o_st{p}"], 16)
                    sp.dma_start(sums.unsqueeze(0)[:, :, ds(b * S, S)], osb[DH:VW, p]).then_inc(s[f"o_st{p}"], 16)

                for p in range(2):
                    sp.wait_ge(s["ones"], p + 1)
                    load(p, p)
                with sp.Fori(0, NB // 2 - 1) as it:
                    for p in range(2):
                        b = it * 2 + p
                        sp.wait_ge(s["qk_free"], b + 1)
                        alone(sp)
                        load(p, b + 2)
                        save(p, b)
                save(0, NB - 2)
                sp.sem_inc(s["qk0"], 16 * nload)
                sp.sem_inc(s["v0"], 16)
                save(1, NB - 1)
                for p in range(2):
                    sp.wait_ge(s[f"o_st{p}"], 32 + 32 * NB // 2)

            @block.tensor
            def _(pe):
                def scores(where, slot, t):
                    p, h, n = where
                    wait(pe, "maxed", n * NT + t - 1)
                    for c in range(NC):
                        rows = KA if c == 0 else KR
                        last = nc.tensor.matmul(aps[:, t % 2, :], Q[0:rows, p, c, ds(h, 1), t * P:(t + 1) * P].rearrange("p o t -> p (o t)"),
                                                K[0:rows, p, c, ds(h, 1), :].rearrange("p o t -> p (o t)"),
                                                start=c == 0, stop=c == NC - 1)
                    last.then_inc(s["score"], 1)

                def shift(where, slot):
                    p, h, n = where
                    pe.wait_ge(s["split"], n + 1)
                    wait(pe, "shift", n)
                    for t in range(NT):
                        last = nc.tensor.matmul(mps[0:4, t * P:(t + 1) * P], mparts[:, slot, t, :], G.identb[:, :], start=True, stop=True)
                    last.then_inc(s["shift_ps"], 1)

                def turned_scores(where, slot, kb):
                    p, h, n = where
                    if kb == 0:
                        pe.wait_ge(s["shift"], n + 1)
                    wait(pe, "expo", n * NT + kb - 1)
                    for c in range(NC):
                        rows = KB if c == 0 else KR
                        last = nc.tensor.matmul(bps[:, kb % 2, :], K[0:rows, p, c, ds(h, 1), kb * P:(kb + 1) * P].rearrange("p o t -> p (o t)"),
                                                Q[0:rows, p, c, ds(h, 1), :].rearrange("p o t -> p (o t)"),
                                                start=c == 0, stop=c == NC - 1)
                    last.then_inc(s["tscore"], 1)

                def weigh(where, slot, kb):
                    if kb == 0:
                        pe.wait_ge(s["vh"], where[2] + 1)
                        pe.wait_ge(s["o_free"], where[2] + 1)
                    pe.wait_ge(s["expo"], where[2] * NT + kb + 1)
                    alone(pe)
                    last = nc.tensor.matmul(ops[:, slot % 2, :], Vh[:, slot, kb, :], expT[:, slot % 2, kb, :],
                                            start=kb == 0, stop=kb == NT - 1)
                    if kb == NT - 1:
                        last.then_inc(s["pv"], 1)

                def group(p, b, g, final):
                    for i in range(GH):
                        now, one, two, three = (place(p, b, g, i, k, final) for k in range(4))
                        if final and i == 1:
                            it = half[0]
                            pe.wait_ge(s[f"qk{1 - p}"], it * (16 * nload) + 16 * nload * (1 + p))
                        for t in range(NT):
                            scores(three, (i + 3) % GH, t)
                            turned_scores(one, (i + 1) % GH, t)
                            if t == 1:
                                shift(two, (i + 2) % GH)
                            weigh(now, i, t)

                half = [None]
                pe.wait_ge(s["qk0"], 16 * nload)
                for k, slot in ((0, 0), (1, 1)):
                    for t in range(NT):
                        scores((0, k, k), slot, t)
                shift((0, 0, 0), 0)
                for t in range(NT):
                    turned_scores((0, 0, 0), 0, t)
                for t in range(NT):
                    scores((0, 2, 2), 2, t)
                shift((0, 1, 1), 1)
                with pe.Fori(0, NB // 2) as it:
                    half[0] = it
                    for p in range(2):
                        b = it * 2 + p
                        with pe.Fori(0, NG - 1) as g:
                            group(p, b, g, False)
                        group(p, b, NG - 1, True)
                        pe.wait_ge(s["pv"], b * H + H)
                        pe.sem_inc(s["qk_free"], 1)

            @block.vector
            def _(dve):
                nc.vector.memset(mparts[:, :, :, :], 0.0 if maskrow is None else 1.0)
                for p in range(2):
                    if maskrow is not None:
                        nc.vector.memset(Q[KR:KR + 1, p, 0], 1.0)
                    nc.vector.memset(K[KR:KB, p, 0], 1.0).then_inc(s["ones"], 1)
                dve.sem_inc(s["o_free"], 2)

                def maxima(where, slot):
                    for t in range(NT):
                        dve.wait_ge(s["score"], where[2] * NT + t + 1)
                        nc.vector.tensor_reduce(nmax[:, slot, t:t + 1], aps[:, t % 2, :], AX.X, ALU.max, negate=True).then_inc(s["maxed"], 1)

                def group(p, b, g, final):
                    for i in range(GH):
                        maxima(place(p, b, g, i, 3, final), (i + 3) % GH)
                        n = b * H + g * GH + i
                        dve.wait_ge(s["pv"], n + 1)
                        alone(dve)
                        nc.vector.tensor_copy(osb[:, p, ds(g * GH + i, 1), :].rearrange("d o t -> d (o t)"),
                                              ops[:, i % 2, :]).then_inc(s["o_free"], 1)

                for k in range(3):
                    maxima((0, k, k), k)
                with dve.Fori(0, NB // 2) as it:
                    for p in range(2):
                        b = it * 2 + p
                        dve.wait_ge(s[f"o_st{p}"], it * 32 + 32)
                        alone(dve)
                        with dve.Fori(0, NG - 1) as g:
                            group(p, b, g, False)
                        group(p, b, NG - 1, True)

            @block.gpsimd
            def _(pool):
                ch = Chain(pool, s["poolc"])

                def values(where, slot):
                    p, h, n = where
                    nc.gpsimd.tensor_copy(Vh[:, slot, :, 0:DH], V[:, p, :, ds(h * DH, DH)]).then_inc(s["vh"], 1)

                def split(where, slot):
                    n = where[2]
                    pool.wait_ge(s["maxed"], n * NT + NT)
                    alone(pool)
                    ch.at(n * 4)
                    ch.link(nc.gpsimd.tensor_copy(mparts[:, slot, :, 1], nmax[:, slot, :]))
                    ch.link(nc.gpsimd.tensor_tensor(r1[:, :], nmax[:, slot, :], mparts[:, slot, :, 1], ALU.subtract))
                    alone(pool)
                    ch.link(nc.gpsimd.tensor_copy(mparts[:, slot, :, 2], r1[:, :]))
                    ch.link(nc.gpsimd.tensor_tensor(r2[:, :], r1[:, :], mparts[:, slot, :, 2], ALU.subtract))
                    alone(pool)
                    nc.gpsimd.tensor_copy(mparts[:, slot, :, 3], r2[:, :]).then_inc(s["split"], 1)

                nc.gpsimd.memset(Vh[:, :, :, :], 1.0).then_inc(s["vones"], 1)
                pool.wait_ge(s["ones"], 1)
                pool.wait_ge(s["vones"], 1)
                pool.wait_ge(s["v0"], 16)
                for k in range(2):
                    split((0, k, k), k)
                    values((0, k, k), k)
                with pool.Fori(0, NB // 2) as it:
                    for p in range(2):
                        b = it * 2 + p
                        with pool.Fori(0, NG - 1) as g:
                            for i in range(GH):
                                two = place(p, b, g, i, 2, False)
                                split(two, (i + 2) % GH)
                                values(two, (i + 2) % GH)
                        for i in range(GH):
                            two = place(p, b, NG - 1, i, 2, True)
                            split(two, (i + 2) % GH)
                            if i == 2:
                                pool.wait_ge(s[f"v{1 - p}"], it * 16 + 16 * (1 + p))
                                alone(pool)
                            values(two, (i + 2) % GH)

            @block.scalar
            def _(act):
                def shift(where, slot):
                    p, h, n = where
                    act.wait_ge(s["shift_ps"], n + 1)
                    nc.scalar.copy(Q[KR:KB, p, 0, ds(h, 1), :].rearrange("p o t -> p (o t)"), mps[0:4, :]).then_inc(s["shift"], 1)

                def exponentials(where, slot, kb):
                    act.wait_ge(s["tscore"], where[2] * NT + kb + 1)
                    nc.scalar.activation(expT[:, slot % 2, kb, :], bps[:, kb % 2, :], ACT.Exp).then_inc(s["expo"], 1)

                def group(p, b, g, final):
                    for i in range(GH):
                        one, two = (place(p, b, g, i, k, final) for k in (1, 2))
                        for kb in range(NT):
                            exponentials(one, (i + 1) % GH, kb)
                            if kb == 1:
                                shift(two, (i + 2) % GH)

                shift((0, 0, 0), 0)
                for kb in range(NT):
                    exponentials((0, 0, 0), 0, kb)
                shift((0, 1, 1), 1)
                with act.Fori(0, NB // 2) as it:
                    for p in range(2):
                        b = it * 2 + p
                        with act.Fori(0, NG - 1) as g:
                            group(p, b, g, False)
                        group(p, b, NG - 1, True)


def rel_scores(nc, G, name, qs, er, rel):
    H, DH = 16, 16
    KR = 6 * DH
    with phase(nc, name, "er cast erp q0 q1 q_free mm mm_free_a mm_free_v cp_a cp_v st0 st1 dvc") as (s, sb, ps):
        er32 = sb("er32", [KR, S])
        erk = sb("erk", [KR, S], BF16)
        r1 = sb("r1", [KR, S])
        pbf = sb("pbf", [DH, 3, S], BF16)
        Q = sb("Q", [KR, 2, H, S], BF16)
        out = sb("out", [P, 2, 10 * P])
        o = ps("o", [P, 8, S])
        OFF = [0, P, 3 * P, 6 * P]

        with nc.Block() as block:

            @block.gpsimd
            def _(pool):
                pool.dma_start(er32[0:DH, :], er).then_inc(s["er"], 16)
                pool.wait_ge(s["cast"], 1)
                for i, (qp, kp) in enumerate(TERMS):
                    pool.dma_start(erk[i * DH:(i + 1) * DH, :], pbf[:, kp - 1, :]).then_inc(s["erp"], 16)
                with pool.Fori(0, NB // 2) as it:
                    for p in range(2):
                        b = it * 2 + p
                        pool.wait_ge(s["q_free"], b + 1)
                        for i, (qp, kp) in enumerate(TERMS):
                            pool.dma_start(Q[i * DH:(i + 1) * DH, p],
                                           qs[qp - 1].rearrange("(h d) t -> d h t", d=DH)[:, :, ds(b * S, S)]).then_inc(s[f"q{p}"], 16)

            @block.sync
            def _(sp):
                for hp in range(2):
                    sp.sem_inc(s[f"st{hp}"], 16 * NT)
                with sp.Fori(0, NB * H // 2) as i:
                    for hp in range(2):
                        n = i * 2 + hp
                        sp.wait_ge(s["cp_a"], n * 2 + 2)
                        sp.wait_ge(s["cp_v"], n * 2 + 2)
                        alone(sp)
                        for t in range(NT):
                            w = (t + 1) * P
                            sp.dma_start(rel[t][ds(n, 1), :].rearrange("o (p c) -> (o p) c", c=w),
                                         out[:, hp, OFF[t]:OFF[t] + w]).then_inc(s[f"st{hp}"], 16)
                for hp in range(2):
                    sp.wait_ge(s[f"st{hp}"], 16 * NT + 16 * NT * NB * H // 2)

            @block.tensor
            def _(pe):
                pe.sem_inc(s["q_free"], 2)
                pe.wait_ge(s["erp"], 96)
                with pe.Fori(0, NB // 2) as it:
                    for p in range(2):
                        b = it * 2 + p
                        pe.wait_ge(s[f"q{p}"], it * 96 + 96)
                        alone(pe)
                        with pe.Fori(0, H // 2) as hh:
                            for hp in range(2):
                                n = b * H + hh * 2 + hp
                                pe.wait_ge(s["mm_free_a"], n + 1)
                                pe.wait_ge(s["mm_free_v"], n + 1)
                                for t in range(NT):
                                    w = (t + 1) * P
                                    last = nc.tensor.matmul(o[:, hp * NT + t, 0:w], Q[:, p, ds(hh * 2 + hp, 1), t * P:(t + 1) * P].rearrange("p o t -> p (o t)"),
                                                            erk[:, S - w:S], start=True, stop=True)
                                last.then_inc(s["mm"], 1)
                        pe.wait_ge(s["mm"], (b + 1) * H)
                        pe.sem_inc(s["q_free"], 1)

            @block.vector
            def _(dve):
                ch = Chain(dve, s["dvc"])
                dve.wait_ge(s["er"], 16)
                ch.link(nc.vector.tensor_copy(pbf[:, 0, :], er32[0:DH, :]))
                ch.link(nc.vector.tensor_tensor(r1[0:DH, :], er32[0:DH, :], pbf[:, 0, :], ALU.subtract))
                ch.link(nc.vector.tensor_copy(pbf[:, 1, :], r1[0:DH, :]))
                ch.link(nc.vector.tensor_tensor(r1[0:DH, :], r1[0:DH, :], pbf[:, 1, :], ALU.subtract))
                nc.vector.tensor_copy(pbf[:, 2, :], r1[0:DH, :]).then_inc(s["cast"], 1)
                dve.sem_inc(s["mm_free_v"], 2)
                with dve.Fori(0, NB * H // 2) as i:
                    for hp in range(2):
                        n = i * 2 + hp
                        dve.wait_ge(s["mm"], n + 1)
                        dve.wait_ge(s[f"st{hp}"], i * (16 * NT) + 16 * NT)
                        for t in (0, 3):
                            w = (t + 1) * P
                            nc.vector.tensor_copy(out[:, hp, OFF[t]:OFF[t] + w], o[:, hp * NT + t, 0:w]).then_inc(s["cp_v"], 1)
                        dve.wait_ge(s["cp_v"], n * 2 + 2)
                        dve.sem_inc(s["mm_free_v"], 1)

            @block.scalar
            def _(act):
                act.sem_inc(s["mm_free_a"], 2)
                with act.Fori(0, NB * H // 2) as i:
                    for hp in range(2):
                        n = i * 2 + hp
                        act.wait_ge(s["mm"], n + 1)
                        act.wait_ge(s[f"st{hp}"], i * (16 * NT) + 16 * NT)
                        for t in (1, 2):
                            w = (t + 1) * P
                            nc.scalar.copy(out[:, hp, OFF[t]:OFF[t] + w], o[:, hp * NT + t, 0:w]).then_inc(s["cp_a"], 1)
                        act.wait_ge(s["cp_a"], n * 2 + 2)
                        act.sem_inc(s["mm_free_a"], 1)


def outproj(nc, G, name, src, w, shape, bias, gate, onto, also=None, tile_k=None, sums=None, H=16):
    KO = shape[1]
    turned = sums is not None
    DH = shape[1] * P // H
    with phase(nc, name, "sums rsums rsums_st w o0 o1 o_free xt_ps xt_ps_free xt xt_free y y_free dvc") as (s, sb, ps):
        W = sb("W", shape)
        B = sb("B", [1, D])
        rows = None if turned else sb("rows", [P, 2, NT, KO * P])
        xT = sb("xT", [P, 2, KO, S])
        xps = None if turned else ps("xps", [P, KO, S])
        if turned:
            rs = sb("rs", [P, H * TOK // P])
            R = sb("R", [P, 2, KO, S])
            flat = sums.rearrange("h t -> (h t)").rearrange("(p c) -> p c", p=P)
        yps = ps("yps", [P, 2, S])
        nw = 2 if bias is not None else 1
        with nc.Block() as block:

            @block.sync
            def _(sp):
                sp.dma_start(W[:, :, :], w).then_inc(s["w"], 16)
                if bias is not None:
                    sp.dma_start(B[:, :], bias).then_inc(s["w"], 16)
                if turned:
                    sp.dma_start(rs[:, :], flat).then_inc(s["sums"], 16)
                    sp.wait_ge(s["rsums"], 1)
                    sp.dma_start(flat, rs[:, :]).then_inc(s["rsums_st"], 16)
                    sp.wait_ge(s["rsums_st"], 16)
                with sp.Fori(0, NB // 2) as it:
                    for p in range(2):
                        b = it * 2 + p
                        if turned:
                            sp.wait_ge(s["xt_free"], b + 1)
                            alone(sp)
                            sp.dma_start(xT[:, p], src.rearrange("(k p) t -> p k t", p=P)[:, :, ds(b * S, S)]).then_inc(s[f"o{p}"], 16)
                            for k in range(KO):
                                each = sums[k * P // DH:(k + 1) * P // DH, ds(b * S, S)].unsqueeze(1).broadcast_to([P // DH, DH, S])
                                sp.dma_start(R[:, p, k, :], each).then_inc(s[f"o{p}"], 16)
                            continue
                        sp.wait_ge(s["o_free"], b + 1)
                        alone(sp)
                        sp.dma_start(rows[:, p], src.rearrange("(t p) d -> p t d", p=P)[:, ds(b * NT, NT), :]).then_inc(s[f"o{p}"], 16)

            @block.tensor
            def _(pe):
                pe.sem_inc(s["o_free"], 2)
                pe.sem_inc(s["xt_free"], 2)
                pe.wait_ge(s["w"], 16 * nw)
                with pe.Fori(0, NB // 2) as it:
                    for p in range(2):
                        b = it * 2 + p
                        if turned:
                            pe.wait_ge(s["xt"], b + 1)
                        else:
                            pe.wait_ge(s[f"o{p}"], it * 16 + 16)
                            pe.wait_ge(s["xt_ps_free"], b + 1)
                            for k in range(KO):
                                for t in range(NT):
                                    last = nc.tensor.transpose(xps[:, k, t * P:(t + 1) * P], rows[:, p, t, k * P:(k + 1) * P], G.ident[:, :])
                            last.then_inc(s["xt_ps"], 1)
                            pe.wait_ge(s["xt_ps"], b + 1)
                            pe.sem_inc(s["o_free"], 1)
                            pe.wait_ge(s["xt"], b + 1)
                        for v in range(2):
                            pe.wait_ge(s["y_free"], b * 2 + v + 1)
                            for t in (2 * v, 2 * v + 1):
                                ks = tile_k(t) if tile_k else [(k, P) for k in range(KO)]
                                m = min(D, sum(r for _, r in ks)) if tile_k else D
                                o = yps[:, v, (t % 2) * D:(t % 2) * D + m]
                                for i, (k, r) in enumerate(ks):
                                    last = nc.tensor.matmul(o, xT[0:r, p, k, t * P:(t + 1) * P], W[0:r, k, 0:m],
                                                            start=i == 0, stop=i == len(ks) - 1 and bias is None)
                                if bias is not None:
                                    last = nc.tensor.matmul(o, G.ones[0:1, :], B[0:1, 0:m], start=False, stop=True)
                            last.then_inc(s["y"], 1)
                        pe.wait_ge(s["y"], b * 2 + 2)
                        pe.sem_inc(s["xt_free"], 1)

            @block.scalar
            def _(act):
                if turned:
                    return
                act.sem_inc(s["xt_ps_free"], 1)
                with act.Fori(0, NB // 2) as it:
                    for p in range(2):
                        b = it * 2 + p
                        act.wait_ge(s["xt_ps"], b + 1)
                        act.wait_ge(s["xt_free"], b + 1)
                        for k in range(KO):
                            last = nc.scalar.copy(xT[:, p, k, :], xps[:, k, :])
                        last.then_inc(s["xt"], 1)
                        act.wait_ge(s["xt"], b + 1)
                        act.sem_inc(s["xt_ps_free"], 1)

            @block.vector
            def _(dve):
                ch = Chain(dve, s["dvc"])
                K = 4 if also is not None else 2
                dve.sem_inc(s["y_free"], 2)
                g = 1.0 if gate is None else G.gate[:, gate:gate + 1]
                if turned:
                    dve.wait_ge(s["sums"], 16)
                    nc.vector.reciprocal(rs[:, :], rs[:, :]).then_inc(s["rsums"], 1)
                with dve.Fori(0, NB // 2) as it:
                    for p in range(2):
                        b = it * 2 + p
                        ch.at(b * K)
                        if turned:
                            dve.wait_ge(s[f"o{p}"], it * (16 * (KO + 1)) + 16 * (KO + 1))
                            nc.vector.tensor_tensor(xT[:, p], xT[:, p], R[:, p], ALU.mult).then_inc(s["xt"], 1)
                        for v in range(2):
                            dve.wait_ge(s["y"], b * 2 + v + 1)
                            if tile_k:
                                for t in (2 * v, 2 * v + 1):
                                    m = sum(r for _, r in tile_k(t))
                                    x = onto[:, ds(b * NT + t, 1), 0:m].rearrange("p o d -> p (o d)")
                                    last = nc.vector.scalar_tensor_tensor(x, yps[:, v, (t % 2) * D:(t % 2) * D + m], g, x, ALU.mult, ALU.add)
                            else:
                                x = onto[:, ds(b * NT + 2 * v, 2), :].rearrange("p t d -> p (t d)")
                                last = nc.vector.scalar_tensor_tensor(x, yps[:, v, :], g, x, ALU.mult, ALU.add)
                            ch.link(last)
                            dve.sem_inc(s["y_free"], 1)
                            if also is not None:
                                x = onto[:, ds(b * NT + 2 * v, 2), :].rearrange("p t d -> p (t d)")
                                y = also[:, ds(b * NT + 2 * v, 2), :].rearrange("p t d -> p (t d)")
                                ch.link(nc.vector.scalar_tensor_tensor(x, y, g, x, ALU.mult, ALU.add))
                        ch.done(K)


def normalise(nc, G, name, src, dst, absmax=None):
    with phase(nc, name, "stats rstd dvc poolc") as (s, sb, ps):
        st = sb("st", [P, TT, 6])
        mv = sb("mv", [P, TT, 2])
        rstd = sb("rstd", [P, TT])
        with nc.Block() as block:

            @block.vector
            def _(dve):
                ch = Chain(dve, s["dvc"])
                for t in range(TT):
                    last = nc.vector.bn_stats(st[:, t, :], src[:, t, :])
                ch.link(last)
                for t in range(TT):
                    last = nc.vector.bn_aggr(mv[:, t, :], st[:, t, :])
                last.then_inc(s["stats"], 1)
                dve.wait_ge(s["rstd"], 1)
                for t in range(TT):
                    last = nc.vector.tensor_scalar(dst[:, t, :], src[:, t, :], mv[:, t, 0:1], rstd[:, t:t + 1], ALU.subtract, ALU.mult)
                if absmax is not None:
                    ch.link(last)
                    nc.vector.tensor_reduce(absmax, dst, AX.X, ALU.max, apply_absolute_value=True)

            @block.gpsimd
            def _(pool):
                ch = Chain(pool, s["poolc"])
                pool.wait_ge(s["stats"], 1)
                ch.link(nc.gpsimd.tensor_scalar(rstd[:, :], mv[:, :, 1], LN_EPS, None, ALU.add))
                nc.gpsimd.tensor_tensor(rstd[:, :], rstd[:, :], G.mhalf[:, 0:TT], ALU.pow).then_inc(s["rstd"], 1)


def key_mask(nc, G, name, mask, dst):
    with phase(nc, name, "in cast out dvc") as (s, sb, ps):
        m = sb("m", [NB, S], mybir.dt.int32)
        f = sb("f", [NB, S])
        o = sb("o", [NB, S], BF16)
        with nc.Block() as block:

            @block.sync
            def _(sp):
                sp.dma_start(m[:, :], mask).then_inc(s["in"], 16)
                sp.wait_ge(s["cast"], 1)
                sp.dma_start(dst, o[:, :]).then_inc(s["out"], 16)
                sp.wait_ge(s["out"], 16)

            @block.vector
            def _(dve):
                dve.wait_ge(s["in"], 16)
                nc.vector.tensor_copy(f[:, :], m[:, :]).then_inc(s["dvc"], 1)
                dve.wait_ge(s["dvc"], 1)
                nc.vector.tensor_scalar(o[:, :], f[:, :], 0.0, -BIG, ALU.is_equal, ALU.mult).then_inc(s["cast"], 1)


MAGIC = 12582912.0


def turn(nc, G, name, src, dst, quant=None):
    with phase(nc, name, "ready turned copied dvc") as (s, sb, ps):
        rows = sb("rows", [P, 2, NT, D])
        xps = ps("xps", [P, 2, KT, S])
        with nc.Block() as block:

            @block.vector
            def _(dve):
                ch = Chain(dve, s["dvc"])
                with dve.Fori(0, NB // 2) as it:
                    for p in range(2):
                        b = it * 2 + p
                        ch.at(b)
                        x = src[:, ds(b * NT, NT), :]
                        dve.wait_ge(s["turned"], b + 1)
                        if quant is not None:
                            ch.link(nc.vector.tensor_scalar(rows[:, p], x, G.quant[:, quant, 1:2], MAGIC, ALU.mult, ALU.add))
                            nc.vector.tensor_scalar(rows[:, p], rows[:, p], MAGIC, G.quant[:, quant, 0:1], ALU.subtract, ALU.mult).then_inc(s["ready"], 1)
                        else:
                            ch.mark(nc.vector.tensor_copy(rows[:, p], x))
                            ch.wait()
                            dve.sem_inc(s["ready"], 1)

            @block.tensor
            def _(pe):
                pe.sem_inc(s["turned"], 2)
                with pe.Fori(0, NB // 2) as it:
                    for p in range(2):
                        b = it * 2 + p
                        pe.wait_ge(s["ready"], b + 1)
                        pe.wait_ge(s["copied"], b + 1)
                        for k in range(KT):
                            for t in range(NT):
                                last = nc.tensor.transpose(xps[:, p, k, t * P:(t + 1) * P], rows[:, p, t, k * P:(k + 1) * P], G.ident[:, :])
                        last.then_inc(s["turned"], 1)

            @block.scalar
            def _(act):
                act.sem_inc(s["copied"], 2)
                with act.Fori(0, NB // 2) as it:
                    for p in range(2):
                        b = it * 2 + p
                        act.wait_ge(s["turned"], b + 3)
                        for k in range(KT):
                            last = nc.scalar.copy(dst[:, k, ds(b * S, S)], xps[:, p, k, :])
                        last.then_inc(s["copied"], 1)


def grid(nc, G, name, maxima, what):
    with phase(nc, name, "mx all dvc") as (s, sb, ps):
        m = sb("m", [P, len(maxima)])
        g = sb("g", [P, len(maxima)])
        with nc.Block() as block:

            @block.vector
            def _(dve):
                ch = Chain(dve, s["dvc"])
                for i, x in enumerate(maxima):
                    last = nc.vector.tensor_reduce(m[:, i:i + 1], x, AX.X, ALU.max)
                last.then_inc(s["mx"], 1)
                dve.wait_ge(s["all"], 1)
                for i, q in enumerate(what):
                    ch.link(nc.vector.tensor_scalar(G.quant[:, q, 0:1], g[:, i:i + 1], 1.0 / 32767.0, 1e-12, ALU.mult, ALU.max))
                    nc.vector.reciprocal(G.quant[:, q, 1:2], G.quant[:, q, 0:1])

            @block.gpsimd
            def _(pool):
                pool.wait_ge(s["mx"], 1)
                nc.gpsimd.partition_all_reduce(g[:, :], m[:, :], P, bass.bass_isa.ReduceOp.max).then_inc(s["all"], 1)


def dequantise(nc, G, name, wg, wu, wd, gT, uT, dT):
    with phase(nc, name, "w ready turned copied dvc") as (s, sb, ps):
        NBK = 48
        raw = sb("raw", [P, 3, NBK, 32])
        amax = sb("amax", [P, 3, NBK])
        sc = sb("sc", [P, 3, NBK])
        inv = sb("inv", [P, 3, NBK])
        wps = ps("wps", [P, 2, S])
        with nc.Block() as block:

            @block.sync
            def _(sp):
                for i, (w, n) in enumerate(((wg, 8), (wu, 8), (wd, 24))):
                    sp.dma_start(raw[:, i].rearrange("p (o n) k -> p o (n k)", n=n), w.rearrange("(o p) i -> p o i", p=P)).then_inc(s["w"], 16)

            @block.vector
            def _(dve):
                ch = Chain(dve, s["dvc"])
                dve.wait_ge(s["w"], 48)
                flat = raw[:, :].rearrange("p w n k -> p (w n) k")
                a2, s2, i2 = (x[:, :].rearrange("p w n -> p (w n)") for x in (amax, sc, inv))
                ch.link(nc.vector.tensor_reduce(a2, flat, AX.X, ALU.max, apply_absolute_value=True))
                ch.link(nc.vector.tensor_scalar(s2, a2, 1.0 / 7.0, 1e-12, ALU.mult, ALU.max))
                ch.link(nc.vector.reciprocal(i2, s2))
                ch.link(nc.vector.tensor_tensor(flat, flat, i2.unsqueeze(2).broadcast_to([P, 3 * NBK, 32]), ALU.mult))
                ch.link(nc.vector.tensor_scalar(flat, flat, MAGIC, None, ALU.add))
                ch.link(nc.vector.tensor_scalar(flat, flat, MAGIC, None, ALU.subtract))
                ch.link(nc.vector.tensor_tensor(flat, flat, s2.unsqueeze(2).broadcast_to([P, 3 * NBK, 32]), ALU.mult))
                dve.sem_inc(s["ready"], 1)

            def turns():
                for i, dst in ((0, gT), (1, uT)):
                    v = raw[:, i].rearrange("p (o n) k -> p o (n k)", n=8)
                    for o in range(6):
                        for k in range(2):
                            yield v[:, o, k * P:(k + 1) * P], dst[:, k, o * P:(o + 1) * P]
                v = raw[:, 2].rearrange("p (o n) k -> p o (n k)", n=24)
                for o in range(2):
                    for k in range(6):
                        yield v[:, o, k * P:(k + 1) * P], dT[:, k, o * P:(o + 1) * P]

            @block.tensor
            def _(pe):
                pe.wait_ge(s["ready"], 1)
                for n, (src, dst) in enumerate(turns()):
                    if n >= 2:
                        pe.wait_ge(s["copied"], n - 1)
                    nc.tensor.transpose(wps[:, n % 2, 0:P], src, G.ident[:, :]).then_inc(s["turned"], 1)

            @block.scalar
            def _(act):
                for n, (src, dst) in enumerate(turns()):
                    act.wait_ge(s["turned"], n + 1)
                    nc.scalar.copy(dst, wps[:, n % 2, 0:P]).then_inc(s["copied"], 1)


def quantised_ffn(nc, G, a):
    FT = 6
    TOKS = NB * S
    with ExitStack() as ctx:
        def sb(name, shape, dt=F32):
            return ctx.enter_context(nc.sbuf_tensor(name, shape, dt))

        G.quant = sb("quant", [P, 5, 2])
        gT = sb("gateT", [P, KT, FT * P])
        uT = sb("upT", [P, KT, FT * P])
        dT = sb("downT", [P, FT, D])
        mx = sb("mx", [P, 4, NB * FT])
        xT = sb("gridT", [P, KT, TOKS])
        act_ = sb("hidden", [P, FT, TOKS])
        Y = act_[:, 0:2, :].rearrange("p a (t d) -> p (a t) d", d=D)
        dequantise(nc, G, "f1w", a["L0_ffn_w_gate"], a["L0_ffn_w_up"], a["L0_ffn_w_down"], gT, uT, dT)
        normalise(nc, G, "f1n", G.X, Y, absmax=mx[:, 0, 0:TT])
        grid(nc, G, "f1g", [mx[:, 0, 0:TT]], [0])
        turn(nc, G, "f1t", Y, xT, quant=0)

        with phase(nc, "f1a", "g u g_cp u_mx") as (s, psb, ps):
            gps = ps("gps", [P, 4, S])
            ups = ps("ups", [P, 4, S])
            with nc.Block() as block:

                @block.tensor
                def _(pe):
                    with pe.Fori(0, NB) as b:
                        for m in range(FT):
                            n = b * FT + m
                            pe.wait_ge(s["g_cp"], n + 1)
                            for k in range(KT):
                                last = nc.tensor.matmul(gps[:, m % 2, :], gT[:, k, m * P:(m + 1) * P], xT[:, k, ds(b * S, S)], start=k == 0, stop=k == 1)
                            last.then_inc(s["g"], 1)
                            pe.wait_ge(s["u_mx"], n + 1)
                            for k in range(KT):
                                last = nc.tensor.matmul(ups[:, m % 2, :], uT[:, k, m * P:(m + 1) * P], xT[:, k, ds(b * S, S)], start=k == 0, stop=k == 1)
                            last.then_inc(s["u"], 1)

                @block.scalar
                def _(act):
                    act.sem_inc(s["g_cp"], 2)
                    with act.Fori(0, NB) as b:
                        for m in range(FT):
                            act.wait_ge(s["g"], b * FT + m + 1)
                            nc.scalar.copy(act_[:, m, ds(b * S, S)], gps[:, m % 2, :]).then_inc(s["g_cp"], 1)

                @block.vector
                def _(dve):
                    dve.sem_inc(s["u_mx"], 2)
                    with dve.Fori(0, NB) as b:
                        for m in range(FT):
                            dve.wait_ge(s["u"], b * FT + m + 1)
                            nc.vector.tensor_reduce(mx[:, 1, ds(b * FT + m, 1)], ups[:, m % 2, :], AX.X, ALU.max, apply_absolute_value=True).then_inc(s["u_mx"], 1)
                        dve.wait_ge(s["g_cp"], b * FT + FT + 2)
                        alone(dve)
                        nc.vector.tensor_reduce(mx[:, 2, ds(b, 1)], act_[:, :, ds(b * S, S)], AX.XY, ALU.max, apply_absolute_value=True)

        grid(nc, G, "f1h", [mx[:, 1, :], mx[:, 2, 0:NB]], [1, 2])

        with phase(nc, "f1b", "set pre r sig sig_free dvc") as (s, psb, ps):
            sg = psb("sg", [P, 2, FT, S // 2])
            magic = psb("magic", [P, 1])
            with nc.Block() as block:
                W2 = S // 2
                N2 = NB * 2

                @block.vector
                def _(dve):
                    ch = Chain(dve, s["dvc"])

                    def first(i, c):
                        x = act_[:, :, ds(i * (2 * W2) + c * W2, W2)]
                        dve.wait_ge(s["pre"], i * 2 + c + 1)
                        nc.vector.tensor_scalar(x, x, MAGIC, G.quant[:, 2, 0:1], ALU.subtract, ALU.mult).then_inc(s["r"], 1)

                    def second(i, c):
                        x = act_[:, :, ds(i * (2 * W2) + c * W2, W2)]
                        y = sg[:, c, :, :]
                        dve.wait_ge(s["sig"], i * 2 + c + 1)
                        ch.link(nc.vector.tensor_scalar(y, y, 65536.0, MAGIC, ALU.mult, ALU.add))
                        ch.link(nc.vector.tensor_scalar(y, y, MAGIC, 65535.0, ALU.subtract, ALU.min))
                        ch.link(nc.vector.scalar_tensor_tensor(x, y, 1.0 / 65536.0, x, ALU.mult, ALU.mult))
                        ch.link(nc.vector.tensor_reduce(mx[:, 3, ds(i * 2 + c, 1)], x, AX.XY, ALU.max, apply_absolute_value=True))
                        dve.sem_inc(s["sig_free"], 1)

                    nc.vector.memset(magic[:, :], MAGIC).then_inc(s["set"], 1)
                    dve.sem_inc(s["sig_free"], 2)
                    with dve.Fori(0, NB) as i:
                        ch.at(i * 8)
                        first(i, 0)
                        first(i, 1)
                        second(i, 0)
                        second(i, 1)
                        ch.done(8)

                @block.scalar
                def _(act):
                    act.wait_ge(s["set"], 1)
                    with act.Fori(0, NB) as i:
                        for c in range(2):
                            x = act_[:, :, ds(i * (2 * W2) + c * W2, W2)]
                            nc.scalar.activation(x, x, ACT.Identity, scale=G.quant[:, 2, 1:2], bias=magic[:, 0:1]).then_inc(s["pre"], 1)
                        for c in range(2):
                            act.wait_ge(s["r"], i * 2 + c + 1)
                            act.wait_ge(s["sig_free"], i * 2 + c + 1)
                            alone(act)
                            nc.scalar.activation(sg[:, c, :, :], act_[:, :, ds(i * (2 * W2) + c * W2, W2)], ACT.Sigmoid).then_inc(s["sig"], 1)

        grid(nc, G, "f1i", [mx[:, 3, 0:2 * NB]], [3])

        with phase(nc, "f1c", "u u_cp up up_free pre dvc actc") as (s, psb, ps):
            up = psb("up", [P, FT, S])
            magic = psb("magic", [P, 1])
            ups = ps("ups", [P, 4, S])
            with nc.Block() as block:

                @block.tensor
                def _(pe):
                    with pe.Fori(0, NB) as b:
                        for m in range(FT):
                            pe.wait_ge(s["u_cp"], b * FT + m + 1)
                            for k in range(KT):
                                last = nc.tensor.matmul(ups[:, m % 2, :], uT[:, k, m * P:(m + 1) * P], xT[:, k, ds(b * S, S)], start=k == 0, stop=k == 1)
                            last.then_inc(s["u"], 1)

                @block.scalar
                def _(act):
                    act.sem_inc(s["u_cp"], 2)
                    act.wait_ge(s["actc"], 1)
                    with act.Fori(0, NB) as b:
                        x = act_[:, :, ds(b * S, S)]
                        nc.scalar.activation(x, x, ACT.Identity, scale=G.quant[:, 3, 1:2], bias=magic[:, 0:1]).then_inc(s["pre"], 1)
                        act.wait_ge(s["up_free"], b + 1)
                        for m in range(FT):
                            act.wait_ge(s["u"], b * FT + m + 1)
                            nc.scalar.activation(up[:, m, :], ups[:, m % 2, :], ACT.Identity, scale=G.quant[:, 1, 1:2], bias=magic[:, 0:1]).then_inc(s["u_cp"], 1)

                @block.vector
                def _(dve):
                    ch = Chain(dve, s["dvc"])
                    nc.vector.memset(magic[:, :], MAGIC).then_inc(s["actc"], 1)
                    dve.sem_inc(s["up_free"], 1)
                    with dve.Fori(0, NB) as b:
                        ch.at(b * 4)
                        x = act_[:, :, ds(b * S, S)]
                        dve.wait_ge(s["pre"], b + 1)
                        ch.link(nc.vector.tensor_scalar(x, x, MAGIC, G.quant[:, 3, 0:1], ALU.subtract, ALU.mult))
                        dve.wait_ge(s["u_cp"], b * FT + FT + 2)
                        ch.link(nc.vector.tensor_scalar(up[:, :, :], up[:, :, :], MAGIC, G.quant[:, 1, 0:1], ALU.subtract, ALU.mult))
                        ch.link(nc.vector.tensor_tensor(x, x, up[:, :, :], ALU.mult))
                        dve.sem_inc(s["up_free"], 1)
                        ch.link(nc.vector.tensor_reduce(mx[:, 0, ds(b, 1)], x, AX.XY, ALU.max, apply_absolute_value=True))
                        ch.done(4)

        grid(nc, G, "f1j", [mx[:, 0, 0:NB]], [4])

        with phase(nc, "f1d", "h h_free y y_free dvc") as (s, psb, ps):
            h = psb("h", [P, 2, FT, S // 2])
            yps = ps("yps", [P, 4, S])
            with nc.Block() as block:
                @block.vector
                def _(dve):
                    ch = Chain(dve, s["dvc"])
                    dve.sem_inc(s["y_free"], 2)
                    g = G.gate[:, 4:5]

                    def grid_rows(i, c):
                        x = act_[:, :, ds(i * S + c * (S // 2), S // 2)]
                        dve.wait_ge(s["h_free"], i * 2 + c + 1)
                        ch.link(nc.vector.tensor_scalar(h[:, c], x, G.quant[:, 4, 1:2], MAGIC, ALU.mult, ALU.add))
                        nc.vector.tensor_scalar(h[:, c], h[:, c], MAGIC, G.quant[:, 4, 0:1], ALU.subtract, ALU.mult).then_inc(s["h"], 1)

                    def add(i, c):
                        dve.wait_ge(s["y"], i * 2 + c + 1)
                        x = G.X[:, ds(i * NT + c * 2, 2), :].rearrange("p t d -> p (t d)")
                        ch.link(nc.vector.scalar_tensor_tensor(x, yps[:, c, :], g, x, ALU.mult, ALU.add))
                        dve.sem_inc(s["y_free"], 1)

                    for c in range(2):
                        grid_rows(0, c)
                    with dve.Fori(0, NB - 1) as i:
                        ch.at(i * 4 + 2)
                        for c in range(2):
                            add(i, c)
                            grid_rows(i + 1, c)
                    ch.at(NB * 4 - 2)
                    for c in range(2):
                        add(NB - 1, c)

                @block.tensor
                def _(pe):
                    pe.sem_inc(s["h_free"], 2)
                    with pe.Fori(0, NB) as i:
                        for c in range(2):
                            pe.wait_ge(s["h"], i * 2 + c + 1)
                            pe.wait_ge(s["y_free"], i * 2 + c + 1)
                            for t in range(2):
                                for k in range(FT):
                                    last = nc.tensor.matmul(yps[:, c, t * D:(t + 1) * D], h[:, c, k, t * P:(t + 1) * P], dT[:, k, :], start=k == 0, stop=k == FT - 1)
                            last.then_inc(s["y"], 1)
                            pe.wait_ge(s["y"], i * 2 + c + 1)
                            pe.sem_inc(s["h_free"], 1)


def route(nc, G, name, xT, rw, bias, combT):
    E, GR, EPG, TOPG, TOPK = 16, 4, 4, 2, 4
    QT = TT // 4
    with phase(nc, name, "w lg lg_cp lt sc comb ct ct_cp dvc") as (s, sb, ps):
        RW = sb("RW", [P, KT, E])
        cb = sb("cb", [P, E])
        before = sb("before", [P, E, E])
        lg = sb("lg", [E, 2, S])
        score = sb("score", [P, TT, E])
        biased = sb("biased", [P, TT, E])
        comb = sb("comb", [P, TT, E])
        hi = sb("hi", [P, TT, GR, 2])
        lo = sb("lo", [P, TT, GR, 2])
        gs = sb("gs", [P, TT, GR])
        g2 = sb("g2", [P, TT, GR])
        gt = sb("gt", [P, QT, E, E])
        eq = sb("eq", [P, QT, E, E])
        tot = sb("tot", [P, TT])
        lps = ps("lps", [P, 2, S])
        tps = ps("tps", [P, 2, S])
        cps = ps("cps", [P, 2, S])
        with nc.Block() as block:

            @block.sync
            def _(sp):
                sp.dma_start(RW[:, :, :], rw).then_inc(s["w"], 16)
                sp.dma_start(cb[:, :], bias.unsqueeze(0).broadcast_to([P, E])).then_inc(s["w"], 16)
                sp.dma_start(before[:, :, :].rearrange("p a b -> p (a b)"), G.before.unsqueeze(0).broadcast_to([P, E * E])).then_inc(s["w"], 16)

            @block.tensor
            def _(pe):
                pe.wait_ge(s["w"], 48)
                with pe.Fori(0, NB // 2) as it:
                    for p in range(2):
                        b = it * 2 + p
                        pe.wait_ge(s["lg_cp"], b + 1)
                        for k in range(KT):
                            last = nc.tensor.matmul(lps[0:E, p, :], RW[:, k, :], xT[:, k, ds(b * S, S)], start=k == 0, stop=k == KT - 1)
                        last.then_inc(s["lg"], 1)
                        pe.wait_ge(s["lg_cp"], b + 3)
                        pe.wait_ge(s["sc"], b + 1)
                        alone(pe)
                        for t in range(NT):
                            last = nc.tensor.transpose(tps[:, p, t * E:(t + 1) * E], lg[:, p, t * P:(t + 1) * P], G.ident[0:E, 0:E])
                        last.then_inc(s["lt"], 1)
                pe.wait_ge(s["comb"], 1)
                for b in range(NB):
                    if b >= 2:
                        pe.wait_ge(s["ct_cp"], b - 1)
                    for t in range(NT):
                        last = nc.tensor.transpose(cps[0:E, b % 2, t * P:(t + 1) * P], comb[:, b * NT + t, :], G.ident[:, :])
                    last.then_inc(s["ct"], 1)

            @block.scalar
            def _(act):
                act.sem_inc(s["lg_cp"], 2)
                act.sem_inc(s["sc"], 2)
                with act.Fori(0, NB // 2) as it:
                    for p in range(2):
                        b = it * 2 + p
                        act.wait_ge(s["lg"], b + 1)
                        nc.scalar.copy(lg[:, p, :], lps[0:E, p, :]).then_inc(s["lg_cp"], 1)
                        act.wait_ge(s["lt"], b + 1)
                        nc.scalar.activation(score[:, ds(b * NT, NT), :], tps[:, p, 0:NT * E].rearrange("p (t e) -> p t e", e=E), ACT.Sigmoid).then_inc(s["sc"], 1)
                for b in range(NB):
                    act.wait_ge(s["ct"], b + 1)
                    nc.scalar.copy(combT[:, b * S:(b + 1) * S], cps[0:E, b % 2, :]).then_inc(s["ct_cp"], 1)

            @block.vector
            def _(dve):
                ch = Chain(dve, s["dvc"])
                V = nc.vector
                dve.wait_ge(s["w"], 48)
                dve.wait_ge(s["sc"], NB + 2)
                ch.link(V.tensor_tensor(biased[:, :, :], score[:, :, :], cb[:, :].unsqueeze(1).broadcast_to([P, TT, E]), ALU.add))
                bg = biased[:, :, :].rearrange("p t (g i) -> p (t g) i", i=EPG)
                h, l = (x[:, :, :, :].rearrange("p t g i -> p (t g) i") for x in (hi, lo))
                g, r = (x[:, :, :].rearrange("p t g -> p (t g)").unsqueeze(2) for x in (gs, g2))
                V.tensor_tensor(h, bg[:, :, 0:2], bg[:, :, 2:4], ALU.max)
                ch.link(V.tensor_tensor(l, bg[:, :, 0:2], bg[:, :, 2:4], ALU.min))
                ch.link(V.tensor_tensor(g, h[:, :, 0:1], h[:, :, 1:2], ALU.max))
                ch.link(V.tensor_tensor(r, h[:, :, 0:1], h[:, :, 1:2], ALU.min))
                ch.link(V.tensor_tensor(h[:, :, 0:1], l[:, :, 0:1], l[:, :, 1:2], ALU.max))
                ch.link(V.tensor_tensor(r, r, h[:, :, 0:1], ALU.max))
                ch.link(V.tensor_tensor(gs[:, :, :], gs[:, :, :], g2[:, :, :], ALU.add))

                def rank(x, n, out, limit):
                    T = x.shape[1]
                    gv, ev = (y[:, :, :, :].rearrange("p t a b -> p (t a b)")[:, 0:T * n * n].rearrange("p (t a b) -> p t a b", a=n, b=n) for y in (gt, eq))
                    one, other = x.unsqueeze(3).broadcast_to([P, T, n, n]), x.unsqueeze(2).broadcast_to([P, T, n, n])
                    V.tensor_tensor(gv, other, one, ALU.is_gt)
                    ch.link(V.tensor_tensor(ev, other, one, ALU.is_equal))
                    ch.link(V.tensor_tensor(ev, ev, before[:, 0:n, 0:n].unsqueeze(1).broadcast_to([P, T, n, n]), ALU.mult))
                    ch.link(V.tensor_tensor(gv, gv, ev, ALU.add))
                    ch.link(V.tensor_reduce(out, gv, AX.X, ALU.add))
                    ch.link(V.tensor_scalar(out, out, float(limit) - 0.5, None, ALU.is_lt))

                rank(gs[:, :, :], GR, g2[:, :, :], TOPG)
                each = g2[:, :, :].rearrange("p t g -> p (t g)").unsqueeze(2).broadcast_to([P, TT * GR, EPG])
                ch.link(V.tensor_tensor(bg, bg, each, ALU.mult))
                ch.link(V.tensor_scalar(g2[:, :, :], g2[:, :, :], 1.0, BIG, ALU.subtract, ALU.mult))
                ch.link(V.tensor_tensor(bg, bg, each, ALU.add))
                for q in range(4):
                    rank(biased[:, q * QT:(q + 1) * QT, :], E, comb[:, q * QT:(q + 1) * QT, :], TOPK)
                ch.link(V.tensor_tensor(comb[:, :, :], comb[:, :, :], score[:, :, :], ALU.mult))
                ch.link(V.tensor_reduce(tot[:, :], comb[:, :, :], AX.X, ALU.add))
                ch.link(V.tensor_scalar(tot[:, :], tot[:, :], 1e-20, None, ALU.add))
                ch.link(V.reciprocal(tot[:, :], tot[:, :]))
                V.tensor_tensor(comb[:, :, :], comb[:, :, :], tot[:, :].unsqueeze(2).broadcast_to([P, TT, E]), ALU.mult).then_inc(s["comb"], 1)


def gated_mlp(nc, G, name, front, wg, wu, wd, NF, func, onto, gate, bg=None, bu=None, bd=None, combT=None, routed=0):
    shift = isinstance(front, tuple)
    nw = len(wg) + len(wu) + len(wd) + (4 if bg is not None else 0) + (1 if shift else 0) + (1 if combT is not None else 0)
    with phase(nc, name, "w in0 in1 in_free xn xn_free stats rstd xt_ps xt_ps_free xt xt_free g g_free u u_free c c_free gl gl_free "
               "h h_free y y_free zero dvc poolc") as (s, sb, ps):
        WG = sb("WG", [P, KT, NF * P])
        WU = sb("WU", [P, KT, NF * P])
        WD = sb("WD", [P, NF, D])
        gl = sb("gl", [P, 2, S])
        h = sb("h", [P, NF, S])
        if bg is not None:
            BG = sb("BG", [P, NF])
            BU = sb("BU", [P, NF])
            BD = sb("BD", [1, D])
        if combT is not None:
            sel = sb("sel", [16, 8, P])
        if shift:
            rows = sb("rows", [P, 2, NT, D])
            xn = sb("xn", [P, 2, NT, D])
            xT = sb("xT", [P, KT, S])
            aff = sb("aff", [P, 2, KT])
            st = sb("st", [P, NT, 6])
            mv = sb("mv", [P, NT, 2])
            rstd = sb("rstd", [P, NT])
            xps = ps("xps", [P, KT, S])
        gps = ps("gps", [P, 2, S])
        ups = ps("ups", [P, 2, S])
        if combT is not None:
            cps = ps("cps", [P, 2, S])
        yps = ps("yps", [P, 2, S])
        RK = NF
        g = 1.0 if gate is None else G.gate[:, gate:gate + 1]

        with nc.Block() as block:

            @block.sync
            def _(sp):
                for view, c in wg:
                    sp.dma_start(WG[:, :, c:c + view.shape[2]], view).then_inc(s["w"], 16)
                for view, c in wu:
                    sp.dma_start(WU[:, :, c:c + view.shape[2]], view).then_inc(s["w"], 16)
                for view, c in wd:
                    sp.dma_start(WD[:, c:c + view.shape[1], :], view).then_inc(s["w"], 16)
                if bg is not None:
                    sp.dma_start(BG[:, :], bg).then_inc(s["w"], 16)
                    sp.dma_start(BU[:, :], bu).then_inc(s["w"], 16)
                    sp.dma_start(BD[:, :], bd).then_inc(s["w"], 16)
                    sp.dma_start(aff[:, 0, :], front[2]).then_inc(s["w"], 16)
                if shift:
                    sp.dma_start(aff[:, 1, :], front[3]).then_inc(s["w"], 16)
                if combT is not None:
                    sp.dma_start(sel[:, :, :], G.spread).then_inc(s["w"], 16)
                if shift:
                    sp.wait_ge(s["zero"], 1)
                    with sp.Fori(0, NB // 2) as it:
                        for p in range(2):
                            b = it * 2 + p
                            sp.wait_ge(s["in_free"], b + 1)
                            alone(sp)
                            shifted_rows(sp, front[1], rows[:, p], b, s[f"in{p}"])

            @block.gpsimd
            def _(pool):
                ch = Chain(pool, s["poolc"])
                if shift:
                    for p in range(2):
                        last = nc.gpsimd.memset(rows[0:1, p, 0, D // 2:D], 0.0)
                    last.then_inc(s["zero"], 1)
                    with pool.Fori(0, NB) as b:
                        ch.at(b)
                        pool.wait_ge(s["stats"], b + 1)
                        alone(pool)
                        ch.link(nc.gpsimd.tensor_scalar(rstd[:, :], mv[:, :, 1], LN_EPS, None, ALU.add))
                        nc.gpsimd.tensor_tensor(rstd[:, :], rstd[:, :], G.mhalf[:, 0:NT], ALU.pow).then_inc(s["rstd"], 1)

            @block.tensor
            def _(pe):
                if shift:
                    pe.sem_inc(s["xn_free"], 2)
                    pe.sem_inc(s["xt_free"], 1)
                pe.sem_inc(s["h_free"], 1)
                pe.wait_ge(s["w"], 16 * nw)

                def hidden(b, x):
                    for m in range(NF):
                        n = b * NF + m
                        for w, o, done, free in ((WG, gps, "g", "g_free"), (WU, ups, "u", "u_free")):
                            pe.wait_ge(s[free], n + 1)
                            for k in range(KT):
                                last = nc.tensor.matmul(o[:, m % 2, :], w[:, k, m * P:(m + 1) * P], x(k), start=k == 0, stop=k == KT - 1)
                            last.then_inc(s[done], 1)
                        if combT is not None and m < routed:
                            pe.wait_ge(s["c_free"], b * routed + m + 1)
                            alone(pe)
                            nc.tensor.matmul(cps[:, m % 2, :], sel[:, m, :], combT[:, ds(b * S, S)], start=True, stop=True).then_inc(s["c"], 1)

                def down(b):
                    pe.wait_ge(s["h"], b + 1)
                    for v in range(2):
                        pe.wait_ge(s["y_free"], b * 2 + v + 1)
                        for t in (2 * v, 2 * v + 1):
                            o = yps[:, v, (t % 2) * D:(t % 2 + 1) * D]
                            for k in range(NF):
                                last = nc.tensor.matmul(o, h[:, k, t * P:(t + 1) * P], WD[:, k, :], start=k == 0, stop=k == NF - 1 and bd is None)
                            if bd is not None:
                                last = nc.tensor.matmul(o, G.ones[0:1, :], BD[0:1, :], start=False, stop=True)
                        last.then_inc(s["y"], 1)
                    pe.wait_ge(s["y"], b * 2 + 2)
                    pe.sem_inc(s["h_free"], 1)

                if shift:
                    def turn_rows(b, p):
                        pe.wait_ge(s["xn"], b + 1)
                        pe.wait_ge(s["xt_ps_free"], b + 1)
                        for k in range(KT):
                            for t in range(NT):
                                last = nc.tensor.transpose(xps[:, k, t * P:(t + 1) * P], xn[:, p, t, k * P:(k + 1) * P], G.ident[:, :])
                        last.then_inc(s["xt_ps"], 1)
                        pe.wait_ge(s["xt_ps"], b + 1)
                        pe.sem_inc(s["xn_free"], 1)

                    def sequence(b, p, more):
                        pe.wait_ge(s["xt"], b + 1)
                        hidden(b, lambda k: xT[:, k, :])
                        pe.wait_ge(s["u"], b * NF + NF)
                        pe.sem_inc(s["xt_free"], 1)
                        if more:
                            turn_rows(b + 1, 1 - p)
                        down(b)

                    turn_rows(0, 0)
                    with pe.Fori(0, NB // 2 - 1) as it:
                        for p in range(2):
                            sequence(it * 2 + p, p, True)
                    sequence(NB - 2, 0, True)
                    sequence(NB - 1, 1, False)
                else:
                    with pe.Fori(0, NB) as b:
                        hidden(b, lambda k: front[:, k, ds(b * S, S)])
                        down(b)

            @block.scalar
            def _(act):
                if shift:
                    act.sem_inc(s["xt_ps_free"], 1)
                act.sem_inc(s["g_free"], 2)
                act.wait_ge(s["w"], 16 * nw)
                with act.Fori(0, NB) as b:
                    if shift:
                        act.wait_ge(s["xt_ps"], b + 1)
                        act.wait_ge(s["xt_free"], b + 1)
                        for k in range(KT):
                            last = nc.scalar.activation(xT[:, k, :], xps[:, k, :], ACT.Identity, scale=aff[:, 0, k:k + 1], bias=aff[:, 1, k:k + 1])
                        last.then_inc(s["xt"], 1)
                        act.wait_ge(s["xt"], b + 1)
                        act.sem_inc(s["xt_ps_free"], 1)
                    for m in range(NF):
                        n = b * NF + m
                        act.wait_ge(s["g"], n + 1)
                        act.wait_ge(s["gl_free"], n + 1)
                        nc.scalar.activation(gl[:, m % 2, :], gps[:, m % 2, :], func, bias=BG[:, m:m + 1] if bg is not None else 0.0).then_inc(s["gl"], 1)
                        act.wait_ge(s["gl"], n + 1)
                        act.sem_inc(s["g_free"], 1)

            @block.vector
            def _(dve):
                ch = Chain(dve, s["dvc"])
                dve.sem_inc(s["gl_free"], 2)
                if shift:
                    dve.sem_inc(s["in_free"], 2)
                dve.sem_inc(s["u_free"], 2)
                dve.sem_inc(s["y_free"], 2)
                if combT is not None:
                    dve.sem_inc(s["c_free"], 2)
                dve.wait_ge(s["w"], 16 * nw)
                KCH = NF + (routed if combT is not None else 0) + 2 + (2 if shift else 0)

                def front_rows(b, p, it):
                    dve.wait_ge(s[f"in{p}"], it * 64 + 64)
                    for t in range(NT):
                        last = nc.vector.bn_stats(st[:, t, :], rows[:, p, t, :])
                    ch.link(last)
                    alone(dve)
                    for t in range(NT):
                        last = nc.vector.bn_aggr(mv[:, t, :], st[:, t, :])
                    last.then_inc(s["stats"], 1)
                    dve.wait_ge(s["rstd"], b + 1)
                    dve.wait_ge(s["xn_free"], b + 1)
                    for t in range(NT):
                        last = nc.vector.tensor_scalar(xn[:, p, t, :], rows[:, p, t, :], mv[:, t, 0:1], rstd[:, t:t + 1], ALU.subtract, ALU.mult)
                    ch.link(last)
                    dve.sem_inc(s["xn"], 1)
                    dve.sem_inc(s["in_free"], 1)

                def body(b, following=None):
                    if following:
                        ch.at(b * KCH + 2)
                        front_rows(*following)
                    ch.at(b * KCH + (2 if shift else 0) + (2 if following else 0))
                    dve.wait_ge(s["h_free"], b + 1)
                    for m in range(NF):
                        n = b * NF + m
                        dve.wait_ge(s["gl"], n + 1)
                        dve.wait_ge(s["u"], n + 1)
                        if bu is not None:
                            ins = nc.vector.scalar_tensor_tensor(h[:, m, :], ups[:, m % 2, :], BU[:, m:m + 1], gl[:, m % 2, :], ALU.add, ALU.mult)
                        else:
                            ins = nc.vector.tensor_tensor(h[:, m, :], ups[:, m % 2, :], gl[:, m % 2, :], ALU.mult)
                        ch.link(ins)
                        dve.sem_inc(s["gl_free"], 1)
                        dve.sem_inc(s["u_free"], 1)
                        if combT is not None and m < routed:
                            dve.wait_ge(s["c"], b * routed + m + 1)
                            ch.link(nc.vector.tensor_tensor(h[:, m, :], cps[:, m % 2, :], h[:, m, :], ALU.mult))
                            dve.sem_inc(s["c_free"], 1)
                    dve.sem_inc(s["h"], 1)
                    for v in range(2):
                        dve.wait_ge(s["y"], b * 2 + v + 1)
                        x = onto[:, ds(b * NT + 2 * v, 2), :].rearrange("p t d -> p (t d)")
                        ch.link(nc.vector.scalar_tensor_tensor(x, yps[:, v, :], g, x, ALU.mult, ALU.add))
                        dve.sem_inc(s["y_free"], 1)

                if shift:
                    ch.at(0)
                    front_rows(0, 0, 0)
                    with dve.Fori(0, NB // 2 - 1) as it:
                        for p in range(2):
                            body(it * 2 + p, (it * 2 + p + 1, 1 - p, it + p))
                    body(NB - 2, (NB - 1, 1, NB // 2 - 1))
                    body(NB - 1)
                else:
                    with dve.Fori(0, NB) as b:
                        body(b)


def shifted_rows(eng, src, rows, b, sem):
    H = D // 2
    eng.dma_start(rows[:, :, 0:H], src[:, ds(b * NT, NT), 0:H]).then_inc(sem, 16)
    eng.dma_start(rows[1:P, :, H:D], src[0:P - 1, ds(b * NT, NT), H:D]).then_inc(sem, 16)
    eng.dma_start(rows[0:1, 1:NT // 2 + 1, H:D], src[P - 1:P, ds(b * NT, NT // 2), H:D]).then_inc(sem, 16)
    eng.dma_start(rows[0:1, NT // 2 + 1:NT, H:D], src[P - 1:P, ds(b * NT + NT // 2, NT // 2 - 1), H:D]).then_inc(sem, 16)


def rotary_qkv(nc, G, name, src, wqkv, q_scale, k_scale, qs, ks, vs):
    H, DH = 8, 64
    HD = H * DH
    HW = DH // 2
    NU = 2 * NT
    AHEAD = 3
    ROWS_AT = 3
    with phase(nc, name, "w zero in0 in1 xt_ps xt qk v v_sb v_st0 v_st1 sq ss held rn qn crossed straight rot "
               "tp p1 r1 p2 pp p_st0 p_st1 tab") as (s, sb, ps):
        W = sb("W", [P, KT, 3 * HD])
        rows = sb("rows", [P, 2, NT, D])
        xT = sb("xT", [P, 2, KT, S])
        tab = sb("tab", [P, 4, NT, DH])
        sc = sb("sc", [P, 2, 2, DH])
        sq = sb("sq", [P, 2, HD])
        ss = sb("ss", [P, 2, H])
        rn = sb("rn", [P, 2, H])
        qn = sb("qn", [P, 2, HD])
        straight = sb("straight", [P, HD])
        crossed = sb("crossed", [P, HD])
        rot = sb("rot", [P, 2, HD])
        parts = sb("parts", [P, 2, 2, 3, NT, S], BF16)
        r1 = sb("r1", [P, 2, S])
        vsb = sb("vsb", [P, 2, HD])
        xps = ps("xps", [P, KT, S])
        qps = ps("qps", [P, 2, S])
        vps = ps("vps", [P, 2, S])
        tps = ps("tps", [P, 2, S])

        def steps(eng, step):
            for m in range(-AHEAD, 0):
                step(lambda i, m=m: (0, 0, 0, m + i) if m + i >= 0 else None, None)
            with eng.Fori(0, NB // 2) as it:
                for p in range(2):
                    for u in range(NU):
                        def at(i, p=p, u=u):
                            if u + i < NU:
                                return p, it, it * 2 + p, u + i
                            return 1 - p, it + p, it * 2 + p + 1, u + i - NU
                        step(at, (1 - p, it + p, it * 2 + p + 1) if u == ROWS_AT else None)

        def heads(x):
            return x.rearrange("p (h d) -> p h d", d=DH)

        with nc.Block() as block:

            @block.sync
            def _(sp):
                sp.dma_start(W[:, :, :], w_view(wqkv)).then_inc(s["w"], 16)
                sp.dma_start(tab[:, :, :, :], G.rotary.rearrange("w (t p) d -> p w t d", p=P)).then_inc(s["w"], 16)
                for i, x in enumerate((q_scale, k_scale)):
                    x = x.unsqueeze(0)
                    sp.dma_start(sc[:, i, 0, :], x.broadcast_to([P, DH])).then_inc(s["w"], 16)
                    sp.dma_start(sc[:, i, 1, 0:HW], x[:, HW:DH].broadcast_to([P, HW])).then_inc(s["w"], 16)
                    sp.dma_start(sc[:, i, 1, HW:DH], x[:, 0:HW].broadcast_to([P, HW])).then_inc(s["w"], 16)
                sp.wait_ge(s["zero"], 1)
                for c in ("v_st0", "v_st1", "p_st0", "p_st1"):
                    sp.sem_inc(s[c], 16)

                def save(p, b):
                    for t in range(NT):
                        sp.wait_ge(s["v_sb"], b * NT + t + 1 + 2)
                        alone(sp)
                        sp.dma_start(vs[ds(b * S + t * P, P), :], vsb[:, t % 2, :]).then_inc(s[f"v_st{t % 2}"], 16)
                    sp.wait_ge(s["pp"], b * NU + NU)
                    alone(sp)
                    for i, dst in enumerate((qs, ks)):
                        for j in range(3):
                            sp.dma_start(dst[j].rearrange("(f p) t -> p f t", p=P)[:, :, ds(b * S, S)], parts[:, p, i, j]).then_inc(s[f"p_st{p}"], 16)

                shifted_rows(sp, src, rows[:, 0], 0, s["in0"])
                shifted_rows(sp, src, rows[:, 1], 1, s["in1"])
                with sp.Fori(0, NB // 2 - 1) as it:
                    for p in range(2):
                        b = it * 2 + p
                        save(p, b)
                        sp.wait_ge(s["xt_ps"], b + 1)
                        alone(sp)
                        shifted_rows(sp, src, rows[:, p], b + 2, s[f"in{p}"])
                save(0, NB - 2)
                sp.sem_inc(s["in0"], 64)
                save(1, NB - 1)
                for p in range(2):
                    sp.wait_ge(s[f"v_st{p}"], 16 + 16 * NB * NT // 2)
                    sp.wait_ge(s[f"p_st{p}"], 16 + 16 * NB // 2 * 6)

            @block.tensor
            def _(pe):
                pe.wait_ge(s["w"], 16 * 8)

                def turn_rows(p, it, b):
                    pe.wait_ge(s[f"in{p}"], it * 64 + 64)
                    alone(pe)
                    for k in range(KT):
                        for t in range(NT):
                            last = nc.tensor.transpose(xps[:, k, t * P:(t + 1) * P], rows[:, p, t, k * P:(k + 1) * P], G.ident[:, :])
                    last.then_inc(s["xt_ps"], 1)

                def step(at, following):
                    if at(3):
                        p, it, b, u = at(3)
                        t, i = u // 2, u % 2
                        if u == 0:
                            pe.wait_ge(s["xt"], b + 1)
                        pe.wait_ge(s["qn"], b * NU + u + 1)
                        for k in range(KT):
                            last = nc.tensor.matmul(qps[:, i, :], xT[:, p, k, t * P:(t + 1) * P], W[:, k, i * HD:(i + 1) * HD], start=k == 0, stop=k == KT - 1)
                        last.then_inc(s["qk"], 1)
                        if i:
                            pe.wait_ge(s["v_sb"], b * NT + t + 1)
                            for k in range(KT):
                                last = nc.tensor.matmul(vps[:, t % 2, :], xT[:, p, k, t * P:(t + 1) * P], W[:, k, 2 * HD:3 * HD], start=k == 0, stop=k == KT - 1)
                            last.then_inc(s["v"], 1)
                    if at(1):
                        p, it, b, u = at(1)
                        pe.wait_ge(s["rot"], b * NU + u + 1)
                        pe.wait_ge(s["r1"], b * NU + u + 1)
                        for f in range(NT):
                            last = nc.tensor.transpose(tps[:, u % 2, f * P:(f + 1) * P], rot[:, u % 2, f * P:(f + 1) * P], G.ident[:, :])
                        last.then_inc(s["tp"], 1)
                    if following:
                        turn_rows(*following)

                turn_rows(0, 0, 0)
                steps(pe, step)

            @block.scalar
            def _(act):
                act.sem_inc(s["v_sb"], 2)

                def copy_rows(b, p):
                    act.wait_ge(s["xt_ps"], b + 1)
                    for k in range(KT):
                        last = nc.scalar.copy(xT[:, p, k, :], xps[:, k, :])
                    last.then_inc(s["xt"], 1)

                def step(at, following):
                    if at(0):
                        p, it, b, u = at(0)
                        i, t = u % 2, u // 2
                        act.wait_ge(s["r1"], b * NU + u + 1 + 2)
                        nc.scalar.copy(parts[:, p, i, 1, :, t * P:(t + 1) * P], r1[:, i, :].rearrange("p (f t) -> p f t", t=P)).then_inc(s["p2"], 1)
                    if at(3):
                        p, it, b, u = at(3)
                        i, t = u % 2, u // 2
                        act.wait_ge(s["qk"], b * NU + u + 1)
                        nc.scalar.activation(sq[:, i, :], qps[:, i, :], ACT.Square).then_inc(s["sq"], 1)
                        if i:
                            act.wait_ge(s["v"], b * NT + t + 1)
                            act.wait_ge(s[f"v_st{t % 2}"], b * 32 + (t // 2) * 16 + 16)
                            nc.scalar.copy(vsb[:, t % 2, :], vps[:, t % 2, :]).then_inc(s["v_sb"], 1)
                    if at(1):
                        p, it, b, u = at(1)
                        i, t = u % 2, u // 2
                        if u == 0:
                            act.wait_ge(s[f"p_st{p}"], it * 96 + 16)
                        act.wait_ge(s["tp"], b * NU + u + 1)
                        nc.scalar.copy(parts[:, p, i, 0, :, t * P:(t + 1) * P], tps[:, i, :].rearrange("p (f t) -> p f t", t=P)).then_inc(s["p1"], 1)
                    if following:
                        copy_rows(following[2], following[0])

                copy_rows(0, 0)
                steps(act, step)

            @block.gpsimd
            def _(pool):
                for p in range(2):
                    last = nc.gpsimd.memset(rows[0:1, p, 0, D // 2:D], 0.0)
                last.then_inc(s["zero"], 1)
                pool.wait_ge(s["tab"], 1)

                def step(at, following):
                    if at(2):
                        p, it, b, u = at(2)
                        t, i = u // 2, u % 2
                        pool.wait_ge(s["qn"], b * NU + u + 1 + 2)
                        nc.gpsimd.tensor_tensor(heads(straight[:, :]), heads(qn[:, i, :]),
                                                tab[:, 2 * i, t, :].unsqueeze(1).broadcast_to([P, H, DH]), ALU.mult).then_inc(s["straight"], 1)
                    if at(3):
                        p, it, b, u = at(3)
                        i, n = u % 2, b * NU + u
                        pool.wait_ge(s["ss"], n + 1)
                        alone(pool)
                        nc.gpsimd.tensor_scalar(rn[:, i, :], ss[:, i, :], 1e-24, None, ALU.max).then_inc(s["held"], 1)
                        pool.wait_ge(s["held"], n + 1)
                        nc.gpsimd.tensor_tensor(rn[:, i, :], rn[:, i, :], G.mhalf[:, 0:H], ALU.pow).then_inc(s["rn"], 1)

                steps(pool, step)

            @block.vector
            def _(dve):
                dve.wait_ge(s["w"], 16 * 8)
                for i in range(2):
                    for j in range(2):
                        x = tab[:, 2 * i + j]
                        last = nc.vector.tensor_tensor(x, x, sc[:, i, j, :].unsqueeze(1).broadcast_to([P, NT, DH]), ALU.mult)
                last.then_inc(s["tab"], 1)
                dve.wait_ge(s["tab"], 1)
                dve.sem_inc(s["qn"], 2)
                dve.sem_inc(s["r1"], 2)

                def step(at, following):
                    if at(0):
                        p, it, b, u = at(0)
                        i, t = u % 2, u // 2
                        dve.wait_ge(s["p1"], b * NU + u + 1)
                        nc.vector.tensor_tensor(r1[:, i, :].rearrange("p (f t) -> p f t", t=P), tps[:, i, :].rearrange("p (f t) -> p f t", t=P),
                                                parts[:, p, i, 0, :, t * P:(t + 1) * P], ALU.subtract).then_inc(s["r1"], 1)
                    if at(3):
                        p, it, b, u = at(3)
                        dve.wait_ge(s["sq"], b * NU + u + 1)
                        nc.vector.tensor_reduce(ss[:, u % 2, :], heads(sq[:, u % 2, :]), AX.X, ALU.add).then_inc(s["ss"], 1)
                    if at(2):
                        p, it, b, u = at(2)
                        i = u % 2
                        dve.wait_ge(s["rn"], b * NU + u + 1)
                        nc.vector.tensor_tensor(heads(qn[:, i, :]), heads(qps[:, i, :]),
                                                rn[:, i, :].unsqueeze(2).broadcast_to([P, H, DH]), ALU.mult).then_inc(s["qn"], 1)
                    if at(2):
                        p, it, b, u = at(2)
                        i, t = u % 2, u // 2
                        dve.wait_ge(s["qn"], b * NU + u + 1 + 2)
                        x, y = (z.rearrange("p (h s d) -> p h s d", s=2, d=HW) for z in (qn[:, i, :], crossed[:, :]))
                        for k in range(2):
                            last = nc.vector.tensor_tensor(y[:, :, k, :], x[:, :, 1 - k, :],
                                                           tab[:, 2 * i + 1, t, k * HW:(k + 1) * HW].unsqueeze(1).broadcast_to([P, H, HW]), ALU.mult)
                        last.then_inc(s["crossed"], 1)
                    if at(0):
                        p, it, b, u = at(0)
                        i, t = u % 2, u // 2
                        dve.wait_ge(s["p2"], b * NU + u + 1)
                        nc.vector.tensor_tensor(parts[:, p, i, 2, :, t * P:(t + 1) * P], r1[:, i, :].rearrange("p (f t) -> p f t", t=P),
                                                parts[:, p, i, 1, :, t * P:(t + 1) * P], ALU.subtract).then_inc(s["pp"], 1)
                    if at(2):
                        p, it, b, u = at(2)
                        dve.wait_ge(s["straight"], b * NU + u + 1)
                        dve.wait_ge(s["crossed"], b * NU + u + 1)
                        nc.vector.tensor_tensor(rot[:, u % 2, :], straight[:, :], crossed[:, :], ALU.add).then_inc(s["rot"], 1)

                steps(dve, step)


def add_stream(nc, G, name, gate):
    with phase(nc, name, "done") as (s, sb, ps):
        with nc.Block() as block:

            @block.vector
            def _(dve):
                for c in range(4):
                    x, y = (v[:, c * 8:(c + 1) * 8, :].rearrange("p t d -> p (t d)") for v in (G.X, G.Y))
                    nc.vector.scalar_tensor_tensor(x, y, G.gate[:, gate:gate + 1], x, ALU.mult, ALU.add)


def cell_gates(nc, G, name, xT, a, Mrow, gT, eT):
    H = 8
    NH = NB * H
    with phase(nc, name, "w c0 c1 c_free gi gi_cp gf_cp lay lin ex ln sc m_st tp tp_cp dvc actc") as (s, sb, ps):
        WI = sb("WI", [P, 6, H])
        WF = sb("WF", [P, 6, H])
        bi = sb("bi", [H, 2])
        cT = sb("cT", [P, 2, KT, S])
        raw = sb("raw", [H, 2, TOK])
        ig = sb("ig", [NH, S])
        fg = sb("fg", [NH, S])
        t1 = sb("t1", [NH, S])
        cs = sb("cs", [NH, S])
        one = sb("one", [NH, S])
        M = sb("M", [NH, S])
        ips = ps("ips", [P, 2, S])
        fps = ps("fps", [P, 2, S])
        tps = ps("tps", [P, 2, S])
        with nc.Block() as block:

            @block.sync
            def _(sp):
                sp.dma_start(WI[:, :, :], w_view(a["L2_xattn_igate_w"])).then_inc(s["w"], 16)
                sp.dma_start(WF[:, :, :], w_view(a["L2_xattn_fgate_w"])).then_inc(s["w"], 16)
                sp.dma_start(bi[:, 0:1], a["L2_xattn_igate_b"]).then_inc(s["w"], 16)
                sp.dma_start(bi[:, 1:2], a["L2_xattn_fgate_b"]).then_inc(s["w"], 16)
                with sp.Fori(0, NB // 2) as it:
                    for p in range(2):
                        b = it * 2 + p
                        sp.wait_ge(s["c_free"], b + 1)
                        alone(sp)
                        sp.dma_start(cT[:, p], a["ctx_T"].rearrange("(k p) t -> p k t", p=P)[:, :, ds(b * S, S)]).then_inc(s[f"c{p}"], 16)
                sp.wait_ge(s["gi_cp"], NB + 2)
                sp.wait_ge(s["gf_cp"], NB + 2)
                for b in range(NB):
                    sp.dma_start(ig[b * H:(b + 1) * H, :], raw[:, 0, b * S:(b + 1) * S]).then_inc(s["lay"], 16)
                    sp.dma_start(fg[b * H:(b + 1) * H, :], raw[:, 1, b * S:(b + 1) * S]).then_inc(s["lay"], 16)
                sp.wait_ge(s["sc"], 1)
                sp.dma_start(Mrow, M[:, :]).then_inc(s["m_st"], 16)
                sp.wait_ge(s["m_st"], 16)

            @block.tensor
            def _(pe):
                pe.sem_inc(s["c_free"], 2)
                pe.wait_ge(s["w"], 64)
                with pe.Fori(0, NB // 2) as it:
                    for p in range(2):
                        b = it * 2 + p
                        pe.wait_ge(s[f"c{p}"], it * 16 + 16)
                        pe.wait_ge(s["gi_cp"], b + 1)
                        pe.wait_ge(s["gf_cp"], b + 1)
                        for W, o in ((WI, ips), (WF, fps)):
                            for j in range(6):
                                x = xT[:, j, ds(b * S, S)] if j < 2 else cT[:, p, j % 2, :]
                                last = nc.tensor.matmul(o[0:H, p, :], W[:, j, :], x, start=j == 0, stop=j == 5)
                        last.then_inc(s["gi"], 1)
                        pe.wait_ge(s["gi"], b + 1)
                        pe.sem_inc(s["c_free"], 1)
                pe.wait_ge(s["sc"], 1)
                for t in range(NT):
                    if t:
                        pe.wait_ge(s["tp_cp"], t)
                    nc.tensor.transpose(tps[:, 0, 0:NH], ig[:, t * P:(t + 1) * P], G.ident[0:NH, 0:NH])
                    nc.tensor.transpose(tps[:, 0, NH:2 * NH], fg[:, t * P:(t + 1) * P], G.ident[0:NH, 0:NH]).then_inc(s["tp"], 1)

            @block.scalar
            def _(act):
                act.wait_ge(s["w"], 64)
                act.sem_inc(s["gi_cp"], 2)
                act.sem_inc(s["gf_cp"], 2)
                with act.Fori(0, NB // 2) as it:
                    for p in range(2):
                        b = it * 2 + p
                        act.wait_ge(s["gi"], b + 1)
                        nc.scalar.activation(raw[:, 0, ds(b * S, S)], ips[0:H, p, :], ACT.Identity, bias=bi[:, 0:1]).then_inc(s["gi_cp"], 1)
                        nc.scalar.activation(raw[:, 1, ds(b * S, S)], fps[0:H, p, :], ACT.Identity, bias=bi[:, 1:2]).then_inc(s["gf_cp"], 1)
                act.wait_ge(s["lin"], 1)
                nc.scalar.activation(t1[:, :], t1[:, :], ACT.Exp).then_inc(s["actc"], 1)
                act.wait_ge(s["actc"], 1)
                nc.scalar.activation(t1[:, :], t1[:, :], ACT.Ln, bias=1.0).then_inc(s["ln"], 1)
                act.wait_ge(s["ex"], 1)
                nc.scalar.activation(fg[:, :], cs[:, :], ACT.Exp, scale=-1.0).then_inc(s["sc"], 1)
                for t in range(NT):
                    act.wait_ge(s["tp"], t + 1)
                    nc.scalar.copy(gT[:, t, :], tps[:, 0, 0:NH])
                    nc.scalar.copy(eT[:, t, :], tps[:, 0, NH:2 * NH]).then_inc(s["tp_cp"], 1)

            @block.vector
            def _(dve):
                ch = Chain(dve, s["dvc"])
                V = nc.vector
                V.memset(one[:, :], 1.0)
                dve.wait_ge(s["lay"], 16 * 2 * NB)
                ch.link(V.tensor_scalar(t1[:, :], fg[:, :], -1.0, None, ALU.mult))
                V.tensor_tensor(t1[:, :], t1[:, :], fg[:, :], ALU.min).then_inc(s["lin"], 1)
                ch.link(V.tensor_scalar(fg[:, :], fg[:, :], 0.0, None, ALU.min))
                dve.wait_ge(s["ln"], 1)
                ch.link(V.tensor_tensor(fg[:, :], fg[:, :], t1[:, :], ALU.subtract))
                ch.link(V.tensor_tensor_scan(cs[:, :], one[:, :], fg[:, :], 0.0, ALU.mult, ALU.add))
                ch.link(V.tensor_tensor(ig[:, :], ig[:, :], cs[:, :], ALU.subtract))
                ch.link(V.tensor_tensor_scan(M[:, :], one[:, :], ig[:, :], -3.0e38, ALU.mult, ALU.max))
                V.tensor_tensor(cs[:, :], cs[:, :], M[:, :], ALU.add).then_inc(s["ex"], 1)


def cell(nc, G, name, qs, ks, vs, Mrow, gT, eT, ln_scale, gate):
    H, DH = 8, 32
    NC, TPC, KR = 2, 3, 96
    DA = DH + 1
    SC = float(DH) ** -0.5
    EPS = 1e-6
    with phase(nc, name, "w qk0 qk1 qk_free v0 v1 ones m0 m1 m_free diag score d ct vh pv o_free turned out_free stats rstd tri dvc poolc") as (s, sb, ps):
        Q = sb("Q", [P, 2, NC, H, S], BF16)
        K = sb("K", [P, 2, NC, H, S], BF16)
        V = sb("V", [P, 2, NT, H, DA])
        Mb = sb("Mb", [P, 2, S])
        Md = sb("Md", [P, 2, S])
        tri = sb("tri", [P, P])
        lns = sb("lns", [P, D])
        decay = sb("decay", [P, NT, S])
        C = sb("C", [P, NT, S])
        den = sb("den", [P, NT, H])
        neg = sb("neg", [P, NT, H])
        hs = sb("hs", [P, NT, D])
        st = sb("st", [P, NT, 6])
        mv = sb("mv", [P, NT, 2])
        rstd = sb("rstd", [P, NT])
        Vh = sb("Vh", [P, 2, NT, DA])
        osb = sb("osb", [DA, H, S])
        sps = ps("sps", [P, 2, S])
        hps = ps("hps", [DA, 2, S])
        ops = ps("ops", [P, NT, S])

        with nc.Block() as block:

            @block.sync
            def _(sp):
                sp.dma_start(lns[:, :], ln_scale.unsqueeze(0).broadcast_to([P, D])).then_inc(s["w"], 16)

                def pieces(b, p):
                    for i, (qp, kp) in enumerate(TERMS):
                        c, r = i // TPC, i % TPC
                        for dst, part, src in ((Q, qp, qs), (K, kp, ks)):
                            yield dst[r * DH:(r + 1) * DH, p, c], src[part - 1].rearrange("(h d) t -> d h t", d=DH)[:, :, ds(b * S, S)], s[f"qk{p}"]
                    for t in range(NT):
                        yield V[:, p, t, :, 0:DH], vs[ds(b * S + t * P, P), :].rearrange("p (h d) -> p h d", d=DH), s[f"v{p}"]

                sp.wait_ge(s["tri"], 1)
                for dst, src, sem in pieces(0, 0):
                    sp.dma_start(dst, src).then_inc(sem, 16)

                def sequence(b, p, more):
                    if more:
                        sp.wait_ge(s["qk_free"], b + 2)
                        alone(sp)
                        loads = list(pieces(b + 1, 1 - p))
                    for h in range(H):
                        n = b * H + h
                        sp.wait_ge(s["m_free"], n + 1)
                        alone(sp)
                        sp.dma_start(Mb[:, h % 2, :], Mrow[ds(n, 1), :].broadcast_to([P, S])).then_inc(s[f"m{h % 2}"], 16)
                        if more:
                            for dst, src, sem in loads[2 * h:2 * h + 2]:
                                sp.dma_start(dst, src).then_inc(sem, 16)

                with sp.Fori(0, NB // 2 - 1) as it:
                    for p in range(2):
                        sequence(it * 2 + p, p, True)
                sequence(NB - 2, 0, True)
                sequence(NB - 1, 1, False)

            @block.gpsimd
            def _(pool):
                ch = Chain(pool, s["poolc"])
                for p in range(2):
                    for t in range(NT):
                        last = nc.gpsimd.memset(V[:, p, t, :, DH:DA], 1.0)
                ch.link(last)
                ch.link(nc.gpsimd.memset(tri[:, :], 0.0))
                nc.gpsimd.affine_select(out=tri[:, :], in_=tri[:, :], compare_op=ALU.is_ge, fill=BIG, base=0,
                                        pattern=[[1, P]], channel_multiplier=-1).then_inc(s["tri"], 1)
                pool.wait_ge(s["tri"], 1)

                def sequence(b):
                    with pool.Fori(0, H // 2) as hh:
                        for hp in range(2):
                            n = b * H + hh * 2 + hp
                            pool.wait_ge(s[f"m{hp}"], b * (8 * H) + hh * 16 + 16)
                            pool.wait_ge(s["m_free"], n + 1)
                            nc.gpsimd.tensor_tensor(Md[:, hp, :].rearrange("p (t c) -> p t c", c=P), Mb[:, hp, :].rearrange("p (t c) -> p t c", c=P),
                                                    tri[:, :].unsqueeze(1).broadcast_to([P, NT, P]), ALU.add).then_inc(s["diag"], 1)
                    pool.wait_ge(s["stats"], b + 1)
                    alone(pool)
                    ch.at(b + 2)
                    ch.link(nc.gpsimd.tensor_scalar(rstd[:, :], mv[:, :, 1], LN_EPS, None, ALU.add))
                    nc.gpsimd.tensor_tensor(rstd[:, :], rstd[:, :], G.mhalf[:, 0:NT], ALU.pow).then_inc(s["rstd"], 1)

                with pool.Fori(0, NB) as b:
                    sequence(b)

            @block.tensor
            def _(pe):
                pe.sem_inc(s["qk_free"], 2)

                def scores(p, b, h, k):
                    w = (NT - k) * P
                    for c in range(NC):
                        last = nc.tensor.matmul(sps[:, k % 2, 0:w], K[0:KR, p, c, ds(h, 1), k * P:(k + 1) * P].rearrange("p o t -> p (o t)"),
                                                Q[0:KR, p, c, ds(h, 1), k * P:S].rearrange("p o t -> p (o t)"), start=c == 0, stop=c == NC - 1)
                    last.then_inc(s["score"], 1)

                def head(p, b, h, slot, final):
                    n = b * H + h
                    for k in range(NT):
                        pe.wait_ge(s["ct"], n * NT + k + 1 + NT)
                        if not (final and k >= NT - 2):
                            scores(p, b, h + (k + 2) // NT, (k + 2) % NT)
                        if k == 0:
                            pe.wait_ge(s["vh"], n + 1)
                            pe.wait_ge(s["o_free"], n + 1)
                            alone(pe)
                        last = nc.tensor.matmul(hps[:, slot, k * P:S], Vh[:, slot, k, :], C[:, k, 0:(NT - k) * P],
                                                start=k == 0, stop=k == NT - 1, skip_group_check=True)
                    last.then_inc(s["pv"], 1)

                with pe.Fori(0, NB // 2) as it:
                    for p in range(2):
                        b = it * 2 + p
                        pe.wait_ge(s[f"qk{p}"], it * (16 * 12) + 16 * 12)
                        alone(pe)
                        scores(p, b, 0, 0)
                        scores(p, b, 0, 1)
                        with pe.Fori(0, H // 2 - 1) as hh:
                            for i in range(2):
                                head(p, b, hh * 2 + i, i, False)
                        for i in range(2):
                            head(p, b, H - 2 + i, i, i == 1)
                        pe.wait_ge(s["pv"], b * H + H)
                        pe.sem_inc(s["qk_free"], 1)
                        pe.wait_ge(s["o_free"], b * H + H + 2)
                        pe.wait_ge(s["out_free"], b + 1)
                        alone(pe)
                        for h in range(H):
                            for t in range(NT):
                                last = nc.tensor.transpose(ops[:, t, h * DA:(h + 1) * DA], osb[:, h, t * P:(t + 1) * P], G.ident[0:DA, 0:DA])
                        last.then_inc(s["turned"], 1)

            @block.scalar
            def _(act):
                act.sem_inc(s["m_free"], 2)
                with act.Fori(0, NB * H // 2) as i:
                    for hp in range(2):
                        n = i * 2 + hp
                        act.wait_ge(s["diag"], n + 1)
                        for k in range(NT):
                            act.wait_ge(s["ct"], n * NT + k + 1)
                            g = gT[:, k, ds(n, 1)]
                            last = nc.scalar.activation(decay[:, k, 0:P], Md[:, hp, k * P:(k + 1) * P], ACT.Exp, scale=-1.0, bias=g)
                            if k < NT - 1:
                                last = nc.scalar.activation(decay[:, k, P:(NT - k) * P], Mb[:, hp, (k + 1) * P:S], ACT.Exp, scale=-1.0, bias=g)
                            last.then_inc(s["d"], 1)
                        act.wait_ge(s["d"], n * NT + NT)
                        act.sem_inc(s["m_free"], 1)

            @block.vector
            def _(dve):
                ch = Chain(dve, s["dvc"])
                dve.sem_inc(s["ct"], NT)
                dve.sem_inc(s["out_free"], 1)
                dve.wait_ge(s["w"], 16)
                KCH = 10
                dve.sem_inc(s["o_free"], 2)

                def keep(n, h, slot):
                    dve.wait_ge(s["pv"], n + 1)
                    alone(dve)
                    nc.vector.tensor_copy(osb[:, ds(h, 1), :].rearrange("d o t -> d (o t)"), hps[:, slot, :]).then_inc(s["o_free"], 1)

                def head(p, b, h, slot, first=False):
                    n = b * H + h
                    nc.vector.tensor_copy(Vh[:, slot, :, :], V[:, p, :, ds(h, 1), :].rearrange("p t o d -> p (t o) d")).then_inc(s["vh"], 1)
                    for k in range(NT):
                        w = (NT - k) * P
                        if k == 2 and not first:
                            keep(n - 1, h - 1, 1 - slot)
                        dve.wait_ge(s["score"], n * NT + k + 1)
                        dve.wait_ge(s["d"], n * NT + k + 1)
                        nc.vector.scalar_tensor_tensor(C[:, k, 0:w], sps[:, k % 2, 0:w], SC, decay[:, k, 0:w], ALU.mult, ALU.mult).then_inc(s["ct"], 1)

                def sequence(p, it):
                    b = it * 2 + p
                    dve.wait_ge(s[f"v{p}"], it * 64 + 64)
                    alone(dve)
                    head(p, b, 0, 0, first=True)
                    head(p, b, 1, 1)
                    with dve.Fori(0, H // 2 - 1) as hh:
                        for i in range(2):
                            head(p, b, hh * 2 + 2 + i, i)
                    keep(b * H + H - 1, H - 1, 1)
                    ch.at(b * KCH)
                    dve.wait_ge(s["turned"], b + 1)
                    rows = ops[:, :, 0:H * DA].rearrange("p t (h d) -> p t h d", d=DA)
                    total = rows[:, :, :, DH]
                    ch.link(nc.vector.tensor_scalar(neg[:, :, :], total, -1.0, None, ALU.mult))
                    ch.link(nc.vector.tensor_tensor(den[:, :, :], total, neg[:, :, :], ALU.max))
                    ch.link(nc.vector.tensor_tensor(den[:, :, :], den[:, :, :], eT[:, :, ds(b * H, H)], ALU.max))
                    ch.link(nc.vector.tensor_scalar(den[:, :, :], den[:, :, :], EPS, None, ALU.add))
                    ch.link(nc.vector.reciprocal(den[:, :, :], den[:, :, :]))
                    for t in range(NT):
                        last = nc.vector.tensor_tensor(hs[:, t, :].rearrange("p (h d) -> p h d", d=DH), rows[:, t, :, 0:DH],
                                                       den[:, t, :].unsqueeze(2).broadcast_to([P, H, DH]), ALU.mult)
                    ch.link(last)
                    dve.sem_inc(s["out_free"], 1)
                    for t in range(NT):
                        last = nc.vector.bn_stats(st[:, t, :], hs[:, t, :])
                    ch.link(last)
                    alone(dve)
                    for t in range(NT):
                        last = nc.vector.bn_aggr(mv[:, t, :], st[:, t, :])
                    last.then_inc(s["stats"], 1)
                    dve.wait_ge(s["rstd"], b + 1)
                    for t in range(NT):
                        last = nc.vector.tensor_scalar(hs[:, t, :], hs[:, t, :], mv[:, t, 0:1], rstd[:, t:t + 1], ALU.subtract, ALU.mult)
                    ch.link(last)
                    ch.link(nc.vector.tensor_tensor(hs[:, :, :], hs[:, :, :], lns[:, :].unsqueeze(1).broadcast_to([P, NT, D]), ALU.mult))
                    x = G.X[:, ds(b * NT, NT), :].rearrange("p t d -> p (t d)")
                    ch.link(nc.vector.scalar_tensor_tensor(x, hs[:, :, :].rearrange("p t d -> p (t d)"), G.gate[:, gate:gate + 1], x, ALU.mult, ALU.add))
                    ch.done(KCH)

                with dve.Fori(0, NB // 2) as it:
                    for p in range(2):
                        sequence(p, it)


class Globals:
    pass


def program(nc, a):
    G = Globals()
    with ExitStack() as ctx:
        def sb(name, shape, dt=F32):
            return ctx.enter_context(nc.sbuf_tensor(name, shape, dt))

        def dram(name, shape, dt=F32):
            return nc.dram_tensor(name, shape, dt).ap()

        G.X = sb("stream", [P, TT, D])
        G.ident = sb("ident", [P, P])
        G.identb = sb("identb", [P, P], BF16)
        G.masks = sb("masks", [P, 3, P], BF16)
        G.gate = sb("gate", [P, 8])
        G.ones = sb("ones", [1, P])
        G.mhalf = sb("mhalf", [P, 32])
        G.qs = dram("q_parts", [3, 512, TOK], BF16)
        G.ks = dram("k_parts", [3, 512, TOK], BF16)
        G.vs = dram("values", [TOK, D])
        G.osT = dram("attended", [D, TOK])
        G.sums = dram("sums", [16, TOK])
        constants(nc, G, a)
        qs, ks = G.qs[:, 0:D, :], G.ks[:, 0:D, :]
        if 0 in STAGES:
            rel = [dram(f"rel{t}", [NB * 16, P * (t + 1) * P]) for t in range(NT)]
            qkv(nc, G, "a0", G.X,
                [("wk", i, "c", "bk", 1.0, ks, i * P) for i in range(KT)] + [("wq", i, "x", "bq", -0.25, qs, i * P) for i in range(KT)],
                {"wq": (w_view(a["L0_xattn_Wq"]), [P, KT, D]), "wk": (w_view(a["L0_xattn_Wk"]), [P, KT, D]),
                 "wv": (w_view(a["L0_xattn_Wv"]), [P, KT, D]), "bq": (a["L0_xattn_bq"], [P, KT]),
                 "bk": (a["L0_xattn_bk"], [P, KT]), "bv": (a["L0_xattn_bv"].unsqueeze(0), [1, D])},
                ("wv", "c", "bv", G.vs, D), ctx=a["ctx_T"])
            rel_scores(nc, G, "r0", qs, a["L0_xattn_Er"], rel)
            attention(nc, G, "t0", qs, ks, G.vs, 16, 16, lambda t: (0, t + 1), lambda t: [(t, 2)], G.osT, G.sums, rel=rel)
            outproj(nc, G, "o0", G.osT, w_view(a["c_eye"]), [P, KT, D], None, 0, G.X, sums=G.sums)
        every = lambda t: (0, NT)
        ident_tile = lambda t: [(k, min(P, (D >> t) - k * P)) for k in range(KT) if (D >> t) > k * P]
        if 1 in STAGES:
            quantised_ffn(nc, G, a)
        if 2 in STAGES:
            maskrow = dram("mask_row", [NB, S], BF16)
            key_mask(nc, G, "m1", a["mask_BxS2_ik0"], maskrow)
            wkv = w_view(a["L1_xattn_Wkv"])
            qkv(nc, G, "a1", G.X,
                [("wk", i, "c", None, 1.0, ks, i * P) for i in range(KT)] + [("wq", i, "x", None, 0.25, qs, i * P) for i in range(KT)],
                {"wq": (w_view(a["L1_xattn_Wq"]), [P, KT, D]), "wk": (wkv[:, :, 0:D], [P, KT, D]), "wv": (wkv[:, :, D:2 * D], [P, KT, D])},
                ("wv", "c", None, G.vs, D), ctx=a["ctx_T"])
            wide_attention(nc, G, "t1", qs, ks, G.vs, 16, 16, G.osT, G.sums, maskrow=maskrow)
            outproj(nc, G, "o1", G.osT, w_view(a["L1_xattn_Wproj"]), [P, KT, D], a["L1_xattn_bproj"].unsqueeze(0), 1, G.X, sums=G.sums)
        if 3 in STAGES:
            with ExitStack() as part:
                xT = part.enter_context(nc.sbuf_tensor("moeT", [P, KT, TOK], F32))
                combT = part.enter_context(nc.sbuf_tensor("combT", [16, TOK], F32))
                with nc.sbuf_tensor("moe_rows", [P, TT, D], F32) as Y:
                    normalise(nc, G, "n3", G.X, Y)
                    turn(nc, G, "x3", Y, xT)
                G.before, G.spread = a["c_before"], a["c_spread"]
                route(nc, G, "r3", xT, w_view(a["L1_ffn_router_w"]), a["L1_ffn_correction_bias"], combT)
                R = 16 * 64

                def both(routed, shared):
                    return [(w_view(a[f"L1_ffn_{routed}_w"]), 0), (w_view(a[f"L1_ffn_shared_{shared}_w"]), R)]

                gated_mlp(nc, G, "f3", xT, both("gate", "gate"), both("up", "up"),
                          [(w_view(a["L1_ffn_down_w"]), 0), (w_view(a["L1_ffn_shared_down_w"]), R // P)],
                          12, ACT.Silu, G.X, 5, combT=combT, routed=8)
        if 4 in STAGES:
            with ExitStack() as part:
                gT = part.enter_context(nc.sbuf_tensor("cell_g", [P, NT, NB * 8], F32))
                eT = part.enter_context(nc.sbuf_tensor("cell_e", [P, NT, NB * 8], F32))
                Mrow = dram("cell_max", [NB * 8, S])
                with ExitStack() as part2:
                    xT = part2.enter_context(nc.sbuf_tensor("cellT", [P, KT, TOK], F32))
                    with nc.sbuf_tensor("cell_rows", [P, TT, D], F32) as Y:
                        normalise(nc, G, "n4", G.X, Y)
                        turn(nc, G, "x4", Y, xT)
                    cell_gates(nc, G, "g4", xT, a, Mrow, gT, eT)
                eye = (w_view(a["c_eye"]), [P, KT, D])
                qkv(nc, G, "a4", G.X,
                    [("eye", i, "c", None, 1.0, ks, i * P) for i in range(KT)] + [("eye", i, "x", None, 1.0, qs, i * P) for i in range(KT)],
                    {"eye": eye}, ("eye", "c", None, G.vs, D), ctx=a["ctx_T"])
                cell(nc, G, "t4", qs, ks, G.vs, Mrow, gT, eT, a["L2_xattn_ln_scale"], 2)
        if 5 in STAGES:
            with nc.sbuf_tensor("inner2", [P, TT, D], F32) as Y:
                G.Y = Y
                G.rotary = a["c_rotary"]
                vs5, os5 = dram("values5", [TOK, 512]), dram("attended5", [512, TOK])
                normalise(nc, G, "n5", G.X, Y)
                for d in range(2):
                    rotary_qkv(nc, G, f"a5{d}", Y, a["L2_ffn_wqkv"][d], a["L2_ffn_q_scale"][d], a["L2_ffn_k_scale"][d], G.qs, G.ks, vs5)
                    attention(nc, G, f"t5{d}", G.qs, G.ks, vs5, 8, 64, lambda t: (max(0, t - 1), t + 1),
                              lambda t: [(t, 0)] if t == 0 else [(t - 1, 1), (t, 0)], os5, G.sums[0:8])
                    outproj(nc, G, f"o5{d}", os5, w_view(a["L2_ffn_wo"][d]), [P, 4, D], None, None, Y, sums=G.sums[0:8], H=8)
                    w1 = w_view(a["L2_ffn_w1"][d])
                    gated_mlp(nc, G, f"f5{d}", ("shift", Y, a["L2_ffn_ln_g"][d], a["L2_ffn_ln_b"][d]),
                              [(w1[:, :, 768:1536], 0)], [(w1[:, :, 0:768], 0)], [(w_view(a["L2_ffn_w2"][d]), 0)], 6, ACT.Gelu, Y, None,
                              bg=a["L2_ffn_b1"][d, :, 6:12], bu=a["L2_ffn_b1"][d, :, 0:6], bd=a["L2_ffn_b2"][d:d + 1, :])
                add_stream(nc, G, "s5", 6)
        if 6 in STAGES:
            qkv(nc, G, "a3", G.X,
                [("wk", i, "c", "bk", 1.0, ks, i * P) for i in range(KT)] + [("wq", i, "x", "bq", 0.25, qs, i * P) for i in range(KT)],
                {"wq": (w_view(a["L3_xattn_Wq"]), [P, KT, D]), "wk": (w_view(a["L3_xattn_Wk"]), [P, KT, D]),
                 "wv": (w_view(a["L3_xattn_Wv"]), [P, KT, D]), "bq": (a["L3_xattn_bq"], [P, KT]),
                 "bk": (a["L3_xattn_bk"], [P, KT]), "bv": (a["L3_xattn_bv"].unsqueeze(0), [1, D])},
                ("wv", "c", "bv", G.vs, D), ctx=a["ctx_T"])
            wide_attention(nc, G, "t3", qs, ks, G.vs, 16, 16, G.osT, G.sums)
            outproj(nc, G, "o3", G.osT, w_view(a["L3_xattn_Wo"]), [P, KT, D], a["L3_xattn_bo"].unsqueeze(0), 3, G.X, sums=G.sums)
        if 7 in STAGES:
            G.Y = sb("inner3", [P, TT, D])
            normalise(nc, G, "n7", G.X, G.Y)
            qkv(nc, G, "a7", G.Y,
                [("wk", i, "x", "bk", 1.0, ks, i * P) for i in range(KT)] + [("wq", i, "x", "bq", D ** -0.5, qs, i * P) for i in range(KT)],
                {"wq": (w_view(a["L3_ffn_q_w"]), [P, KT, D]), "wk": (w_view(a["L3_ffn_k_w"]), [P, KT, D]),
                 "wv": (w_view(a["L3_ffn_v_w"]), [P, KT, D]), "bq": (a["L3_ffn_q_b"], [P, KT]),
                 "bk": (a["L3_ffn_k_b"], [P, KT]), "bv": (a["L3_ffn_v_b"].unsqueeze(0), [1, D]),
                 "nw": (a["L3_ffn_norm_w"], [P, KT]), "nb": (a["L3_ffn_norm_b"], [P, KT])},
                ("wv", "x", "bv", G.vs, D), affine=("nw", "nb"), tile_k=ident_tile)
            wide_attention(nc, G, "t7", qs, ks, G.vs, 8, 32, G.osT, G.sums[0:8])
            outproj(nc, G, "o7", G.osT, w_view(a["L3_ffn_o_w"]), [P, KT, D], a["L3_ffn_o_b"].unsqueeze(0), 7, G.X, also=G.Y, tile_k=ident_tile, sums=G.sums[0:8], H=8)
        store(nc, G, a)


TRANSPOSED = ("L0_xattn_Wq", "L0_xattn_Wk", "L0_xattn_Wv", "L0_xattn_Er",
              "L3_ffn_q_w", "L3_ffn_k_w", "L3_ffn_v_w", "L3_ffn_o_w", "L1_ffn_router_w", "L1_ffn_shared_gate_w",
              "L1_ffn_shared_up_w", "L1_ffn_shared_down_w", "L2_xattn_igate_w", "L2_xattn_fgate_w")

COLUMNS = ("L0_xattn_bq", "L0_xattn_bk", "L3_xattn_bq", "L3_xattn_bk", "L3_ffn_q_b", "L3_ffn_k_b", "L3_ffn_norm_w",
           "L3_ffn_norm_b")


def rotary_tables(np):
    DH, WINDOW = 64, 128
    half = np.arange(0, DH, 2, dtype=np.float32)
    inv_freq = (1.0 / np.float32(10000.0) ** (half / DH)).astype(np.float32)
    t = np.arange(S, dtype=np.float32)
    freqs = (t[:, None] * inv_freq[None, :]).astype(np.float32)
    base = ((half + 0.4 * DH) / (1.4 * DH)).astype(np.float32)
    power = ((t - S // 2) / (WINDOW // 2)).astype(np.float32)
    scale = (base[None, :] ** power[:, None]).astype(np.float32)
    cos, sin = np.cos(freqs), np.sin(freqs)
    turned = [np.concatenate(x, 1) for x in ((cos * scale, cos * scale), (-sin * scale, sin * scale), (cos / scale, cos / scale), (-sin / scale, sin / scale))]
    return np.stack([turned[0] * 8, turned[1] * 8, turned[2], turned[3]]).astype(np.float32)


def kernel(**inputs):
    import numpy as np
    import concourse.bacc as bacc
    from concourse.bass_utils import run_bass_kernel_spmd

    arrays = {}
    for name, v in inputs.items():
        v = np.asarray(v)
        if name in TRANSPOSED:
            v = v.T
        if name in COLUMNS:
            v = v.reshape(-1, P).T
        arrays[name] = np.ascontiguousarray(v)
    arrays["ctx_T"] = np.ascontiguousarray(arrays.pop("ctx_1024").transpose(2, 0, 1).reshape(D, TOK))
    p, c = np.meshgrid(np.arange(P), np.arange(P), indexing="ij")
    for n in ("gate", "up"):
        w = arrays[f"L1_ffn_{n}_w"]
        arrays[f"L1_ffn_{n}_w"] = np.ascontiguousarray(w.transpose(1, 0, 2).reshape(D, -1))
    arrays["L1_ffn_down_w"] = arrays["L1_ffn_down_w"].reshape(-1, D)
    for n in ("igate", "fgate"):
        arrays[f"L2_xattn_{n}_b"] = arrays[f"L2_xattn_{n}_b"].reshape(-1, 1)
    half, full = arrays["L2_ffn_w2"].shape[1], 6 * P
    for n, axis in (("L2_ffn_w1", 2), ("L2_ffn_b1", 1)):
        arrays[n] = np.concatenate([np.concatenate([x, np.zeros_like(x[..., :full - half])], axis) for x in np.split(arrays[n], 2, axis)], axis)
    arrays["L2_ffn_w2"] = np.concatenate([arrays["L2_ffn_w2"], np.zeros_like(arrays["L2_ffn_w2"][:, :full - half])], 1)
    for n in ("L2_ffn_b1", "L2_ffn_ln_g", "L2_ffn_ln_b"):
        arrays[n] = np.ascontiguousarray(arrays[n].reshape(2, -1, P).transpose(0, 2, 1))
    arrays["c_eye"] = np.eye(D, dtype=np.float32)
    arrays["c_before"] = np.tril(np.ones((16, 16), np.float32), -1).reshape(-1)
    arrays["c_spread"] = np.repeat(np.eye(16, dtype=np.float32).reshape(16, 8, 2), 64, axis=2)
    arrays["c_rotary"] = rotary_tables(np)
    arrays["c_ident"] = np.eye(P, dtype=np.float32)
    arrays["c_masks"] = np.stack([np.where(c <= p, 0.0, -BIG), np.where(c >= p, 0.0, -BIG), np.where(c <= p, 0.0, BIG)]).astype(np.float32)
    nc = bacc.Bacc("TRN2", target_bir_lowering=False, num_devices=1)
    feeds, a = {}, {}
    for name, v in arrays.items():
        feeds[f"in_{name}"] = v
        a[name] = nc.dram_tensor(f"in_{name}", v.shape, mybir.dt.from_np(v.dtype), kind="ExternalInput").ap()
    a["out"] = nc.dram_tensor("out_x", (NB, S, D), F32, kind="ExternalOutput").ap()
    program(nc, a)
    r = run_bass_kernel_spmd(nc, [feeds], core_ids=[0])
    return r.results[0]["out_x"]
```
